# Optimizing a Trainium2 kernel written in Bass

```python
import numpy as np
import jax
import jax.numpy as jnp

def _softmax(x, axis=-1):
    return jax.nn.softmax(x, axis=axis)

def _gelu(x):
    return jax.nn.gelu(x, approximate=True)

def _silu(x):
    return jax.nn.silu(x)

def _sigmoid(x):
    return jax.nn.sigmoid(x)

def _layernorm(x, axis=-1, eps=1e-05):
    m = jnp.mean(x, axis=axis, keepdims=True)
    v = jnp.var(x, axis=axis, keepdims=True)
    return (x - m) / jnp.sqrt(v + eps)

def _scatter_add(tgt, idx, src, axis=0):
    return tgt.at[idx].add(src)

def _segment_sum(src, seg, n):
    return jax.ops.segment_sum(src, seg, n)
kernel_name = 'mk_recurrent_d2_jaxref_r8_e56ce1'

def setup_inputs(seed: int=0):
    np.random.seed(seed)
    _w = jnp.asarray

    def _L0_attn_setup():
        import jax, jax.numpy as jnp
        import numpy as np
        H = 8
        DIM = 128
        DH = DIM // H // 2
        B, N = (2, 256)
        LAMBDA_INIT = 0.5
        COS_MIN, COS_MAX = (0.0, 15.0)
        ALPHA = 0.5
        COS_EPS = 1e-06
        RMS_EPS = 1e-05
        RAW_INIT = float(np.log(1.0 / 15.0 / (1.0 - 1.0 / 15.0)))

        def _l2norm(t):
            return t / jnp.maximum(jnp.linalg.norm(t, axis=-1, keepdims=True), COS_EPS)
        key = jax.random.key(seed)
        ks = jax.random.split(key, 10)
        s = 1.0 / np.sqrt(DIM)
        return {'x': jax.random.normal(ks[0], (B, N, DIM), jnp.float32), 'Wq': jax.random.normal(ks[1], (DIM, DIM), jnp.float32) * s, 'Wk': jax.random.normal(ks[2], (DIM, DIM), jnp.float32) * s, 'Wv': jax.random.normal(ks[3], (DIM, DIM), jnp.float32) * s, 'Wo': jax.random.normal(ks[4], (DIM, DIM), jnp.float32) * s, 'bo': jnp.zeros((DIM,), jnp.float32), 'lambda_q1': jax.random.normal(ks[5], (DH,), jnp.float32) * 0.1, 'lambda_k1': jax.random.normal(ks[6], (DH,), jnp.float32) * 0.1, 'lambda_q2': jax.random.normal(ks[7], (DH,), jnp.float32) * 0.1, 'lambda_k2': jax.random.normal(ks[8], (DH,), jnp.float32) * 0.1, 'delta_gain': jax.random.normal(ks[9], (H,), jnp.float32) * 0.1, 'cos_head_delta': jnp.zeros((H,), jnp.float32), 'cos_logit_scale_raw': jnp.float32(RAW_INIT), 'subln_weight': jnp.ones((2 * DH,), jnp.float32)}
    _L0_attn_in = _L0_attn_setup()

    def _L0_ffn_setup():
        import jax, jax.numpy as jnp
        import numpy as np
        D = 128
        H = 4
        DF = 512
        E = 8
        EPS = 1e-05

        def _layer_norm(x, g, b):
            mu = jnp.mean(x, axis=-1, keepdims=True)
            var = jnp.mean(jnp.square(x - mu), axis=-1, keepdims=True)
            return (x - mu) * jax.lax.rsqrt(var + EPS) * g + b

        def _mha(x, Wqkv, bqkv, Wo, bo):
            S, B, _ = x.shape
            hd = D // H
            qkv = x @ Wqkv.T + bqkv
            q, k, v = jnp.split(qkv, 3, axis=-1)
            to_heads = lambda t: t.reshape(S, B, H, hd).transpose(1, 2, 0, 3)
            q, k, v = (to_heads(q), to_heads(k), to_heads(v))
            scores = jnp.einsum('bhqd,bhkd->bhqk', q, k) * (1.0 / np.sqrt(hd))
            att = jax.nn.softmax(scores, axis=-1)
            o = jnp.einsum('bhqk,bhkd->bhqd', att, v)
            o = o.transpose(2, 0, 1, 3).reshape(S, B, D)
            return o @ Wo.T + bo

        def _moe(x, Wg, W1, b1, W2, b2):
            S, B, _ = x.shape
            xf = x.reshape(S * B, D)
            logits = xf @ Wg.T
            idx = jnp.argmax(logits, axis=-1)
            out = jnp.zeros_like(xf)
            for e in range(E):
                m = (idx == e)[:, None].astype(xf.dtype)
                h = jax.nn.relu(xf @ W1[e] + b1[e])
                out = out + m * (h @ W2[e] + b2[e])
            return out.reshape(S, B, D)
        key = jax.random.key(seed)
        ks = jax.random.split(key, 16)
        S, B = (64, 8)
        s = lambda k, shape, fan: jax.random.normal(k, shape, jnp.float32) * (1.0 / np.sqrt(fan))
        return {'x': jax.random.normal(ks[0], (S, B, D), jnp.float32), 'Wqkv': s(ks[1], (3 * D, D), D), 'bqkv': jnp.zeros((3 * D,), jnp.float32), 'Wo': s(ks[2], (D, D), D), 'bo': jnp.zeros((D,), jnp.float32), 'g1': jnp.ones((D,), jnp.float32), 'be1': jnp.zeros((D,), jnp.float32), 'g2': jnp.ones((D,), jnp.float32), 'be2': jnp.zeros((D,), jnp.float32), 'Wg': s(ks[3], (E, D), D), 'W1': s(ks[4], (E, D, DF), D), 'b1': jnp.zeros((E, DF), jnp.float32), 'W2': s(ks[5], (E, DF, D), DF), 'b2': jnp.zeros((E, D), jnp.float32)}
    _L0_ffn_in = _L0_ffn_setup()

    def _L1_attn_setup():
        import jax, jax.numpy as jnp
        import numpy as np
        DIM = 128
        DEPTH = 4
        D_STATE = 16
        D_CONV = 4
        D_INNER = 2 * DIM
        DT_RANK = (DIM + 15) // 16
        B_SZ, L = (4, 256)

        def _selective_scan(u, delta, A, Bm, Cm, D):

            def step(h, inp):
                u_t, d_t, b_t, c_t = inp
                dA = jnp.exp(d_t[:, :, None] * A)
                h = dA * h + (d_t * u_t)[:, :, None] * b_t[:, None, :]
                y = jnp.einsum('bds,bs->bd', h, c_t)
                return (h, y)
            h0 = jnp.zeros((u.shape[0], u.shape[2], A.shape[1]), u.dtype)
            xs = (u.transpose(1, 0, 2), delta.transpose(1, 0, 2), Bm.transpose(1, 0, 2), Cm.transpose(1, 0, 2))
            _, ys = jax.lax.scan(step, h0, xs)
            return ys.transpose(1, 0, 2) + u * D

        def _mamba_layer(x, in_w, cw, cb, xp_w, dtw, dtb, A_log, D, ow):
            xz = jnp.einsum('bld,ed->ble', x, in_w)
            xi, z = jnp.split(xz, 2, axis=-1)
            xc = jax.lax.conv_general_dilated(xi.transpose(0, 2, 1), cw[:, None, :], window_strides=(1,), padding=[(D_CONV - 1, 0)], feature_group_count=D_INNER, dimension_numbers=('NCH', 'OIH', 'NCH'))
            xc = jax.nn.silu(xc.transpose(0, 2, 1) + cb)
            dbc = jnp.einsum('bld,ed->ble', xc, xp_w)
            dt, Bm, Cm = jnp.split(dbc, [DT_RANK, DT_RANK + D_STATE], axis=-1)
            delta = jax.nn.softplus(jnp.einsum('blr,dr->bld', dt, dtw) + dtb)
            A = -jnp.exp(A_log)
            y = _selective_scan(xc, delta, A, Bm, Cm, D)
            y = y * jax.nn.silu(z)
            return jnp.einsum('bld,od->blo', y, ow)
        key = jax.random.key(seed)
        ks = jax.random.split(key, 10)
        s = 0.02
        x = jax.random.normal(ks[0], (B_SZ, L, DIM), jnp.float32)
        in_proj_w = jax.random.normal(ks[1], (DEPTH, 2 * D_INNER, DIM), jnp.float32) * s
        conv_w = jax.random.normal(ks[2], (DEPTH, D_INNER, D_CONV), jnp.float32) * 0.2
        conv_b = jnp.zeros((DEPTH, D_INNER), jnp.float32)
        x_proj_w = jax.random.normal(ks[3], (DEPTH, DT_RANK + 2 * D_STATE, D_INNER), jnp.float32) * s
        dt_proj_w = jax.random.normal(ks[4], (DEPTH, D_INNER, DT_RANK), jnp.float32) * s
        dt_proj_b = jnp.full((DEPTH, D_INNER), float(np.log(np.expm1(0.01))), jnp.float32)
        A_log = jnp.broadcast_to(jnp.log(jnp.arange(1, D_STATE + 1, dtype=jnp.float32)), (D_INNER, D_STATE))
        A_log = jnp.broadcast_to(A_log, (DEPTH, D_INNER, D_STATE))
        D = jnp.ones((DEPTH, D_INNER), jnp.float32)
        out_proj_w = jax.random.normal(ks[5], (DEPTH, DIM, D_INNER), jnp.float32) * s
        return {'x': x, 'in_proj_w': in_proj_w, 'conv_w': conv_w, 'conv_b': conv_b, 'x_proj_w': x_proj_w, 'dt_proj_w': dt_proj_w, 'dt_proj_b': dt_proj_b, 'A_log': A_log, 'D': D, 'out_proj_w': out_proj_w}
    _L1_attn_in = _L1_attn_setup()

    def _L1_ffn_setup():
        import jax, jax.numpy as jnp
        import numpy as np
        B, S, H = (4, 256, 128)
        E, K = (8, 2)
        I_R, I_S = (4 * H, 8 * H)
        CAP_FACTOR = 1.25
        SCALE = 1.0
        key = jax.random.key(seed)
        ks = jax.random.split(key, 9)
        std = 0.02
        return {'x': jax.random.normal(ks[0], (B, S, H), jnp.float32), 'router_w': std * jax.random.normal(ks[1], (E, H), jnp.float32), 'rg': std * jax.random.normal(ks[2], (E, H, I_R), jnp.float32), 'ru': std * jax.random.normal(ks[3], (E, H, I_R), jnp.float32), 'rd': std * jax.random.normal(ks[4], (E, I_R, H), jnp.float32), 'sg': std * jax.random.normal(ks[5], (H, I_S), jnp.float32), 'su': std * jax.random.normal(ks[6], (H, I_S), jnp.float32), 'sd': std * jax.random.normal(ks[7], (I_S, H), jnp.float32)}
    _L1_ffn_in = _L1_ffn_setup()
    _d = {'L0_attn_x': _L0_attn_in['x'], 'L0_attn_Wq': _L0_attn_in['Wq'], 'L0_attn_Wk': _L0_attn_in['Wk'], 'L0_attn_Wv': _L0_attn_in['Wv'], 'L0_attn_Wo': _L0_attn_in['Wo'], 'L0_attn_bo': _L0_attn_in['bo'], 'L0_attn_lambda_q1': _L0_attn_in['lambda_q1'], 'L0_attn_lambda_k1': _L0_attn_in['lambda_k1'], 'L0_attn_lambda_q2': _L0_attn_in['lambda_q2'], 'L0_attn_lambda_k2': _L0_attn_in['lambda_k2'], 'L0_attn_delta_gain': _L0_attn_in['delta_gain'], 'L0_attn_cos_head_delta': _L0_attn_in['cos_head_delta'], 'L0_attn_cos_logit_scale_raw': _L0_attn_in['cos_logit_scale_raw'], 'L0_attn_subln_weight': _L0_attn_in['subln_weight'], 'L0_ffn_Wqkv': _L0_ffn_in['Wqkv'], 'L0_ffn_bqkv': _L0_ffn_in['bqkv'], 'L0_ffn_Wo': _L0_ffn_in['Wo'], 'L0_ffn_bo': _L0_ffn_in['bo'], 'L0_ffn_g1': _L0_ffn_in['g1'], 'L0_ffn_be1': _L0_ffn_in['be1'], 'L0_ffn_g2': _L0_ffn_in['g2'], 'L0_ffn_be2': _L0_ffn_in['be2'], 'L0_ffn_Wg': _L0_ffn_in['Wg'], 'L0_ffn_W1': _L0_ffn_in['W1'], 'L0_ffn_b1': _L0_ffn_in['b1'], 'L0_ffn_W2': _L0_ffn_in['W2'], 'L0_ffn_b2': _L0_ffn_in['b2'], 'L1_attn_in_proj_w': _L1_attn_in['in_proj_w'], 'L1_attn_conv_w': _L1_attn_in['conv_w'], 'L1_attn_conv_b': _L1_attn_in['conv_b'], 'L1_attn_x_proj_w': _L1_attn_in['x_proj_w'], 'L1_attn_dt_proj_w': _L1_attn_in['dt_proj_w'], 'L1_attn_dt_proj_b': _L1_attn_in['dt_proj_b'], 'L1_attn_A_log': _L1_attn_in['A_log'], 'L1_attn_D': _L1_attn_in['D'], 'L1_attn_out_proj_w': _L1_attn_in['out_proj_w'], 'L1_ffn_router_w': _L1_ffn_in['router_w'], 'L1_ffn_rg': _L1_ffn_in['rg'], 'L1_ffn_ru': _L1_ffn_in['ru'], 'L1_ffn_rd': _L1_ffn_in['rd'], 'L1_ffn_sg': _L1_ffn_in['sg'], 'L1_ffn_su': _L1_ffn_in['su'], 'L1_ffn_sd': _L1_ffn_in['sd']}
    _x0 = _d['L0_attn_x']
    _d['L0_attn_x'] = jax.random.normal(jax.random.fold_in(jax.random.key(seed), 1), (4, 512, 128), dtype=_x0.dtype)
    del _x0
    return _d

def reference(L0_attn_x, L0_attn_Wq, L0_attn_Wk, L0_attn_Wv, L0_attn_Wo, L0_attn_bo, L0_attn_lambda_q1, L0_attn_lambda_k1, L0_attn_lambda_q2, L0_attn_lambda_k2, L0_attn_delta_gain, L0_attn_cos_head_delta, L0_attn_cos_logit_scale_raw, L0_attn_subln_weight, L0_ffn_Wqkv, L0_ffn_bqkv, L0_ffn_Wo, L0_ffn_bo, L0_ffn_g1, L0_ffn_be1, L0_ffn_g2, L0_ffn_be2, L0_ffn_Wg, L0_ffn_W1, L0_ffn_b1, L0_ffn_W2, L0_ffn_b2, L1_attn_in_proj_w, L1_attn_conv_w, L1_attn_conv_b, L1_attn_x_proj_w, L1_attn_dt_proj_w, L1_attn_dt_proj_b, L1_attn_A_log, L1_attn_D, L1_attn_out_proj_w, L1_ffn_router_w, L1_ffn_rg, L1_ffn_ru, L1_ffn_rd, L1_ffn_sg, L1_ffn_su, L1_ffn_sd):

    def _L0_attn_ref(x, Wq, Wk, Wv, Wo, bo, lambda_q1, lambda_k1, lambda_q2, lambda_k2, delta_gain, cos_head_delta, cos_logit_scale_raw, subln_weight):
        import jax, jax.numpy as jnp
        import numpy as np
        H = 8
        DIM = 128
        DH = DIM // H // 2
        B, N = (2, 256)
        LAMBDA_INIT = 0.5
        COS_MIN, COS_MAX = (0.0, 15.0)
        ALPHA = 0.5
        COS_EPS = 1e-06
        RMS_EPS = 1e-05
        RAW_INIT = float(np.log(1.0 / 15.0 / (1.0 - 1.0 / 15.0)))

        def _l2norm(t):
            return t / jnp.maximum(jnp.linalg.norm(t, axis=-1, keepdims=True), COS_EPS)
        b, n, c = x.shape
        q = (x @ Wq.T).reshape(b, n, H, 2, DH).transpose(0, 2, 3, 1, 4)
        k = (x @ Wk.T).reshape(b, n, H, 2, DH).transpose(0, 2, 3, 1, 4)
        v = (x @ Wv.T).reshape(b, n, H, 2 * DH).transpose(0, 2, 1, 3)
        q1, q2 = (q[:, :, 0], q[:, :, 1])
        k1, k2 = (k[:, :, 0], k[:, :, 1])
        gscale = COS_MIN + (COS_MAX - COS_MIN) * jax.nn.sigmoid(cos_logit_scale_raw)
        head_delta = cos_head_delta - cos_head_delta.mean()
        cos_scale = (gscale * (1.0 + ALPHA * jnp.tanh(head_delta))).reshape(1, H, 1, 1)
        L1 = jnp.einsum('bhnd,bhmd->bhnm', _l2norm(q1), _l2norm(k1)) * cos_scale
        L2 = jnp.einsum('bhnd,bhmd->bhnm', _l2norm(q2), _l2norm(k2)) * cos_scale
        L1 = jnp.nan_to_num(L1)
        L2 = jnp.nan_to_num(L2)
        G = jnp.tanh(delta_gain.reshape(1, H, 1, 1) * (L1 - L2))
        A1 = jax.nn.softmax((L1 + G).astype(jnp.float32), axis=-1).astype(x.dtype)
        A2 = jax.nn.softmax((L2 - G).astype(jnp.float32), axis=-1).astype(x.dtype)
        lambda_1 = jnp.exp(jnp.sum(lambda_q1 * lambda_k1))
        lambda_2 = jnp.exp(jnp.sum(lambda_q2 * lambda_k2))
        lambda_full = (lambda_1 - lambda_2 + LAMBDA_INIT).astype(x.dtype)
        attn = A1 - lambda_full * A2
        y = jnp.einsum('bhnm,bhmd->bhnd', attn, v)
        y = y * jax.lax.rsqrt(jnp.mean(y * y, axis=-1, keepdims=True) + RMS_EPS) * subln_weight
        y = y * (1.0 - LAMBDA_INIT)
        y = y.transpose(0, 2, 1, 3).reshape(b, n, c)
        return y @ Wo.T + bo

    def _L0_ffn_ref(x, Wqkv, bqkv, Wo, bo, g1, be1, g2, be2, Wg, W1, b1, W2, b2):
        import jax, jax.numpy as jnp
        import numpy as np
        D = 128
        H = 4
        DF = 512
        E = 8
        EPS = 1e-05

        def _layer_norm(x, g, b):
            mu = jnp.mean(x, axis=-1, keepdims=True)
            var = jnp.mean(jnp.square(x - mu), axis=-1, keepdims=True)
            return (x - mu) * jax.lax.rsqrt(var + EPS) * g + b

        def _mha(x, Wqkv, bqkv, Wo, bo):
            S, B, _ = x.shape
            hd = D // H
            qkv = x @ Wqkv.T + bqkv
            q, k, v = jnp.split(qkv, 3, axis=-1)
            to_heads = lambda t: t.reshape(S, B, H, hd).transpose(1, 2, 0, 3)
            q, k, v = (to_heads(q), to_heads(k), to_heads(v))
            scores = jnp.einsum('bhqd,bhkd->bhqk', q, k) * (1.0 / np.sqrt(hd))
            att = jax.nn.softmax(scores, axis=-1)
            o = jnp.einsum('bhqk,bhkd->bhqd', att, v)
            o = o.transpose(2, 0, 1, 3).reshape(S, B, D)
            return o @ Wo.T + bo

        def _moe(x, Wg, W1, b1, W2, b2):
            S, B, _ = x.shape
            xf = x.reshape(S * B, D)
            logits = xf @ Wg.T
            idx = jnp.argmax(logits, axis=-1)
            out = jnp.zeros_like(xf)
            for e in range(E):
                m = (idx == e)[:, None].astype(xf.dtype)
                h = jax.nn.relu(xf @ W1[e] + b1[e])
                out = out + m * (h @ W2[e] + b2[e])
            return out.reshape(S, B, D)
        y = _layer_norm(x + _mha(x, Wqkv, bqkv, Wo, bo), g1, be1)
        z = _layer_norm(y + _moe(y, Wg, W1, b1, W2, b2), g2, be2)
        return z

    def _L1_attn_ref(x, in_proj_w, conv_w, conv_b, x_proj_w, dt_proj_w, dt_proj_b, A_log, D, out_proj_w):
        import jax, jax.numpy as jnp
        import numpy as np
        DIM = 128
        DEPTH = 4
        D_STATE = 16
        D_CONV = 4
        D_INNER = 2 * DIM
        DT_RANK = (DIM + 15) // 16
        B_SZ, L = (4, 256)

        def _selective_scan(u, delta, A, Bm, Cm, D):

            def step(h, inp):
                u_t, d_t, b_t, c_t = inp
                dA = jnp.exp(d_t[:, :, None] * A)
                h = dA * h + (d_t * u_t)[:, :, None] * b_t[:, None, :]
                y = jnp.einsum('bds,bs->bd', h, c_t)
                return (h, y)
            h0 = jnp.zeros((u.shape[0], u.shape[2], A.shape[1]), u.dtype)
            xs = (u.transpose(1, 0, 2), delta.transpose(1, 0, 2), Bm.transpose(1, 0, 2), Cm.transpose(1, 0, 2))
            _, ys = jax.lax.scan(step, h0, xs)
            return ys.transpose(1, 0, 2) + u * D

        def _mamba_layer(x, in_w, cw, cb, xp_w, dtw, dtb, A_log, D, ow):
            xz = jnp.einsum('bld,ed->ble', x, in_w)
            xi, z = jnp.split(xz, 2, axis=-1)
            xc = jax.lax.conv_general_dilated(xi.transpose(0, 2, 1), cw[:, None, :], window_strides=(1,), padding=[(D_CONV - 1, 0)], feature_group_count=D_INNER, dimension_numbers=('NCH', 'OIH', 'NCH'))
            xc = jax.nn.silu(xc.transpose(0, 2, 1) + cb)
            dbc = jnp.einsum('bld,ed->ble', xc, xp_w)
            dt, Bm, Cm = jnp.split(dbc, [DT_RANK, DT_RANK + D_STATE], axis=-1)
            delta = jax.nn.softplus(jnp.einsum('blr,dr->bld', dt, dtw) + dtb)
            A = -jnp.exp(A_log)
            y = _selective_scan(xc, delta, A, Bm, Cm, D)
            y = y * jax.nn.silu(z)
            return jnp.einsum('bld,od->blo', y, ow)
        for i in range(DEPTH):
            x = _mamba_layer(x, in_proj_w[i], conv_w[i], conv_b[i], x_proj_w[i], dt_proj_w[i], dt_proj_b[i], A_log[i], D[i], out_proj_w[i])
        return x

    def _L1_ffn_ref(x, router_w, rg, ru, rd, sg, su, sd):
        import jax, jax.numpy as jnp
        import numpy as np
        B, S, H = (4, 256, 128)
        E, K = (8, 2)
        I_R, I_S = (4 * H, 8 * H)
        CAP_FACTOR = 1.25
        SCALE = 1.0
        b, s, h = x.shape
        T = b * s
        capacity = max(int(CAP_FACTOR * T / E), 1)
        xf = x.reshape(T, h)
        eps = jnp.finfo(x.dtype).eps
        xn = xf * jax.lax.rsqrt(jnp.mean(xf * xf, axis=-1, keepdims=True) + eps)
        logits = xn @ router_w.T
        probs = jax.nn.softmax(logits, axis=-1)
        topk_p, topk_i = jax.lax.top_k(probs, K)
        rw = topk_p / jnp.sum(topk_p, axis=-1, keepdims=True)
        one_hot = jax.nn.one_hot(topk_i, E, dtype=x.dtype)
        mask = one_hot.sum(1)
        wdense = (one_hot * rw[..., None]).sum(1)
        sel = mask.T.astype(bool)
        order = jnp.argsort(~sel, axis=1, stable=True)
        dispatch = order[:, :capacity]
        count = sel.sum(axis=1)
        valid = (jnp.arange(capacity)[None, :] < count[:, None]).astype(x.dtype)
        xg = xf[dispatch]
        gate = jax.nn.silu(jnp.einsum('ech,ehi->eci', xg, rg))
        up = jnp.einsum('ech,ehi->eci', xg, ru)
        eout = jnp.einsum('eci,eih->ech', gate * up, rd)
        w = jnp.take_along_axis(wdense.T, dispatch, axis=1)
        contrib = eout * (w * valid)[..., None]
        routed = jnp.zeros_like(xf).at[dispatch.reshape(-1)].add(contrib.reshape(-1, h))
        shared = jax.nn.silu(x @ sg) * (x @ su) @ sd
        return shared + SCALE * routed.reshape(b, s, h)
    x = L0_attn_x
    xn = _layernorm(x, axis=-1)
    s = _L0_attn_ref(xn, L0_attn_Wq, L0_attn_Wk, L0_attn_Wv, L0_attn_Wo, L0_attn_bo, L0_attn_lambda_q1, L0_attn_lambda_k1, L0_attn_lambda_q2, L0_attn_lambda_k2, L0_attn_delta_gain, L0_attn_cos_head_delta, L0_attn_cos_logit_scale_raw, L0_attn_subln_weight)
    g = _silu(_L0_ffn_ref(xn, L0_ffn_Wqkv, L0_ffn_bqkv, L0_ffn_Wo, L0_ffn_bo, L0_ffn_g1, L0_ffn_be1, L0_ffn_g2, L0_ffn_be2, L0_ffn_Wg, L0_ffn_W1, L0_ffn_b1, L0_ffn_W2, L0_ffn_b2))
    x = x + s * g
    xn = _layernorm(x, axis=-1)
    s = _L1_attn_ref(xn, L1_attn_in_proj_w, L1_attn_conv_w, L1_attn_conv_b, L1_attn_x_proj_w, L1_attn_dt_proj_w, L1_attn_dt_proj_b, L1_attn_A_log, L1_attn_D, L1_attn_out_proj_w)
    g = _silu(_L1_ffn_ref(xn, L1_ffn_router_w, L1_ffn_rg, L1_ffn_ru, L1_ffn_rd, L1_ffn_sg, L1_ffn_su, L1_ffn_sd))
    x = x + s * g
    return x

_drawn_inputs = setup_inputs


def setup_inputs(seed=0):
    import zlib

    import numpy as np

    out = dict(_drawn_inputs(seed))
    spreads = {'L0_attn_bo': (0.0, 0.1),
     'L0_attn_cos_head_delta': (0.0, 0.8),
     'L0_attn_subln_weight': (1.0, 0.2),
     'L0_ffn_bqkv': (0.0, 0.1),
     'L0_ffn_bo': (0.0, 0.1),
     'L0_ffn_g1': (1.0, 0.2),
     'L0_ffn_be1': (0.0, 0.1),
     'L0_ffn_g2': (1.0, 0.2),
     'L0_ffn_be2': (0.0, 0.1),
     'L0_ffn_b1': (0.0, 0.446),
     'L0_ffn_b2': (0.0, 0.31),
     'L1_attn_conv_b': (0.0, 0.1),
     'L1_attn_dt_proj_b': (-4.600165843963623, 0.2),
     'L1_attn_D': (1.0, 0.2)}
    factors = {'L0_attn_lambda_q1': 8.0,
     'L0_attn_lambda_k1': 5.199,
     'L0_attn_lambda_q2': 14.539,
     'L0_attn_lambda_k2': 11.278}
    for name, (base, spread) in spreads.items():
        noise = np.random.default_rng([zlib.crc32(name.encode()), seed]).standard_normal(out[name].shape)
        drawn = base * np.exp(spread * noise) if base else spread * noise
        out[name] = jnp.asarray(drawn.astype(out[name].dtype))
    for name, factor in factors.items():
        out[name] = (out[name] * factor).astype(out[name].dtype)
    return out
```

```python
import concourse.bass as bass
from concourse import mybir
from contextlib import ExitStack

fp32 = mybir.dt.float32
bf16 = mybir.dt.bfloat16
u32 = mybir.dt.uint32
ALU = mybir.AluOpType
ACT = mybir.ActivationFunctionType
AX = mybir.AxisListType

P = 128
B, N, D = 4, 512, 128
T = B * N
NT = T // P
NH = 8
NE = 8
EPS = 1e-5


class Chain:

    def __init__(self, engine, semaphore, start=0):
        self.engine, self.semaphore, self.done = engine, semaphore, start

    def __call__(self, instruction, then=None):
        self.done += 1
        instruction.then_inc(self.semaphore, 1)
        self.engine.wait_ge(self.semaphore, self.done)
        if then is not None:
            self.engine.sem_inc(then, 1)


def first_max(nc, link, lg, cand, lmax, source, rank_desc, onehot):
    link(nc.vector.tensor_copy(lg[:, :, :], source))
    link(nc.vector.tensor_reduce(lmax[:, :], lg[:, :, :], AX.X, ALU.max))
    link(nc.vector.tensor_tensor(cand[:, :, :], lg[:, :, :], lmax[:, :].unsqueeze(2).broadcast_to([P, NT, NE]), ALU.is_ge))
    link(nc.vector.tensor_tensor(cand[:, :, :], cand[:, :, :], rank_desc[:, :, :], ALU.mult))
    link(nc.vector.tensor_reduce(lmax[:, :], cand[:, :, :], AX.X, ALU.max))
    link(nc.vector.tensor_tensor(onehot[:, :, :], cand[:, :, :], lmax[:, :].unsqueeze(2).broadcast_to([P, NT, NE]), ALU.is_equal))




def build_stages(nc, A, out):
    keep = ExitStack()
    with keep:
        def sb(stack, name, shape, dtype=fp32):
            return stack.enter_context(nc.sbuf_tensor(name, shape, dtype))

        X = sb(keep, "X", [P, NT, D])
        XT = sb(keep, "XT", [P, B, 512])
        ident = sb(keep, "ident_sb", [P, P])
        rank_desc = sb(keep, "rank_desc", [P, NT, NE])
        GATE = sb(keep, "GATE", [P, NT, D])
        keepx = ExitStack()
        XN = sb(keepx, "XN", [P, NT, D])
        keep0 = ExitStack()
        with keep0:
            Y1 = sb(keep0, "Y1", [P, NT, D])
            Y1T = sb(keep0, "Y1T", [P, T])
            ACC = sb(keep0, "ACC", [P, NT, D])
            v_tok = sb(keep0, "v_tok", [P, NT, D])
            mask0 = sb(keep0, "mask0", [P, NT, NE])
            ybig = sb(keep0, "ybig", [P, NT, NH * 34])
            delta_gain = sb(keep0, "delta_gain_sb", [P, NH])
            neg_lam = sb(keep0, "neg_lam", [P, 1])
            subln = sb(keep0, "subln_sb", [P, 16])
            bo_row = sb(keep0, "bo_row", [P, D])
            g2_row = sb(keep0, "g2_row", [P, D])
            be2_row = sb(keep0, "be2_row", [P, D])
            wo_att = sb(keep0, "wo_att_sb", [P, D])
            qk_dram = nc.dram_tensor("qk_parts", [2, 3, P, T], bf16).ap()
            st1 = ExitStack()
            with st1:
                psum = [st1.enter_context(nc.psum_tensor(f"s1_bank{i}", [P, 512], fp32)) for i in range(8)]
                w_att = sb(st1, "w_att", [P, 3 * D])
                w_mha = sb(st1, "w_mha", [P, 3 * D])
                w_mo = sb(st1, "w_mo", [P, D])
                w_gate = sb(st1, "w_gate", [P, NE])
                b_mha = sb(st1, "b_mha", [P, 3 * D])
                b_mo = sb(st1, "b_mo", [P, D])
                g1_row = sb(st1, "g1_row", [P, D])
                be1_row = sb(st1, "be1_row", [P, D])
                chd = sb(st1, "chd", [P, NH])
                craw = sb(st1, "craw", [P, 1])
                lam_in = sb(st1, "lam_in", [P, 4, 8])
                stats = sb(st1, "stats", [P, NT, 6])
                mv = sb(st1, "mv", [P, NT, 2])
                rstd = sb(st1, "rstd", [P, NT])
                neghalf = sb(st1, "neghalf", [P, 512])
                qkv = sb(st1, "qkv", [P, NT, 3 * D])
                sq = sb(st1, "sq", [P, 4, 2 * D])
                ss = sb(st1, "ss", [P, NT, 32])
                cosb = sb(st1, "cosb", [P, 16])
                xnT = sb(st1, "xnT", [P, T])
                parts = {(w, i): sb(st1, f"part_{w}{i}", [P, T], bf16) for w in "qk" for i in range(3)}
                rest = {w: sb(st1, f"rest_{w}", [P, 512]) for w in "qk"}
                prod = sb(st1, "prod", [P, 2, 4, D])
                att = sb(st1, "att", [P, 4, 4, 4, 4])
                amax = sb(st1, "amax", [P, 64])
                mo = sb(st1, "mo", [P, NT, D])
                mh = sb(st1, "mh", [P, NT, 3 * D])
                smalls = sb(st1, "smalls", [P, 64])
                lg = sb(st1, "lg", [P, NT, NE])
                lgt = sb(st1, "lgt", [P, NT, NE])
                lmax = sb(st1, "lmax", [P, NT])

                sem = lambda name: st1.enter_context(nc.semaphore(name))
                s_x = [sem(f"x_loaded{b}") for b in range(B)]
                s_w = sem("weights_loaded")
                s_stat, s_rstd, s_xn, s_xnt_ps, s_xnt = map(sem, ("stats_ready", "rstd_ready", "xn_ready", "xnT_in_psum", "xnT_ready"))
                s_proj, s_qkv, s_mh = map(sem, ("proj_in_psum", "qkv_ready", "mha_in_ready"))
                s_sq, s_ss, s_rn, s_nrm, s_qkn = map(sem, ("squares_ready", "sumsq_ready", "sumsq_bounded", "norms_ready", "qk_normed"))
                s_qkt, s_hi, s_r1, s_mid, s_lo, s_qkst = map(sem, ("qkT_in_psum", "hi_ready", "rest_ready", "mid_ready", "lo_ready", "parts_stored"))
                s_cos, s_act, s_nh = map(sem, ("cos_steps", "act_steps", "neghalf_ready"))
                s_pr, s_sc, s_ex, s_at, s_pv, s_o = map(sem, ("qk_products", "scores_ready", "exps_ready", "att_ready", "pv_products", "mha_out"))
                s_ot_ps, s_ot, s_wo, s_y0, s_ys, s_yr, s_y1 = map(sem, ("oT_in_psum", "oT_ready", "wo_in_psum", "y_summed", "y_stats", "y_rstd", "y_normed"))
                s_yt_ps, s_yt, s_lgp, s_dch, s_pch, s_ach = map(sem, ("yT_in_psum", "yT_ready", "logits_in_psum", "vector_steps", "pool_steps", "scalar_steps"))
                NW = 0

                with nc.Block() as block:
                    loads = [(ident[:, :], A["ident"]), (w_att[:, :], A["w_att"]), (w_mha[:, :], A["w_mha"]), (w_mo[:, :], A["w_mo"]),
                             (w_gate[:, :], A["w_gate0"]), (b_mha[:, :], A["b_mha"].partition_broadcast(P)),
                             (b_mo[:, :], A["b_mo"].partition_broadcast(P)), (g1_row[:, :], A["g1"].partition_broadcast(P)),
                             (be1_row[:, :], A["be1"].partition_broadcast(P)), (chd[:, :], A["cos_head_delta"].partition_broadcast(P)),
                             (craw[:, :], A["cos_raw"].partition_broadcast(P)), (delta_gain[:, :], A["delta_gain"].partition_broadcast(P)),
                             (bo_row[:, :], A["bo"].partition_broadcast(P)), (subln[:, :], A["subln"].partition_broadcast(P)),
                             (g2_row[:, :], A["g2"].partition_broadcast(P)), (be2_row[:, :], A["be2"].partition_broadcast(P)),
                             (wo_att[:, :], A["wo_att"])]
                    loads += [(lam_in[:, i, :], A[n].partition_broadcast(P)) for i, n in enumerate(("lq1", "lk1", "lq2", "lk2"))]
                    ALL_W = 16 * len(loads)

                    @block.sync
                    def _(sp):
                        for b in range(B):
                            sp.dma_start(X[:, 4 * b:4 * b + 4, :], A["x"][b].rearrange("(k p) d -> p k d", p=P)).then_inc(s_x[b], 16)
                        for dst, src in loads:
                            sp.dma_start(dst, src).then_inc(s_w, 16)
                        for b in range(B):
                            sp.wait_ge(s_mid, 2 * b + 2)
                            sp.wait_ge(s_lo, 2 * b + 2)
                            for n, w in enumerate("qk"):
                                for i in range(3):
                                    sp.dma_start(qk_dram[n, i, :, 512 * b:512 * b + 512], parts[w, i][:, 512 * b:512 * b + 512]).then_inc(s_qkst, 16)
                        sp.wait_ge(s_qkst, 16 * 6 * B)

                    @block.vector
                    def _(dve):
                        link = Chain(dve, s_dch)
                        nc.vector.memset(neghalf[:, :], -0.5).then_inc(s_nh, 1)
                        for b in range(B):
                            dve.wait_ge(s_x[b], 16)
                            for t in range(4 * b, 4 * b + 4):
                                last = nc.vector.bn_stats(stats[:, t, :], X[:, t, :])
                            link(last)
                            for t in range(4 * b, 4 * b + 4):
                                last = nc.vector.bn_aggr(mv[:, t, :], stats[:, t, :])
                            last.then_inc(s_stat, 1)
                        for b in range(B):
                            dve.wait_ge(s_rstd, b + 1)
                            for t in range(4 * b, 4 * b + 4):
                                last = nc.vector.tensor_scalar(XN[:, t, :], X[:, t, :], mv[:, t, 0:1], rstd[:, t:t + 1], ALU.subtract, ALU.mult)
                            last.then_inc(s_xn, 1)
                        dve.wait_ge(s_w, ALL_W)
                        link(nc.vector.tensor_reduce(smalls[:, 0:1], chd[:, :], AX.X, ALU.add))
                        link(nc.vector.tensor_scalar(smalls[:, 1:2], smalls[:, 0:1], 1.0 / NH, None, ALU.mult))
                        nc.vector.tensor_scalar(smalls[:, 8:16], chd[:, :], smalls[:, 1:2], None, ALU.subtract).then_inc(s_cos, 1)
                        link(nc.vector.tensor_tensor(smalls[:, 16:24], lam_in[:, 0, :], lam_in[:, 1, :], ALU.mult))
                        link(nc.vector.tensor_tensor(smalls[:, 24:32], lam_in[:, 2, :], lam_in[:, 3, :], ALU.mult))
                        nc.vector.tensor_reduce(smalls[:, 2:4], smalls[:, 16:32].rearrange("p (a b) -> p a b", b=8), AX.X, ALU.add).then_inc(s_cos, 1)
                        dve.wait_ge(s_act, 3)
                        link(nc.vector.tensor_scalar(smalls[:, 6:7], smalls[:, 4:5], 1.0, None, ALU.add))
                        link(nc.vector.reciprocal(smalls[:, 7:8], smalls[:, 6:7]))
                        link(nc.vector.tensor_scalar(smalls[:, 40:48], smalls[:, 32:40], 0.5, 1.0, ALU.mult, ALU.add))
                        link(nc.vector.tensor_scalar(smalls[:, 48:56], smalls[:, 40:48], smalls[:, 7:8], 15.0, ALU.mult, ALU.mult))
                        cv = cosb[:, :].rearrange("p (h s) -> p h s", s=2)
                        link(nc.vector.tensor_scalar(cv[:, :, 0], smalls[:, 48:56], 1.0, None, ALU.mult))
                        link(nc.vector.tensor_scalar(cv[:, :, 1], smalls[:, 48:56], -1.0, None, ALU.mult))
                        link(nc.vector.tensor_tensor(smalls[:, 56:57], smalls[:, 59:60], smalls[:, 58:59], ALU.subtract))
                        link(nc.vector.tensor_scalar(neg_lam[:, :], smalls[:, 56:57], 0.5, None, ALU.subtract))
                        def norm_and_split(b):
                            dve.wait_ge(s_sq, b + 1)
                            ssb = ss[:, 4 * b:4 * b + 4, :]
                            nc.vector.tensor_reduce(ssb.rearrange("p t g -> p (t g)"), sq[:, :, :].rearrange("p t (g d) -> p (t g) d", d=8),
                                                    AX.X, ALU.add).then_inc(s_ss, 1)
                            dve.wait_ge(s_nrm, b + 1)
                            link(nc.vector.reciprocal(ssb.rearrange("p t g -> p (t g)"), ssb.rearrange("p t g -> p (t g)")))
                            link(nc.vector.tensor_tensor(ssb[:, :, 0:16], ssb[:, :, 0:16], cosb[:, :].unsqueeze(1).broadcast_to([P, 4, 16]), ALU.mult))
                            qk = qkv[:, 4 * b:4 * b + 4, 0:2 * D].rearrange("p t (g d) -> p t g d", d=8)
                            nc.vector.tensor_tensor(qk, qk, ssb.unsqueeze(3).broadcast_to([P, 4, 32, 8]), ALU.mult).then_inc(s_qkn, 1)
                            for n, w in enumerate("qk"):
                                c = slice(512 * b, 512 * b + 512)
                                dve.wait_ge(s_hi, 2 * b + n + 1)
                                if b:
                                    dve.wait_ge(s_lo, 2 * b + n - 1)
                                    dve.wait_ge(s_mid, 2 * b + n - 1)
                                nc.vector.tensor_tensor(rest[w][:, :], psum[4 + n][:, :], parts[w, 0][:, c], ALU.subtract).then_inc(s_r1, 1)
                                dve.wait_ge(s_mid, 2 * b + n + 1)
                                nc.vector.tensor_tensor(parts[w, 2][:, c], rest[w][:, :], parts[w, 1][:, c], ALU.subtract).then_inc(s_lo, 1)
                        for b in range(B):
                            for t in range(4 * b, 4 * b + 4):
                                dve.wait_ge(s_proj, t + 1)
                                nc.vector.tensor_tensor(mh[:, t, :], psum[2 * (t % 2) + 1][:, 0:3 * D], b_mha[:, :], ALU.add).then_inc(s_mh, 1)
                            if b:
                                norm_and_split(b - 1)
                        norm_and_split(B - 1)
                        for u in range(16):
                            nb, b1 = u // 4, u % 4
                            dve.wait_ge(s_pr, u + 1)
                            nc.vector.tensor_reduce(att[:, nb, b1, :, :].rearrange("p k h -> p (k h)"),
                                                    prod[:, u % 2, :, :].rearrange("p k (h d) -> p (k h) d", d=32), AX.X, ALU.add).then_inc(s_sc, 1)
                        a_kh = att[:, :, :, :, :].rearrange("p n q k h -> p (n q) k h")
                        a_hk = att[:, :, :, :, :].rearrange("p n q k h -> p (n q) h k")
                        am = amax[:, :].rearrange("p (a h) -> p a h", h=4)
                        dve.wait_ge(s_sc, 16)
                        link(nc.vector.tensor_reduce(am, a_hk, AX.X, ALU.max))
                        nc.vector.tensor_tensor(a_kh, a_kh, am.unsqueeze(2).broadcast_to([P, 16, 4, 4]), ALU.subtract).then_inc(s_sc, 1)
                        dve.wait_ge(s_ex, 1)
                        link(nc.vector.tensor_reduce(am, a_hk, AX.X, ALU.add))
                        link(nc.vector.reciprocal(amax[:, :], amax[:, :]))
                        nc.vector.tensor_tensor(a_kh, a_kh, am.unsqueeze(2).broadcast_to([P, 16, 4, 4]), ALU.mult).then_inc(s_at, 1)
                        for u in range(16):
                            nb, b1 = u // 4, u % 4
                            dve.wait_ge(s_pv, u + 1)
                            nc.vector.tensor_reduce(mo[:, 4 * b1 + nb, :], prod[:, u % 2, :, :].rearrange("p k d -> p d k"), AX.X, ALU.add).then_inc(s_o, 1)
                        for b in range(B):
                            dve.wait_ge(s_wo, b + 1)
                            tl = slice(4 * b, 4 * b + 4)
                            link(nc.vector.tensor_tensor(Y1[:, tl, :], psum[6 + b % 2][:, :].rearrange("p (t d) -> p t d", d=D), XN[:, tl, :], ALU.add))
                            nc.vector.tensor_tensor(Y1[:, tl, :], Y1[:, tl, :], b_mo[:, :].unsqueeze(1).broadcast_to([P, 4, D]), ALU.add).then_inc(s_y0, 1)
                            dve.wait_ge(s_y0, b + 1)
                            for t in range(4 * b, 4 * b + 4):
                                last = nc.vector.bn_stats(stats[:, t, :], Y1[:, t, :])
                            link(last)
                            for t in range(4 * b, 4 * b + 4):
                                last = nc.vector.bn_aggr(mv[:, t, :], stats[:, t, :])
                            last.then_inc(s_ys, 1)
                        for b in range(B):
                            tl = slice(4 * b, 4 * b + 4)
                            dve.wait_ge(s_yr, b + 1)
                            for t in range(4 * b, 4 * b + 4):
                                last = nc.vector.tensor_scalar(Y1[:, t, :], Y1[:, t, :], mv[:, t, 0:1], rstd[:, t:t + 1], ALU.subtract, ALU.mult)
                            link(last)
                            link(nc.vector.tensor_tensor(Y1[:, tl, :], Y1[:, tl, :], g1_row[:, :].unsqueeze(1).broadcast_to([P, 4, D]), ALU.mult))
                            nc.vector.tensor_tensor(Y1[:, tl, :], Y1[:, tl, :], be1_row[:, :].unsqueeze(1).broadcast_to([P, 4, D]), ALU.add).then_inc(s_y1, 1)
                        dve.wait_ge(s_lgp, 1)
                        first_max(nc, link, lg, lgt, lmax, psum[0][:, 0:NT * NE].rearrange("p (t e) -> p t e", e=NE), rank_desc, mask0)

                    @block.gpsimd
                    def _(pool):
                        link = Chain(pool, s_pch)
                        pool.wait_ge(s_nh, 1)
                        for e in range(NE):
                            link(nc.gpsimd.memset(rank_desc[:, :, e:e + 1], float(NE - e)))
                        for b in range(B):
                            pool.wait_ge(s_stat, b + 1)
                            link(nc.gpsimd.tensor_scalar(rstd[:, 4 * b:4 * b + 4], mv[:, 4 * b:4 * b + 4, 1], EPS, None, ALU.add))
                            nc.gpsimd.tensor_tensor(rstd[:, 4 * b:4 * b + 4], rstd[:, 4 * b:4 * b + 4], neghalf[:, 0:4], ALU.pow).then_inc(s_rstd, 1)
                        for b in range(B):
                            tl = slice(4 * b, 4 * b + 4)
                            pool.wait_ge(s_qkv, 4 * b + 4)
                            if b:
                                pool.wait_ge(s_ss, b)
                            nc.gpsimd.tensor_tensor(sq[:, :, :], qkv[:, tl, 0:2 * D], qkv[:, tl, 0:2 * D], ALU.mult).then_inc(s_sq, 1)
                            pool.wait_ge(s_ss, b + 1)
                            ssb = ss[:, tl, :].rearrange("p t g -> p (t g)")
                            nc.gpsimd.tensor_scalar(ssb, ssb, 1e-12, None, ALU.max).then_inc(s_rn, 1)
                        pool.wait_ge(s_mh, NT)
                        mt = mh[:, :, :].rearrange("p (b n) c -> p n b c", n=4)
                        for u in range(16):
                            nb, b1 = u // 4, u % 4
                            if u >= 2:
                                pool.wait_ge(s_sc, u - 1)
                            nc.gpsimd.tensor_tensor(prod[:, u % 2, :, :], mt[:, nb, b1, 0:D].unsqueeze(1).broadcast_to([P, 4, D]),
                                                    mt[:, nb, :, D:2 * D], ALU.mult).then_inc(s_pr, 1)
                        pool.wait_ge(s_at, 1)
                        for u in range(16):
                            nb, b1 = u // 4, u % 4
                            if u >= 2:
                                pool.wait_ge(s_o, u - 1)
                            for b2 in range(4):
                                last = nc.gpsimd.tensor_tensor(prod[:, u % 2, b2, :].rearrange("p (h d) -> p h d", d=32),
                                                    mt[:, nb, b2, 2 * D:3 * D].rearrange("p (h d) -> p h d", d=32),
                                                    att[:, nb, b1, b2, :].unsqueeze(2).broadcast_to([P, 4, 32]), ALU.mult)
                            last.then_inc(s_pv, 1)
                        for b in range(B):
                            pool.wait_ge(s_ys, b + 1)
                            link(nc.gpsimd.tensor_scalar(rstd[:, 4 * b:4 * b + 4], mv[:, 4 * b:4 * b + 4, 1], EPS, None, ALU.add))
                            nc.gpsimd.tensor_tensor(rstd[:, 4 * b:4 * b + 4], rstd[:, 4 * b:4 * b + 4], neghalf[:, 0:4], ALU.pow).then_inc(s_yr, 1)

                    @block.scalar
                    def _(act):
                        act.preload_act_table_set("exp_and_others")

                        def parts_of(b):
                            act.wait_ge(s_rn, b + 1)
                            ssb = ss[:, 4 * b:4 * b + 4, :].rearrange("p t g -> p (t g)")
                            nc.scalar.activation(ssb, ssb, ACT.Sqrt).then_inc(s_nrm, 1)
                            c = slice(512 * b, 512 * b + 512)
                            for n, w in enumerate("qk"):
                                act.wait_ge(s_qkt, 2 * b + n + 1)
                                nc.scalar.activation(parts[w, 0][:, c], psum[4 + n][:, :], ACT.Copy).then_inc(s_hi, 1)
                            for n, w in enumerate("qk"):
                                act.wait_ge(s_r1, 2 * b + n + 1)
                                nc.scalar.activation(parts[w, 1][:, c], rest[w][:, :], ACT.Copy).then_inc(s_mid, 1)

                        for b in range(B):
                            act.wait_ge(s_xnt_ps, b + 1)
                            nc.scalar.activation(xnT[:, 512 * b:512 * b + 512], psum[6 + b % 2][:, :], ACT.Copy).then_inc(s_xnt, 1)
                            if b == 0:
                                act.wait_ge(s_w, ALL_W)
                                nc.scalar.activation(smalls[:, 4:5], craw[:, :], ACT.Exp, scale=-1.0).then_inc(s_act, 1)
                                act.wait_ge(s_cos, 2)
                                nc.scalar.activation(smalls[:, 32:40], smalls[:, 8:16], ACT.Tanh).then_inc(s_act, 1)
                                nc.scalar.activation(smalls[:, 58:60], smalls[:, 2:4], ACT.Exp).then_inc(s_act, 1)
                            for t in range(4 * b, 4 * b + 4):
                                act.wait_ge(s_proj, t + 1)
                                nc.scalar.activation(qkv[:, t, :], psum[2 * (t % 2)][:, 0:3 * D], ACT.Copy).then_inc(s_qkv, 1)
                            if b:
                                parts_of(b - 1)
                        parts_of(B - 1)
                        nc.scalar.activation(v_tok[:, :, :], qkv[:, :, 2 * D:3 * D], ACT.Copy).then_inc(s_ach, 1)
                        act.wait_ge(s_sc, 17)
                        af = att[:, :, :, :, :].rearrange("p n q k h -> p (n q k h)")
                        nc.scalar.activation(af, af, ACT.Exp, scale=32.0 ** -0.5).then_inc(s_ex, 1)
                        for b in range(B):
                            act.wait_ge(s_ot_ps, b + 1)
                            nc.scalar.activation(xnT[:, 512 * b:512 * b + 512], psum[b % 2][:, :], ACT.Copy).then_inc(s_ot, 1)
                        for b in range(B):
                            act.wait_ge(s_yt_ps, b + 1)
                            nc.scalar.activation(Y1T[:, 512 * b:512 * b + 512], psum[2 + b % 2][:, :], ACT.Copy).then_inc(s_yt, 1)

                    @block.tensor
                    def _(pe):
                        pe.wait_ge(s_w, ALL_W)

                        def qk_transposes(b):
                            pe.wait_ge(s_qkn, b + 1)
                            for n in range(2):
                                if b:
                                    pe.wait_ge(s_r1, 2 * b + n - 1)
                                for t in range(4):
                                    last = nc.tensor.transpose(psum[4 + n][:, P * t:P * t + P], qkv[:, 4 * b + t, n * D:n * D + D], ident[:, :])
                                last.then_inc(s_qkt, 1)

                        for b in range(B):
                            pe.wait_ge(s_xn, b + 1)
                            if b >= 2:
                                pe.wait_ge(s_xnt, b - 1)
                            for t in range(4):
                                last = nc.tensor.transpose(psum[6 + b % 2][:, P * t:P * t + P], XN[:, 4 * b + t, :], ident[:, :])
                            last.then_inc(s_xnt_ps, 1)
                            pe.wait_ge(s_xnt, b + 1)
                            for t in range(4 * b, 4 * b + 4):
                                if t >= 2:
                                    pe.wait_ge(s_qkv, t - 1)
                                    pe.wait_ge(s_mh, t - 1)
                                nc.tensor.matmul(psum[2 * (t % 2)][:, 0:3 * D], xnT[:, P * t:P * t + P], w_att[:, :], start=True, stop=True)
                                nc.tensor.matmul(psum[2 * (t % 2) + 1][:, 0:3 * D], xnT[:, P * t:P * t + P], w_mha[:, :], start=True, stop=True).then_inc(s_proj, 1)
                            if b:
                                qk_transposes(b - 1)
                        qk_transposes(B - 1)
                        for b in range(B):
                            pe.wait_ge(s_o, 12 + b + 1)
                            pe.wait_ge(s_qkv, NT)
                            pe.wait_ge(s_mh, NT)
                            if b >= 2:
                                pe.wait_ge(s_ot, b - 1)
                            for t in range(4):
                                last = nc.tensor.transpose(psum[b % 2][:, P * t:P * t + P], mo[:, 4 * b + t, :], ident[:, :])
                            last.then_inc(s_ot_ps, 1)
                        for b in range(B):
                            pe.wait_ge(s_ot, b + 1)
                            if b >= 2:
                                pe.wait_ge(s_y0, b - 1)
                            for t in range(4):
                                last = nc.tensor.matmul(psum[6 + b % 2][:, P * t:P * t + P], xnT[:, 512 * b + P * t:512 * b + P * t + P], w_mo[:, :], start=True, stop=True)
                            last.then_inc(s_wo, 1)
                        for b in range(B):
                            pe.wait_ge(s_y1, b + 1)
                            if b >= 2:
                                pe.wait_ge(s_yt, b - 1)
                            for t in range(4):
                                last = nc.tensor.transpose(psum[2 + b % 2][:, P * t:P * t + P], Y1[:, 4 * b + t, :], ident[:, :])
                            last.then_inc(s_yt_ps, 1)
                        pe.wait_ge(s_yt, B)
                        pe.wait_ge(s_ot, B)
                        for t in range(NT):
                            last = nc.tensor.matmul(psum[0][:, NE * t:NE * t + NE], Y1T[:, P * t:P * t + P], w_gate[:, :], start=True, stop=True)
                        last.then_inc(s_lgp, 1)
            st2 = ExitStack()
            with st2:
                bank_d = st2.enter_context(nc.psum_tensor("bank_d", [P, 512], fp32))
                bank_l = [st2.enter_context(nc.psum_tensor(f"bank_l{i}", [P, 2, 512], fp32)) for i in range(2)]
                bank_pv = st2.enter_context(nc.psum_tensor("bank_pv", [P, 512], fp32))
                bank_h = st2.enter_context(nc.psum_tensor("bank_h", [P, 512], fp32))
                bank_o = st2.enter_context(nc.psum_tensor("bank_o", [P, 4, D], fp32))
                kst = [sb(st2, f"k_stack{i}", [112, T], bf16) for i in range(2)]
                qst = [sb(st2, f"q_stack{i}", [112, T], bf16) for i in range(2)]
                w1 = [sb(st2, f"w1_{i}", [P, 512]) for i in range(2)]
                w2 = [sb(st2, f"w2_{i}", [P, 4, D]) for i in range(2)]
                b1 = [sb(st2, f"b1_{i}", [P, 4]) for i in range(2)]
                vh = [sb(st2, f"v_head{i}", [P, NT, 32]) for i in range(2)]
                dgh = sb(st2, "dgh", [P, 2])
                gt = sb(st2, "gt", [P, 2, 512])
                tt = sb(st2, "tt", [P, 2, 2, 512])
                ex = sb(st2, "ex", [P, 2, 4, 2, 512])
                hid = sb(st2, "hid", [P, 2, 4, 512])
                pvs = sb(st2, "pvs", [P, 512])
                tmp = sb(st2, "tmp", [P, 4, D])

                sem = lambda name: st2.enter_context(nc.semaphore(name))
                s_ld = [sem(f"head_loaded{i}") for i in range(2)]
                s_z, s_vh, s_dg = sem("stacks_cleared"), sem("v_head_ready"), sem("gain_of_head")
                s_D, s_L, s_G, s_T, s_E = map(sem, ("diff_in_psum", "logits_in_psum2", "gate_ready", "sums_ready", "exp_ready"))
                s_pvd, s_pvs, s_pvt, s_yb = map(sem, ("pv_done", "pv_copied", "pv_turned", "pv_kept"))
                s_h, s_relu, s_dn, s_acc, s_dch = map(sem, ("hidden_in_psum", "hidden_ready", "expert_out", "expert_added", "vector_steps2"))
                LEAD, STEPS, UNITS, LOADS = 2, 32, 8, 15
                step = lambda q, n: LEAD + STEPS * q + n
                unit = lambda q, n: LEAD + UNITS * q + n

                with nc.Block() as block:
                    def load_head(sp, h, i):
                        for s in range(2):
                            rows = bass.ds(h * 16 + 8 * s, 8)
                            for n, (stack, order) in enumerate(((qst[i], (0, 1, 2, 0, 1, 0)), (kst[i], (0, 0, 0, 1, 1, 2)))):
                                if n == 0:
                                    groups = [(0, 0, 3), (3, 0, 2), (5, 0, 1)]
                                    for at, part, k in groups:
                                        sp.dma_start(stack[64 * s + 8 * at:64 * s + 8 * (at + k), :], qk_dram[0, part:part + k, rows, :]).then_inc(s_ld[i], 16)
                                else:
                                    groups = [(0, 0, 3), (3, 1, 2), (5, 2, 1)]
                                    for at, part, k in groups:
                                        sp.dma_start(stack[64 * s + 8 * at:64 * s + 8 * (at + k), :],
                                                     qk_dram[1, part:part + 1, rows, :].broadcast_to([k, 8, T])).then_inc(s_ld[i], 16)
                        sp.dma_start(w1[i][:, :], A["w1"][bass.ds(h, 1), :, :].rearrange("o p f -> p (o f)")).then_inc(s_ld[i], 16)
                        sp.dma_start(w2[i][:, :, :], A["w2"][bass.ds(h, 1), :, :].rearrange("o (k p) d -> p (o k) d", p=P)).then_inc(s_ld[i], 16)
                        sp.dma_start(b1[i][:, :], A["b1"][bass.ds(h, 1), :, :].rearrange("o p k -> p (o k)")).then_inc(s_ld[i], 16)

                    @block.sync
                    def _(sp):
                        sp.wait_ge(s_z, 4)
                        for i in range(2):
                            load_head(sp, i, i)
                        with sp.Fori(0, 3) as q:
                            for i in range(2):
                                sp.wait_ge(s_dn, unit(q, 4 * i + 4))
                                sp.wait_ge(s_z, 4)
                                load_head(sp, q * 2 + (2 + i), i)

                    @block.gpsimd
                    def _(pool):
                        for t in (kst[0], kst[1], qst[0], qst[1]):
                            nc.gpsimd.memset(t[:, :], 0.0).then_inc(s_z, 1)
                        nc.gpsimd.memset(ACC[:, :, :], 0.0).then_inc(s_z, 1)
                        for i in range(2):
                            nc.gpsimd.memset(vh[i][:, :, :], 0.0).then_inc(s_z, 1)
                        pool.wait_ge(s_z, 7)
                        for i in range(2):
                            nc.gpsimd.memset(vh[i][:, :, 16:17], 1.0).then_inc(s_z, 1)

                        def copy_v(h, i):
                            nc.gpsimd.tensor_copy(dgh[:, i:i + 1], delta_gain[:, bass.ds(h, 1)]).then_inc(s_dg, 1)
                            nc.gpsimd.tensor_copy(vh[i][:, :, 0:16], v_tok[:, :, bass.ds(h * 16, 16)]).then_inc(s_vh, 1)

                        for i in range(2):
                            copy_v(i, i)
                        with pool.Fori(0, 3) as q:
                            for i in range(2):
                                pool.wait_ge(s_pvd, unit(q, 4 * i + 4))
                                copy_v(q * 2 + (2 + i), i)

                    @block.tensor
                    def _(pe):
                        for s in (s_D, s_L, s_pvd, s_pvt, s_h, s_dn):
                            pe.sem_inc(s, LEAD)
                        pe.wait_ge(s_z, 9)

                        def scores(q, st):
                            u, mb = st // 4, st % 4
                            i, b = u // 4, u % 4
                            if st % 16 == 0:
                                pe.wait_ge(s_ld[i], q * (16 * LOADS) + 16 * LOADS)
                            k = slice(512 * b + P * mb, 512 * b + P * mb + P)
                            n = slice(512 * b, 512 * b + 512)
                            pe.wait_ge(s_G, step(q, st))
                            nc.tensor.matmul(bank_d[:, :], kst[i][:, k], qst[i][:, n], start=True, stop=True).then_inc(s_D, 1)
                            pe.wait_ge(s_T, step(q, st - 1))
                            nc.tensor.matmul(bank_l[st % 2][:, 0, :], kst[i][0:48, k], qst[i][0:48, n], start=True, stop=True)
                            nc.tensor.matmul(bank_l[st % 2][:, 1, :], kst[i][64:112, k], qst[i][64:112, n], start=True, stop=True).then_inc(s_L, 1)

                        def hidden(q, st):
                            u, f = st // 4, st % 4
                            i, b = u // 4, u % 4
                            pe.wait_ge(s_relu, step(q, st))
                            nc.tensor.matmul(bank_h[:, :], w1[i][:, P * f:P * f + P], Y1T[:, 512 * b:512 * b + 512], start=True, stop=True).then_inc(s_h, 1)

                        def weigh(q, u, pair):
                            i, b = u // 4, u % 4
                            if pair == 0:
                                pe.wait_ge(s_yb, unit(q, u))
                                pe.wait_ge(s_vh, q * 2 + (i + 1))
                            pe.wait_ge(s_E, step(q, 4 * u + 2 * pair + 2))
                            for m in range(2):
                                for s in range(2):
                                    j = 2 * s + m
                                    mb = 2 * pair + m
                                    last = nc.tensor.matmul(bank_pv[32 * j:32 * j + 32, :], vh[i][:, 4 * b + mb, :], ex[:, u % 2, mb, s, :],
                                                            start=(pair == 0), stop=(pair == 1), tile_position=(0, 32 * j), skip_group_check=True)
                            if pair == 1:
                                last.then_inc(s_pvd, 1)

                        def turn(q, u):
                            pe.wait_ge(s_pvs, unit(q, u + 1))
                            for t in range(4):
                                last = nc.tensor.transpose(bank_pv[:, P * t:P * t + P], pvs[:, P * t:P * t + P], ident[:, :])
                            last.then_inc(s_pvt, 1)

                        def expert_out(q, u):
                            i, b = u // 4, u % 4
                            pe.wait_ge(s_relu, step(q, 4 * u + 4))
                            pe.wait_ge(s_acc, unit(q, u))
                            for t in range(4):
                                for f in range(4):
                                    last = nc.tensor.matmul(bank_o[:, t, :], hid[:, u % 2, f, P * t:P * t + P], w2[i][:, f, :], start=(f == 0), stop=(f == 3))
                            last.then_inc(s_dn, 1)

                        with pe.Fori(0, 4) as q:
                            scores(q, 0)
                            for st in range(STEPS):
                                u, mb = st // 4, st % 4
                                if st < STEPS - 1:
                                    scores(q, st + 1)
                                hidden(q, st)
                                if mb == 1 and u:
                                    weigh(q, u - 1, 1)
                                if mb == 2 and u:
                                    expert_out(q, u - 1)
                                    turn(q, u - 1)
                                if mb == 3:
                                    weigh(q, u, 0)
                            weigh(q, UNITS - 1, 1)
                            expert_out(q, UNITS - 1)
                            turn(q, UNITS - 1)

                    @block.scalar
                    def _(act):
                        act.preload_act_table_set("exp_and_others")
                        for s in (s_G, s_E, s_pvs):
                            act.sem_inc(s, LEAD)
                        with act.Fori(0, 4) as q:
                            def gate(st):
                                if st % 16 == 0:
                                    act.wait_ge(s_dg, q * 2 + (st // 16 + 1))
                                act.wait_ge(s_D, step(q, st + 1))
                                act.wait_ge(s_T, step(q, st - 1))
                                nc.scalar.activation(gt[:, st % 2, :], bank_d[:, :], ACT.Tanh, scale=dgh[:, st // 16:st // 16 + 1]).then_inc(s_G, 1)

                            def exps(st):
                                act.wait_ge(s_T, step(q, st + 1))
                                if st % 4 == 0:
                                    act.wait_ge(s_pvd, unit(q, st // 4 - 1))
                                nc.scalar.activation(ex[:, (st // 4) % 2, st % 4, :, :], tt[:, st % 2, :, :], ACT.Exp).then_inc(s_E, 1)

                            def keep(u):
                                act.wait_ge(s_pvd, unit(q, u + 1))
                                act.wait_ge(s_pvt, unit(q, u))
                                nc.scalar.activation(pvs[:, :], bank_pv[:, :], ACT.Copy).then_inc(s_pvs, 1)

                            gate(0)
                            for st in range(1, STEPS):
                                gate(st)
                                exps(st - 1)
                                if st % 4 == 2 and st > 4:
                                    keep(st // 4 - 1)
                            exps(STEPS - 1)
                            keep(UNITS - 1)

                    @block.vector
                    def _(dve):
                        for s in (s_T, s_yb, s_relu, s_acc):
                            dve.sem_inc(s, LEAD)
                        dve.wait_ge(s_z, 9)
                        with dve.Fori(0, 4) as q:
                            def settle(u):
                                b = u % 4
                                e = q * 2 + u // 4
                                dve.wait_ge(s_dn, unit(q, u + 1))
                                nc.vector.tensor_tensor(tmp[:, :, :], bank_o[:, :, :], mask0[:, 4 * b:4 * b + 4, bass.ds(e, 1)].broadcast_to([P, 4, D]),
                                                        ALU.mult).then_inc(s_dch, 1)
                                dve.wait_ge(s_dch, UNITS * q + (u + 1))
                                nc.vector.tensor_tensor(ACC[:, 4 * b:4 * b + 4, :], ACC[:, 4 * b:4 * b + 4, :], tmp[:, :, :], ALU.add).then_inc(s_acc, 1)
                                dve.wait_ge(s_pvt, unit(q, u + 1))
                                nc.vector.tensor_reduce(ybig[:, 4 * b:4 * b + 4, bass.ds(e * 34, 34)].rearrange("p t (s c) -> p t s c", s=2),
                                                        bank_pv[:, :].rearrange("p (t s m c) -> p t s c m", t=4, s=2, m=2)[:, :, :, 0:17, :],
                                                        AX.X, ALU.add).then_inc(s_yb, 1)

                            for st in range(STEPS):
                                u, mb = st // 4, st % 4
                                i = u // 4
                                dve.wait_ge(s_L, step(q, st + 1))
                                dve.wait_ge(s_G, step(q, st + 1))
                                dve.wait_ge(s_E, step(q, st - 1))
                                nc.vector.tensor_tensor(tt[:, st % 2, 0, :], bank_l[st % 2][:, 0, :], gt[:, st % 2, :], ALU.add)
                                nc.vector.scalar_tensor_tensor(tt[:, st % 2, 1, :], bank_l[st % 2][:, 1, :], -1.0, gt[:, st % 2, :],
                                                               ALU.mult, ALU.subtract).then_inc(s_T, 1)
                                dve.wait_ge(s_h, step(q, st + 1))
                                if mb == 0:
                                    dve.wait_ge(s_dn, unit(q, u - 1))
                                if mb == 0 and u % 4 == 0:
                                    dve.wait_ge(s_ld[i], q * (16 * LOADS) + 16 * LOADS)
                                nc.vector.tensor_scalar(hid[:, u % 2, mb, :], bank_h[:, :], b1[i][:, mb:mb + 1], 0.0, ALU.add, ALU.max).then_inc(s_relu, 1)
                                if mb == 3 and u:
                                    settle(u - 1)
                            settle(UNITS - 1)
            st3 = ExitStack()
            with st3:
                bank = [st3.enter_context(nc.psum_tensor(f"s3_bank{i}", [P, 4, D], fp32)) for i in range(8)]
                b2blk = sb(st3, "b2blk", [P, NT, D])
                rs = sb(st3, "rs", [P, NT * NH * 2])
                yv = sb(st3, "yv", [P, NT, D])
                y2 = sb(st3, "y2", [P, NT, D])
                ms = sb(st3, "ms", [P, NT * NH])
                yT = sb(st3, "yT", [P, T])
                maskT = sb(st3, "maskT", [P, P])
                z = sb(st3, "z", [P, NT, D])
                gg = sb(st3, "gg", [P, NT, D])
                stats = sb(st3, "stats3", [P, NT, 6])
                mv = sb(st3, "mv3", [P, NT, 2])
                mw = sb(st3, "mw3", [P, NT, 2])
                rstd = sb(st3, "rstd3", [P, NT])
                rstw = sb(st3, "rstw3", [P, NT])
                neghalf = sb(st3, "neghalf3", [P, P])
                sem = lambda name: st3.enter_context(nc.semaphore(name))
                s_b2, s_dch, s_pch, s_z0 = map(sem, ("b2_loaded", "vector_steps3", "pool_steps3", "b2_cleared"))
                s_ms, s_rms, s_yv, s_yt_ps, s_yt, s_so = map(sem, ("meansq3", "rms3", "y_ready3", "yT_in_psum3", "yT_ready3", "attention_out"))
                s_mt_ps, s_mt, s_b2o, s_zst, s_zr, s_zz, s_gg = map(sem, ("maskT_in_psum", "maskT_ready", "b2_in_psum", "z_stats", "z_rstd", "z_ready", "gate_done"))
                s_xst, s_xr, s_xn, s_xt_ps, s_xt = map(sem, ("x_stats", "x_rstd", "xn_ready3", "xT_in_psum", "xT_ready"))

                with nc.Block() as block:
                    @block.sync
                    def _(sp):
                        sp.wait_ge(s_z0, 1)
                        for t in range(NT):
                            sp.dma_start(b2blk[NE * t:NE * t + NE, t, :], A["b2"]).then_inc(s_b2, 16)

                    @block.gpsimd
                    def _(pool):
                        link = Chain(pool, s_pch)
                        nc.gpsimd.memset(b2blk[:, :, :], 0.0).then_inc(s_z0, 1)
                        link(nc.gpsimd.memset(neghalf[:, :], -0.5))
                        pool.wait_ge(s_ms, 1)
                        link(nc.gpsimd.tensor_scalar(ms[:, :], ms[:, :], 1.0 / 16, 1e-5, ALU.mult, ALU.add))
                        nc.gpsimd.tensor_tensor(ms[:, :], ms[:, :], neghalf[:, :], ALU.pow).then_inc(s_rms, 1)
                        pool.wait_ge(s_zst, 1)
                        link(nc.gpsimd.tensor_scalar(rstd[:, :], mv[:, :, 1], EPS, None, ALU.add))
                        nc.gpsimd.tensor_tensor(rstd[:, :], rstd[:, :], neghalf[:, 0:NT], ALU.pow).then_inc(s_zr, 1)
                        pool.wait_ge(s_xst, 1)
                        link(nc.gpsimd.tensor_scalar(rstw[:, :], mw[:, :, 1], EPS, None, ALU.add))
                        nc.gpsimd.tensor_tensor(rstw[:, :], rstw[:, :], neghalf[:, 0:NT], ALU.pow).then_inc(s_xr, 1)

                    @block.scalar
                    def _(act):
                        act.wait_ge(s_mt_ps, 1)
                        nc.scalar.activation(maskT[:, :], bank[0][:, 0, :], ACT.Copy).then_inc(s_mt, 1)
                        for b in range(B):
                            act.wait_ge(s_yt_ps, b + 1)
                            nc.scalar.activation(yT[:, 512 * b:512 * b + 512], bank[b % 2][:, :, :].rearrange("p t d -> p (t d)"), ACT.Copy).then_inc(s_yt, 1)
                        act.wait_ge(s_zz, 1)
                        nc.scalar.activation(gg[:, :, :], z[:, :, :], ACT.Silu).then_inc(s_gg, 1)
                        for b in range(B):
                            act.wait_ge(s_xt_ps, b + 1)
                            nc.scalar.activation(XT[:, b, :], bank[4 + b][:, :, :].rearrange("p t d -> p (t d)"), ACT.Copy).then_inc(s_xt, 1)

                    @block.tensor
                    def _(pe):
                        nc.tensor.transpose(bank[0][:, 0, :], mask0[:, :, :].rearrange("p t e -> p (t e)"), ident[:, :]).then_inc(s_mt_ps, 1)
                        pe.wait_ge(s_mt, 1)
                        pe.wait_ge(s_b2, 16 * NT)
                        for t in range(NT):
                            last = nc.tensor.matmul(bank[4 + t // 4][:, t % 4, :], maskT[:, :], b2blk[:, t, :], start=True, stop=True)
                        last.then_inc(s_b2o, 1)
                        pe.wait_ge(s_yv, 1)
                        for b in range(B):
                            if b >= 2:
                                pe.wait_ge(s_yt, b - 1)
                            for t in range(4):
                                last = nc.tensor.transpose(bank[b % 2][:, t, :], yv[:, 4 * b + t, :], ident[:, :])
                            last.then_inc(s_yt_ps, 1)
                        pe.wait_ge(s_yt, B)
                        for b in range(B):
                            for t in range(4):
                                last = nc.tensor.matmul(bank[b][:, t, :], yT[:, P * (4 * b + t):P * (4 * b + t) + P], wo_att[:, :], start=True, stop=True)
                        last.then_inc(s_so, 1)
                        pe.wait_ge(s_xn, 1)
                        for b in range(B):
                            for t in range(4):
                                last = nc.tensor.transpose(bank[4 + b][:, t, :], XN[:, 4 * b + t, :], ident[:, :])
                            last.then_inc(s_xt_ps, 1)

                    @block.vector
                    def _(dve):
                        link = Chain(dve, s_dch)
                        yb = ybig[:, :, :].rearrange("p t (h s c) -> p (t h s) c", s=2, c=17)
                        link(nc.vector.reciprocal(rs[:, :].unsqueeze(2), yb[:, :, 16:17]))
                        rv = rs[:, :].rearrange("p (a s) -> p a s", s=2)
                        link(nc.vector.tensor_scalar(rv[:, :, 1], rv[:, :, 1], neg_lam[:, :], None, ALU.mult))
                        link(nc.vector.tensor_scalar(subln[:, :], subln[:, :], 0.5, None, ALU.mult))
                        link(nc.vector.tensor_tensor(yb[:, :, 0:16], yb[:, :, 0:16], rs[:, :].unsqueeze(2).broadcast_to([P, NT * NH * 2, 16]), ALU.mult))
                        y4 = ybig[:, :, :].rearrange("p t (h s c) -> p (t h) s c", s=2, c=17)
                        yf = yv[:, :, :].rearrange("p t (h d) -> p (t h) d", d=16)
                        y2f = y2[:, :, :].rearrange("p t (h d) -> p (t h) d", d=16)
                        link(nc.vector.tensor_tensor(yf, y4[:, :, 0, 0:16], y4[:, :, 1, 0:16], ALU.add))
                        link(nc.vector.tensor_tensor(y2[:, :, :], yv[:, :, :], yv[:, :, :], ALU.mult))
                        nc.vector.tensor_reduce(ms[:, :], y2f, AX.X, ALU.add).then_inc(s_ms, 1)
                        dve.wait_ge(s_b2o, 1)
                        link(nc.vector.tensor_tensor(z[:, :, :], ACC[:, :, :], Y1[:, :, :], ALU.add))
                        for b in range(B):
                            last = nc.vector.tensor_tensor(z[:, 4 * b:4 * b + 4, :], z[:, 4 * b:4 * b + 4, :], bank[4 + b][:, :, :], ALU.add)
                        link(last)
                        for t in range(NT):
                            last = nc.vector.bn_stats(stats[:, t, :], z[:, t, :])
                        link(last)
                        for t in range(NT):
                            last = nc.vector.bn_aggr(mv[:, t, :], stats[:, t, :])
                        last.then_inc(s_zst, 1)
                        dve.wait_ge(s_rms, 1)
                        link(nc.vector.tensor_tensor(yf, yf, ms[:, :].unsqueeze(2).broadcast_to([P, NT * NH, 16]), ALU.mult))
                        nc.vector.tensor_tensor(yf, yf, subln[:, :].unsqueeze(1).broadcast_to([P, NT * NH, 16]), ALU.mult).then_inc(s_yv, 1)
                        dve.wait_ge(s_zr, 1)
                        for t in range(NT):
                            last = nc.vector.tensor_scalar(z[:, t, :], z[:, t, :], mv[:, t, 0:1], rstd[:, t:t + 1], ALU.subtract, ALU.mult)
                        link(last)
                        link(nc.vector.tensor_tensor(z[:, :, :], z[:, :, :], g2_row[:, :].unsqueeze(1).broadcast_to([P, NT, D]), ALU.mult))
                        nc.vector.tensor_tensor(z[:, :, :], z[:, :, :], be2_row[:, :].unsqueeze(1).broadcast_to([P, NT, D]), ALU.add).then_inc(s_zz, 1)
                        dve.wait_ge(s_so, 1)
                        for b in range(B):
                            last = nc.vector.tensor_tensor(y2[:, 4 * b:4 * b + 4, :], bank[b][:, :, :], bo_row[:, :].unsqueeze(1).broadcast_to([P, 4, D]), ALU.add)
                        link(last)
                        dve.wait_ge(s_gg, 1)
                        link(nc.vector.tensor_tensor(y2[:, :, :], y2[:, :, :], gg[:, :, :], ALU.mult))
                        link(nc.vector.tensor_tensor(X[:, :, :], X[:, :, :], y2[:, :, :], ALU.add))
                        for t in range(NT):
                            last = nc.vector.bn_stats(stats[:, t, :], X[:, t, :])
                        link(last)
                        for t in range(NT):
                            last = nc.vector.bn_aggr(mw[:, t, :], stats[:, t, :])
                        last.then_inc(s_xst, 1)
                        dve.wait_ge(s_xr, 1)
                        for t in range(NT):
                            last = nc.vector.tensor_scalar(XN[:, t, :], X[:, t, :], mw[:, t, 0:1], rstw[:, t:t + 1], ALU.subtract, ALU.mult)
                        last.then_inc(s_xn, 1)
        st4 = ExitStack()
        with st4:
            CAP = int(1.25 * T / NE)
            ROWS = NE * CAP
            FAR = 1.0e6
            g_bank = [st4.enter_context(nc.psum_tensor(f"g_bank{i}", [P, 512], fp32)) for i in range(2)]
            u_bank = [st4.enter_context(nc.psum_tensor(f"u_bank{i}", [P, 512], fp32)) for i in range(2)]
            o_bank = st4.enter_context(nc.psum_tensor("o_bank4", [P, 4, D], fp32))
            e_bank = st4.enter_context(nc.psum_tensor("e_bank4", [P, 4, D], fp32))
            x_bank = st4.enter_context(nc.psum_tensor("x_bank4", [P, 512], fp32))
            r_bank = st4.enter_context(nc.psum_tensor("r_bank4", [P, 512], fp32))
            xg_dram = nc.dram_tensor("expert_rows", [ROWS, D], fp32).ap()
            eo_dram = nc.dram_tensor("expert_outs", [ROWS, D], fp32).ap()
            w_r = sb(st4, "w_r", [P, NE])
            w_sg = sb(st4, "w_sg", [P, 1024])
            w_su = sb(st4, "w_su", [P, 1024])
            w_sd = sb(st4, "w_sd", [P, 8, D])
            w_rg = [sb(st4, f"w_rg{i}", [P, 512]) for i in range(2)]
            w_ru = [sb(st4, f"w_ru{i}", [P, 512]) for i in range(2)]
            w_rd = [sb(st4, f"w_rd{i}", [P, 4, D]) for i in range(2)]
            below = sb(st4, "below_sb", [P, P])
            ones = sb(st4, "ones4", [P, P])
            zeros = sb(st4, "zeros4", [P, 20, D])
            neghalf = sb(st4, "neghalf4", [P, NT])
            base_row = sb(st4, "base_row", [P, NT, NE])
            sq = sb(st4, "sq4", [P, NT, D])
            pr = sb(st4, "pr", [P, NT, NE])
            p2 = sb(st4, "p2", [P, NT, NE])
            cand = sb(st4, "cand4", [P, NT, NE])
            oh = [sb(st4, f"oh{i}", [P, NT, NE]) for i in range(2)]
            sel = sb(st4, "sel", [P, NT, NE])
            cum = [sb(st4, f"cum{i}", [P, NT + 1, NE]) for i in range(2)]
            kept = sb(st4, "kept", [P, NT, NE])
            row = sb(st4, "row4", [P, NT, NE])
            cols = sb(st4, "cols4", [P, 12, NT])
            rows_u = [sb(st4, f"rows_u{i}", [P, NT], u32) for i in range(2)]
            hid = sb(st4, "hid4", [P, 2, 8, 512])
            sil = sb(st4, "sil4", [P, 2, 512])
            SH = sb(st4, "SH", [P, NT, D])
            GB = [sb(st4, f"GB{i}", [P, NT, D]) for i in range(2)]
            xg = [sb(st4, f"xg{i}", [P, 3, D]) for i in range(2)]
            xgT = sb(st4, "xgT", [P, 2, CAP])
            eo = sb(st4, "eo", [P, 2, 3, D])

            sem = lambda name: st4.enter_context(nc.semaphore(name))
            s_w4, s_w8 = sem("shared_loaded"), [sem(f"expert_loaded{i}") for i in range(2)]
            s_xg = [sem(f"rows_loaded{i}") for i in range(2)]
            s_lg4, s_sq4, s_ms4, s_rn4, s_x4, s_e4, s_sel, s_rk, s_rows = map(sem, ("logits4", "squares4", "meansq4", "rnorm4", "logits_shifted", "exps4", "selected", "ranks", "rows_known"))
            s_dch, s_pch, s_clr, s_zf, s_scat, s_gath, s_fin, s_gz = map(sem, ("vector_steps4", "pool_steps4", "cleared4", "rows_cleared", "scattered", "gathered", "sum_done", "gather_cleared"))
            s_gu, s_si, s_hd, s_od, s_oc = map(sem, ("gate_up_in_psum", "silu_done", "hidden_done", "shared_out_in_psum", "shared_out_kept"))
            s_tp, s_tc, s_gu8, s_si8, s_hd8, s_ed, s_ec = map(sem, ("rowsT_in_psum", "rowsT_kept", "gate_up_in_psum8", "silu_done8", "hidden_done8", "expert_out_in_psum", "expert_out_kept"))
            s_es = [sem(f"expert_out_stored{i}") for i in range(2)]
            LEAD = 4
            at = lambda i, per, k: i * per + (LEAD + k)

            with nc.Block() as block:
                @block.sync
                def _(sp):
                    for dst, src in ((w_r[:, :], A["w_router"]), (below[:, :], A["below"]), (w_sg[:, :], A["w_sg"]), (w_su[:, :], A["w_su"]), (w_sd[:, :, :], A["w_sd"])):
                        sp.dma_start(dst, src).then_inc(s_w4, 16)
                    sp.wait_ge(s_clr, 1)
                    sp.dma_start(xg_dram.rearrange("(p k) d -> p k d", p=P), zeros[:, :, :]).then_inc(s_zf, 16)

                    def load_weights(e, i):
                        one = lambda x: x[bass.ds(e, 1)]
                        sp.dma_start(w_rg[i][:, :], one(A["w_rg"]).rearrange("o p f -> p (o f)")).then_inc(s_w8[i], 16)
                        sp.dma_start(w_ru[i][:, :], one(A["w_ru"]).rearrange("o p f -> p (o f)")).then_inc(s_w8[i], 16)
                        sp.dma_start(w_rd[i][:, :, :], one(A["w_rd"]).rearrange("o (k p) d -> p (o k) d", p=P)).then_inc(s_w8[i], 16)

                    def load_rows(e, i):
                        for k in range(3):
                            n = min(P, CAP - P * k)
                            sp.dma_start(xg[i][0:n, k, :], xg_dram[bass.ds(e * CAP + P * k, n), :]).then_inc(s_xg[i], 16)

                    for i in range(2):
                        load_weights(i, i)
                    sp.wait_ge(s_scat, 16 * 2 * NT)
                    for i in range(2):
                        load_rows(i, i)
                    def turn(q, more):
                        for i in range(2):
                            sp.wait_ge(s_ec, at(q, 2, i + 1))
                            sp.wait_ge(s_clr, 1)
                            for k in range(3):
                                n = min(P, CAP - P * k)
                                sp.dma_start(eo_dram[bass.ds((q * 2 + i) * CAP + P * k, n), :], eo[0:n, i, k, :]).then_inc(s_es[i], 16)
                            if more:
                                load_weights(q * 2 + (2 + i), i)
                                load_rows(q * 2 + (2 + i), i)

                    with sp.Fori(0, 3) as q:
                        turn(q, True)
                    turn(3, False)

                @block.gpsimd
                def _(pool):
                    link = Chain(pool, s_pch)
                    nc.gpsimd.memset(zeros[:, :, :], 0.0).then_inc(s_clr, 1)
                    link(nc.gpsimd.memset(neghalf[:, :], -0.5))
                    nc.gpsimd.tensor_tensor(sq[:, :, :], XN[:, :, :], XN[:, :, :], ALU.mult).then_inc(s_sq4, 1)
                    for e in range(NE):
                        nc.gpsimd.memset(base_row[:, :, e:e + 1], float(CAP * e)).then_inc(s_clr, 1)
                    nc.gpsimd.memset(ones[:, :], 1.0).then_inc(s_clr, 1)
                    pool.wait_ge(s_ms4, 1)
                    link(nc.gpsimd.tensor_scalar(cols[:, 0, :], cols[:, 0, :], 1.0 / D, 1.1920929e-07, ALU.mult, ALU.add))
                    nc.gpsimd.tensor_tensor(cols[:, 0, :], cols[:, 0, :], neghalf[:, :], ALU.pow).then_inc(s_rn4, 1)
                    for i in range(2):
                        nc.gpsimd.memset(GB[i][:, :, :], 0.0).then_inc(s_gz, 1)
                    pool.wait_ge(s_rows, 1)
                    pool.wait_ge(s_zf, 16)
                    for t in range(NT):
                        for i in range(2):
                            nc.gpsimd.indirect_dma_start(xg_dram[:, :], bass.IndirectOffsetOnAxis(ap=rows_u[i][:, t:t + 1], axis=0), XN[:, t, :], None,
                                                         bounds_check=ROWS - 1, oob_is_err=False).then_inc(s_scat, 16)
                    pool.wait_ge(s_gz, 2)
                    for i in range(2):
                        pool.wait_ge(s_es[i], 16 + 4 * 48)
                    for t in range(NT):
                        for i in range(2):
                            nc.gpsimd.indirect_dma_start(GB[i][:, t, :], None, eo_dram[:, :], bass.IndirectOffsetOnAxis(ap=rows_u[i][:, t:t + 1], axis=0),
                                                         bounds_check=ROWS - 1, oob_is_err=False).then_inc(s_gath, 16)

                @block.tensor
                def _(pe):
                    for s in (s_gu, s_od, s_tp, s_gu8, s_ed):
                        pe.sem_inc(s, LEAD)
                    mm = nc.tensor.matmul
                    pe.wait_ge(s_w4, 16 * 5)
                    for t in range(NT):
                        last = mm(r_bank[:, NE * t:NE * t + NE], XT[:, t // 4, P * (t % 4):P * (t % 4) + P], w_r[:, :], start=True, stop=True)
                    last.then_inc(s_lg4, 1)

                    def shared(c):
                        for f in range(8):
                            pe.wait_ge(s_hd, at(c, 8, f - 1))
                            mm(g_bank[f % 2][:, :], w_sg[:, P * f:P * f + P], XT[:, bass.ds(c, 1), :], start=True, stop=True)
                            mm(u_bank[f % 2][:, :], w_su[:, P * f:P * f + P], XT[:, bass.ds(c, 1), :], start=True, stop=True).then_inc(s_gu, 1)

                    def shared_down(c):
                        pe.wait_ge(s_hd, at(c, 8, 8))
                        pe.wait_ge(s_oc, at(c, 1, 0))
                        for t in range(4):
                            for f in range(8):
                                last = mm(o_bank[:, t, :], hid[:, 0, f, P * t:P * t + P], w_sd[:, f, :], start=(f == 0), stop=(f == 7))
                        last.then_inc(s_od, 1)

                    with pe.Fori(0, 4) as c:
                        shared(c)
                        shared_down(c)
                    pe.wait_ge(s_clr, 10)
                    pe.wait_ge(s_sel, 1)
                    mm(x_bank[:, 0:P], below[:, :], sel[:, :, :].rearrange("p t e -> p (t e)"), start=True, stop=False)
                    mm(x_bank[:, 0:P], ones[:, :], cum[0][:, 0:NT, :].rearrange("p t e -> p (t e)"), start=False, stop=True).then_inc(s_rk, 1)
                    pe.wait_ge(s_rows, 1)
                    with pe.Fori(0, 4) as q:
                        for i in range(2):
                            n = lambda per, k: at(q, 2 * per, i * per + k)
                            pe.wait_ge(s_xg[i], q * 48 + 48)
                            pe.wait_ge(s_tc, n(1, 0))
                            for k in range(3):
                                r = min(P, CAP - P * k)
                                last = nc.tensor.transpose(x_bank[:, P * k:P * k + r], xg[i][0:r, k, :], ident[0:r, 0:r])
                            last.then_inc(s_tp, 1)
                            pe.wait_ge(s_tc, n(1, 1))
                            pe.wait_ge(s_w8[i], q * 48 + 48)
                            for f in range(4):
                                pe.wait_ge(s_hd8, n(4, f - 1))
                                mm(g_bank[f % 2][:, 0:CAP], w_rg[i][:, P * f:P * f + P], xgT[:, i, :], start=True, stop=True)
                                mm(u_bank[f % 2][:, 0:CAP], w_ru[i][:, P * f:P * f + P], xgT[:, i, :], start=True, stop=True).then_inc(s_gu8, 1)
                            pe.wait_ge(s_hd8, n(4, 4))
                            pe.wait_ge(s_ec, n(1, 0))
                            for k in range(3):
                                r = min(P, CAP - P * k)
                                for f in range(4):
                                    last = mm(e_bank[0:r, k, :], hid[:, i, f, P * k:P * k + r], w_rd[i][:, f, :], start=(f == 0), stop=(f == 3))
                            last.then_inc(s_ed, 1)

                @block.scalar
                def _(act):
                    for s in (s_si, s_oc, s_tc, s_si8, s_ec):
                        act.sem_inc(s, LEAD)
                    for s in s_es:
                        act.sem_inc(s, 16)
                    act.wait_ge(s_x4, 1)
                    nc.scalar.activation(pr[:, :, :], pr[:, :, :], ACT.Exp).then_inc(s_e4, 1)
                    act.preload_act_table(ACT.Silu)
                    with act.Fori(0, 4) as c:
                        for f in range(8):
                            act.wait_ge(s_gu, at(c, 8, f + 1))
                            act.wait_ge(s_hd, at(c, 8, f - 1))
                            nc.scalar.activation(sil[:, f % 2, :], g_bank[f % 2][:, :], ACT.Silu).then_inc(s_si, 1)
                        act.wait_ge(s_od, at(c, 1, 1))
                        nc.scalar.activation(SH[:, bass.ds(c * 4, 4), :], o_bank[:, :, :], ACT.Copy).then_inc(s_oc, 1)
                    with act.Fori(0, 4) as q:
                        for i in range(2):
                            n = lambda per, k: at(q, 2 * per, i * per + k)
                            act.wait_ge(s_tp, n(1, 1))
                            act.wait_ge(s_ed, n(1, -1))
                            nc.scalar.activation(xgT[:, i, :], x_bank[:, 0:CAP], ACT.Copy).then_inc(s_tc, 1)
                            for f in range(4):
                                act.wait_ge(s_gu8, n(4, f + 1))
                                act.wait_ge(s_hd8, n(4, f - 1))
                                nc.scalar.activation(sil[:, f % 2, 0:CAP], g_bank[f % 2][:, 0:CAP], ACT.Silu).then_inc(s_si8, 1)
                            act.wait_ge(s_ed, n(1, 1))
                            act.wait_ge(s_es[i], q * 48 + 16)
                            nc.scalar.activation(eo[:, i, 0:2, :], e_bank[:, 0:2, :], ACT.Copy)
                            nc.scalar.activation(eo[0:CAP - 2 * P, i, 2, :], e_bank[0:CAP - 2 * P, 2, :], ACT.Copy).then_inc(s_ec, 1)
                    act.wait_ge(s_fin, 1)
                    nc.scalar.activation(GATE[:, :, :], SH[:, :, :], ACT.Silu).then_inc(s_fin, 1)

                @block.vector
                def _(dve):
                    link = Chain(dve, s_dch)
                    for s in (s_hd, s_hd8):
                        dve.sem_inc(s, LEAD)
                    TT = nc.vector.tensor_tensor
                    wide = lambda col: col.unsqueeze(2).broadcast_to([P, NT, NE])
                    dve.wait_ge(s_sq4, 1)
                    nc.vector.tensor_reduce(cols[:, 0, :], sq[:, :, :], AX.X, ALU.add).then_inc(s_ms4, 1)
                    dve.wait_ge(s_rn4, 1)
                    dve.wait_ge(s_lg4, 1)
                    link(TT(pr[:, :, :], r_bank[:, 0:NT * NE].rearrange("p (t e) -> p t e", e=NE), wide(cols[:, 0, :]), ALU.mult))
                    link(nc.vector.tensor_reduce(cols[:, 1, :], pr[:, :, :], AX.X, ALU.max))
                    TT(pr[:, :, :], pr[:, :, :], wide(cols[:, 1, :]), ALU.subtract).then_inc(s_x4, 1)
                    dve.wait_ge(s_e4, 1)
                    link(nc.vector.tensor_reduce(cols[:, 2, :], pr[:, :, :], AX.X, ALU.add))
                    link(nc.vector.reciprocal(cols[:, 2, :], cols[:, 2, :]))
                    link(TT(pr[:, :, :], pr[:, :, :], wide(cols[:, 2, :]), ALU.mult))
                    for i, src in enumerate((pr, p2)):
                        link(nc.vector.tensor_reduce(cols[:, 3 + i, :], src[:, :, :], AX.X, ALU.max))
                        link(TT(cand[:, :, :], src[:, :, :], wide(cols[:, 3 + i, :]), ALU.is_ge))
                        link(TT(cand[:, :, :], cand[:, :, :], rank_desc[:, :, :], ALU.mult))
                        link(nc.vector.tensor_reduce(cols[:, 5, :], cand[:, :, :], AX.X, ALU.max))
                        link(TT(oh[i][:, :, :], cand[:, :, :], wide(cols[:, 5, :]), ALU.is_equal))
                        if i == 0:
                            link(nc.vector.scalar_tensor_tensor(p2[:, :, :], oh[0][:, :, :], -2.0, pr[:, :, :], ALU.mult, ALU.add))
                    link(TT(cols[:, 6, :], cols[:, 3, :], cols[:, 4, :], ALU.add))
                    link(nc.vector.reciprocal(cols[:, 6, :], cols[:, 6, :]))
                    link(TT(cols[:, 3:5, :], cols[:, 3:5, :], cols[:, 6, :].unsqueeze(1).broadcast_to([P, 2, NT]), ALU.mult))
                    link(TT(sel[:, :, :], oh[0][:, :, :], oh[1][:, :, :], ALU.add))
                    for c in range(2):
                        link(nc.vector.memset(cum[c][:, :, :], 0.0))
                    link(nc.vector.tensor_copy(cum[0][:, 1:NT + 1, :], sel[:, :, :]))
                    for n, step4 in enumerate((1, 2, 4, 8)):
                        a, z = cum[n % 2], cum[(n + 1) % 2]
                        link(nc.vector.tensor_copy(z[:, 0:step4, :], a[:, 0:step4, :]))
                        link(TT(z[:, step4:NT + 1, :], a[:, step4:NT + 1, :], a[:, 0:NT + 1 - step4, :], ALU.add), s_sel if n == 3 else None)

                    def shared(c):
                        for f in range(8):
                            dve.wait_ge(s_si, at(c, 8, f + 1))
                            if f == 0:
                                dve.wait_ge(s_od, at(c, 1, 0))
                            TT(hid[:, 0, f, :], sil[:, f % 2, :], u_bank[f % 2][:, :], ALU.mult).then_inc(s_hd, 1)

                    with dve.Fori(0, 4) as c:
                        shared(c)
                    dve.wait_ge(s_rk, 1)
                    dve.wait_ge(s_clr, 10)
                    rk = x_bank[:, 0:P].rearrange("p (t e) -> p t e", e=NE)
                    link(nc.vector.tensor_scalar(kept[:, :, :], rk, float(CAP), None, ALU.is_lt))
                    link(TT(row[:, :, :], rk, base_row[:, :, :], ALU.add))
                    link(nc.vector.tensor_scalar(cand[:, :, :], kept[:, :, :], -FAR, FAR, ALU.mult, ALU.add))
                    link(TT(row[:, :, :], row[:, :, :], cand[:, :, :], ALU.add))
                    for i in range(2):
                        link(TT(cand[:, :, :], oh[i][:, :, :], row[:, :, :], ALU.mult))
                        link(nc.vector.tensor_reduce(cols[:, 7, :], cand[:, :, :], AX.X, ALU.add))
                        link(nc.vector.tensor_copy(rows_u[i][:, :], cols[:, 7, :]))
                        link(TT(cand[:, :, :], oh[i][:, :, :], kept[:, :, :], ALU.mult))
                        link(nc.vector.tensor_reduce(cols[:, 8 + i, :], cand[:, :, :], AX.X, ALU.add))
                    link(TT(cols[:, 3:5, :], cols[:, 3:5, :], cols[:, 8:10, :], ALU.mult), s_rows)
                    with dve.Fori(0, 4) as q:
                        for i in range(2):
                            n = lambda per, k: at(q, 2 * per, i * per + k)
                            for f in range(4):
                                dve.wait_ge(s_si8, n(4, f + 1))
                                if f == 0:
                                    dve.wait_ge(s_ed, n(1, -1))
                                TT(hid[:, i, f, 0:CAP], sil[:, f % 2, 0:CAP], u_bank[f % 2][:, 0:CAP], ALU.mult).then_inc(s_hd8, 1)
                    dve.wait_ge(s_gath, 16 * 2 * NT)
                    dve.wait_ge(s_oc, at(4, 1, 0))
                    full = lambda col: col.unsqueeze(2).broadcast_to([P, NT, D])
                    for i in range(2):
                        link(TT(GB[i][:, :, :], GB[i][:, :, :], full(cols[:, 3 + i, :]), ALU.mult))
                        last = TT(SH[:, :, :], SH[:, :, :], GB[i][:, :, :], ALU.add)
                        if i == 0:
                            link(last)
                    last.then_inc(s_fin, 1)
        keepx.close()
        st5 = ExitStack()
        with st5:
            NB, GR, KS, UN = B, 8, 4, 32
            slot_bank = [st5.enter_context(nc.psum_tensor(f"slot_bank{i}", [P, 512], fp32)) for i in range(4)]
            du_bank = [st5.enter_context(nc.psum_tensor(f"du_bank{i}", [P, 512], fp32)) for i in range(2)]
            dec_bank = [st5.enter_context(nc.psum_tensor(f"decay_bank{i}", [P, 512], fp32)) for i in range(2)]
            w_in = sb(st5, "w_in", [P, 512])
            w_xp = sb(st5, "w_xp", [P, 2, 40])
            w_dt = sb(st5, "w_dt", [40, 256])
            pre_cols = sb(st5, "pre_cols", [P, 12])
            w_out = sb(st5, "w_out", [P, 2, D])
            d_col = sb(st5, "d_col", [P, 2])
            a_all = sb(st5, "a_all", [P, 4, UN])
            a_cur = sb(st5, "a_cur", [P, UN])
            spread = sb(st5, "spread_sb", [P, 4, P])
            pick = sb(st5, "pick_sb", [40, 8, P])
            fold = sb(st5, "fold_sb", [P, 32])
            bc = sb(st5, "bc", [P, 2, 8, 512])
            dtr = sb(st5, "dtr", [P, 2, GR, 512])
            xc = sb(st5, "xc", [P, 2, 2, 512])
            zs = sb(st5, "zs", [P, 2, 2, 512])
            du = sb(st5, "du", [P, 2, 2, 512])
            dt = sb(st5, "dt", [P, 2, 512])
            cacc = sb(st5, "cacc", [P, 2, 512])
            spa = sb(st5, "spa", [P, 2, 512])
            spr = sb(st5, "spr", [P, 2, 512])
            dbc = sb(st5, "dbc", [40, 512])
            dbx = sb(st5, "dbx", [P, 2, 512])
            hs = sb(st5, "hs", [P, 4, 512])
            hc = sb(st5, "hc", [P, 16, 512])
            yv = sb(st5, "yv5", [P, 2, 512])

            sem = lambda name: st5.enter_context(nc.semaphore(name))
            s_cst, s_wpre, s_wpost, s_zero, s_neg = map(sem, ("consts5", "pre_weights", "post_weights", "w_dt_cleared", "a_steps"))
            s_slot, s_fA, s_fV = map(sem, ("slot_written", "slot_left_by_scalar", "slot_left_by_vector"))
            s_du, s_dec, s_bx, s_sc, s_hc, s_yr = map(sem, ("du_spread", "decay_ready", "dbx_ready", "scan_done", "hc_ready", "round_summed"))
            s_ci, s_cs, s_xc, s_ln, s_dt, s_dun, s_yd, s_yv, s_ac = map(sem, ("conv_begun", "conv_steps", "xc_ready", "softplus_log", "dt_ready", "du_ready", "y_with_d", "yv_ready", "a_of_layer"))
            s_dtr = [sem(f"dt_spread{i}") for i in range(2)]
            s_spx = sem("softplus_exp")

            LEAD = 32
            SCALAR, VECTOR = s_fA, s_fV
            PRE = [("xi0", VECTOR), ("xi1", VECTOR), ("z0", SCALAR), ("z1", SCALAR), ("xp", SCALAR), ("dt0", SCALAR), ("dt1", SCALAR)] + \
                  [(f"bc{i}", SCALAR) for i in range(8)]
            order = []
            for b in range(NB):
                if b:
                    order.append(("y1", b - 1, VECTOR))
                order += [("xi0", b, VECTOR), ("xi1", b, VECTOR)]
                if b:
                    order.append(("out", b - 1, SCALAR))
                order += [("z0", b, SCALAR), ("z1", b, SCALAR), ("xp", b, SCALAR), ("y0", b, VECTOR), ("dt0", b, SCALAR), ("dt1", b, SCALAR)]
                order += [(f"bc{i}", b, SCALAR) for i in range(8)]
            order += [("y1", NB - 1, VECTOR), ("out", NB - 1, SCALAR)]
            place = {(name, b): n for n, (name, b, _) in enumerate(order)}
            left = lambda n, who: sum(1 for x in order[:n] if x[2] is who)
            per = {who: left(len(order), who) for who in (SCALAR, VECTOR)}
            assert len(order) % 4 == 0
            pre_left = {who: sum(1 for x in PRE if x[1] is who) + 1 for who in (SCALAR, VECTOR)}
            written_before = lambda n: sum(1 for x in order[:n] if x[0][0] != "y")

            class Slot:

                def __init__(self, name, b, l):
                    self.l = l
                    if l is None:
                        self.n = [x[0] for x in PRE].index(name)
                        self.who = PRE[self.n][1]
                    else:
                        self.n = place[name, b]
                        self.who = order[self.n][2]
                    self.bank = slot_bank[self.n % 4]

                def written(self):
                    if self.l is None:
                        return LEAD + self.n + 1
                    return self.l * written_before(len(order)) + (LEAD + len(PRE) + written_before(self.n + 1))

                def free(self, pe):
                    if self.l is None:
                        if self.n >= 4:
                            who = PRE[self.n - 4][1]
                            pe.wait_ge(who, LEAD + sum(1 for x in PRE[:self.n - 3] if x[1] is who))
                        return
                    m = self.n - 4
                    who = order[m][2]
                    count = left(m + 1, who) if m >= 0 else left(len(order) + m + 1, who) - per[who]
                    pe.wait_ge(who, self.l * per[who] + (LEAD + pre_left[who] + count))

                def left_at(self):
                    if self.l is None:
                        return LEAD + sum(1 for x in PRE[:self.n + 1] if x[1] is self.who)
                    return self.l * per[self.who] + (LEAD + pre_left[self.who] + left(self.n + 1, self.who))

            at = lambda l, b, per_turn, k: (0 if l is None else l) * (4 * per_turn) + (LEAD + per_turn * b + k)

            with nc.Block() as block:
                last_bc = lambda l: l * per[SCALAR] + (LEAD + pre_left[SCALAR] + (left(place["bc7", NB - 1] + 1, SCALAR) - per[SCALAR]))
                consts = [(spread[:, :, :], A["spread"]), (pick[:, :, :], A["pick"]), (fold[:, :], A["fold"]), (a_all[:, :, :], A["a_log"])]

                @block.sync
                def _(sp):
                    for dst, src in consts:
                        sp.dma_start(dst, src).then_inc(s_cst, 16)

                    def load_pre(l):
                        one = lambda x: x[bass.ds(l, 1)]
                        sp.dma_start(w_in[:, :], one(A["w_in"]).rearrange("o p e -> p (o e)")).then_inc(s_wpre, 16)
                        sp.dma_start(w_xp[:, :, :], one(A["w_xp"]).rearrange("o p k e -> p (o k) e")).then_inc(s_wpre, 16)
                        sp.dma_start(w_dt[0:8, :], one(A["w_dt"]).rearrange("o p e -> p (o e)")).then_inc(s_wpre, 16)
                        sp.dma_start(pre_cols[:, :], one(A["pre_cols"]).rearrange("o p e -> p (o e)")).then_inc(s_wpre, 16)

                    def load_post(l):
                        one = lambda x: x[bass.ds(l, 1)]
                        sp.dma_start(w_out[:, :, :], one(A["w_out"]).rearrange("o p k e -> p (o k) e")).then_inc(s_wpost, 16)
                        sp.dma_start(d_col[:, :], one(A["d_col"]).rearrange("o p e -> p (o e)")).then_inc(s_wpost, 16)

                    def spread_dt(l, b, n):
                        sp.wait_ge(s_dt, at(l, n, 1, 1))
                        for s in range(4):
                            for j in range(4):
                                sp.dma_start(dtr[32 * s:32 * s + 32, n % 2, j:GR:4, :], dt[32 * j:32 * j + 32, :, :]).then_inc(s_dtr[n % 2], 16)

                    sp.wait_ge(s_zero, 1)
                    load_pre(0)
                    spread_dt(0, None, 0)
                    with sp.Fori(0, 4) as l:
                        for b in range(NB):
                            if b == 0:
                                sp.wait_ge(SCALAR, l * per[SCALAR] + (LEAD + pre_left[SCALAR]))
                                sp.wait_ge(s_zero, 1)
                                load_post(l)
                            if b == 3:
                                sp.wait_ge(s_dt, at(l, 3, 1, 1))
                                sp.wait_ge(s_zero, 1)
                                load_pre(l + 1)
                            spread_dt(l, b, b + 1)

                @block.gpsimd
                def _(pool):
                    nc.gpsimd.memset(w_dt[:, :], 0.0).then_inc(s_zero, 1)
                    pool.sem_inc(s_hc, LEAD)
                    with pool.Fori(0, 4) as l:
                        for b in range(NB):
                            for u in range(UN):
                                k = u % 4
                                pool.wait_ge(s_sc, at(l, b, UN, u + 1))
                                if u % 16 < 4:
                                    pool.wait_ge(s_yr, at(l, b, 8, 4 * (u // 16) - 3 + k))
                                if u == 0:
                                    pool.wait_ge(SCALAR, Slot("bc7", b - 1, l).left_at() if b else last_bc(l))
                                nc.gpsimd.tensor_tensor(hc[:, u % 16, :], hs[:, u % 4, :], bc[:, b % 2, 4 + k, :], ALU.mult).then_inc(s_hc, 1)

                @block.tensor
                def _(pe):
                    for s in (s_slot, s_du, s_yr):
                        pe.sem_inc(s, LEAD)
                    pe.wait_ge(s_cst, 16 * len(consts))
                    mm = nc.tensor.matmul

                    def in_proj(l, b, n, names):
                        for name in names:
                            sl = Slot(name, b, l)
                            sl.free(pe)
                            col = {"xi0": 0, "xi1": 1, "z0": 2, "z1": 3}[name]
                            if name == "xi0":
                                if l is not None:
                                    pe.wait_ge(SCALAR, Slot("out", n % 4, l).left_at() if n == 4 else
                                               l * per[SCALAR] + (LEAD + pre_left[SCALAR] + left(place["out", n] + 1, SCALAR) - per[SCALAR]))
                                pe.wait_ge(s_wpre, 64 if l is None else l * 64 + 64 * (1 + n // 4))
                            mm(sl.bank[:, :], w_in[:, P * col:P * col + P], XT[:, n % 4, :], start=True, stop=True).then_inc(s_slot, 1)

                    def x_proj(l, b, n):
                        sl = Slot("xp", b, l)
                        sl.free(pe)
                        pe.wait_ge(s_xc, at(l, n, 2, 2))
                        for h in range(2):
                            last = mm(sl.bank[0:40, :], w_xp[:, h, :], xc[:, n % 2, h, :], start=(h == 0), stop=(h == 1))
                        last.then_inc(s_slot, 1)

                    def dt_proj(l, b):
                        pe.wait_ge(SCALAR, Slot("xp", b, l).left_at())
                        for h in range(2):
                            sl = Slot(f"dt{h}", b, l)
                            sl.free(pe)
                            mm(sl.bank[:, :], w_dt[:, P * h:P * h + P], dbc[:, :], start=True, stop=True).then_inc(s_slot, 1)

                    def pick_bc(l, b, which):
                        for i in which:
                            sl = Slot(f"bc{i}", b, l)
                            sl.free(pe)
                            mm(sl.bank[:, :], pick[:, i, :], dbc[:, :], start=True, stop=True).then_inc(s_slot, 1)

                    def spread_du(l, b, g, n):
                        if g == 0:
                            pe.wait_ge(s_dun, at(l, n, 1, 1))
                        pe.wait_ge(s_bx, at(l, n, UN, 4 * g - 4))
                        mm(du_bank[g % 2][:, :], spread[:, g % 4, :], du[:, n % 2, g // 4, :], start=True, stop=True).then_inc(s_du, 1)

                    def sum_states(l, b, half, in_turn):
                        sl = Slot(f"y{half}", b, l)
                        sl.free(pe)
                        for k in range(KS):
                            pe.wait_ge(s_hc, at(l, b, UN, 16 * half + 13 + k))
                            for j in range(4):
                                last = mm(sl.bank[32 * j:32 * j + 32, :], fold[:, :], hc[:, 4 * j + k, :], start=(k == 0), stop=(k == KS - 1),
                                          tile_position=(0, 32 * j), skip_group_check=True)
                            last.then_inc(s_yr, 1)

                    def out_proj(l, b):
                        sl = Slot("out", b, l)
                        sl.free(pe)
                        pe.wait_ge(s_yv, at(l, b, 2, 2))
                        pe.wait_ge(s_wpost, l * 32 + 32)
                        for h in range(2):
                            last = mm(sl.bank[:, :], w_out[:, h, :], yv[:, h, :], start=(h == 0), stop=(h == 1))
                        last.then_inc(s_slot, 1)

                    in_proj(None, None, 0, ("xi0", "xi1", "z0", "z1"))
                    x_proj(None, None, 0)
                    dt_proj(None, None)
                    pick_bc(None, None, range(8))
                    pe.wait_ge(SCALAR, LEAD + pre_left[SCALAR])
                    pe.wait_ge(VECTOR, LEAD + pre_left[VECTOR])
                    spread_du(0, None, 0, 0)
                    spread_du(0, None, 1, 0)
                    with pe.Fori(0, 4) as l:
                        for b in range(NB):
                            if b:
                                sum_states(l, b - 1, 1, b)
                            spread_du(l, b, 2, b)
                            in_proj(l, b, b + 1, ("xi0", "xi1"))
                            if b:
                                out_proj(l, b - 1)
                            in_proj(l, b, b + 1, ("z0", "z1"))
                            spread_du(l, b, 3, b)
                            spread_du(l, b, 4, b)
                            x_proj(l, b, b + 1)
                            sum_states(l, b, 0, b)
                            dt_proj(l, b)
                            spread_du(l, b, 5, b)
                            pick_bc(l, b, range(0, 4))
                            spread_du(l, b, 6, b)
                            pick_bc(l, b, range(4, 6))
                            spread_du(l, b, 7, b)
                            pick_bc(l, b, range(6, 8))
                            spread_du(l, b, 0, b + 1)
                            spread_du(l, b, 1, b + 1)
                        sum_states(l, NB - 1, 1, NB)
                        out_proj(l, NB - 1)

                @block.scalar
                def _(act):
                    for s in (s_fA, s_dec, s_ci, s_xc, s_ln, s_spx):
                        act.sem_inc(s, LEAD)
                    act.wait_ge(s_cst, 16 * len(consts))
                    act.preload_act_table_set("natural_log_exp_and_others")
                    flat = a_all[:, :, :].rearrange("p l u -> p (l u)")
                    nc.scalar.activation(flat, flat, ACT.Exp).then_inc(s_neg, 1)
                    act.wait_ge(s_neg, 1)
                    nc.scalar.activation(flat, flat, ACT.Copy, scale=-1.0).then_inc(s_neg, 1)
                    act.wait_ge(s_neg, 2)

                    def conv_begin(l, b, n):
                        act.wait_ge(s_wpre, 64 if l is None else l * 64 + 64 * (1 + n // 4))
                        act.wait_ge(s_xc, at(l, n, 2, 0))
                        for h in range(2):
                            sl = Slot(f"xi{h}", b, l)
                            act.wait_ge(s_slot, sl.written())
                            nc.scalar.activation(cacc[:, h, :], sl.bank[:, :], ACT.Identity, scale=pre_cols[:, 4 * h + 3:4 * h + 4],
                                                 bias=pre_cols[:, 8 + h:9 + h]).then_inc(s_ci, 1)

                    def silus(l, b, n):
                        if l is not None:
                            act.wait_ge(s_yv, at(l, b, 2, 0))
                        for h in range(2):
                            act.wait_ge(s_cs, at(l, n, 6, 3 * h + 3))
                            nc.scalar.activation(xc[:, n % 2, h, :], cacc[:, h, :], ACT.Silu).then_inc(s_xc, 1)
                        for h in range(2):
                            sl = Slot(f"z{h}", b, l)
                            act.wait_ge(s_slot, sl.written())
                            nc.scalar.activation(zs[:, n % 2, h, :], sl.bank[:, :], ACT.Silu).then_inc(SCALAR, 1)

                    def copy_dbc(l, b):
                        sl = Slot("xp", b, l)
                        act.wait_ge(s_slot, sl.written())
                        nc.scalar.activation(dbc[:, :], sl.bank[0:40, :], ACT.Copy).then_inc(SCALAR, 1)

                    def softplus(l, b, n):
                        act.wait_ge(s_dt, at(l, n, 1, 0))
                        for h in range(2):
                            sl = Slot(f"dt{h}", b, l)
                            act.wait_ge(s_slot, sl.written())
                            bias = pre_cols[:, 10 + h:11 + h]
                            nc.scalar.activation(spa[:, h, :], sl.bank[:, :], ACT.Abs, bias=bias).then_inc(s_spx, 1)
                            nc.scalar.activation(spr[:, h, :], sl.bank[:, :], ACT.Relu, bias=bias).then_inc(SCALAR, 1)
                        act.wait_ge(s_spx, at(l, n, 3, 2))
                        nc.scalar.activation(spa[:, :, :], spa[:, :, :], ACT.Exp, scale=-1.0).then_inc(s_spx, 1)
                        act.wait_ge(s_spx, at(l, n, 3, 3))
                        nc.scalar.activation(spa[:, :, :], spa[:, :, :], ACT.Ln, bias=1.0).then_inc(s_ln, 1)

                    def copy_bc(l, b, n, i):
                        sl = Slot(f"bc{i}", b, l)
                        act.wait_ge(s_slot, sl.written())
                        nc.scalar.activation(bc[:, n % 2, i, :], sl.bank[:, :], ACT.Copy).then_inc(SCALAR, 1)

                    def copy_out(l, b):
                        sl = Slot("out", b, l)
                        act.wait_ge(s_slot, sl.written())
                        nc.scalar.activation(XT[:, b, :], sl.bank[:, :], ACT.Copy).then_inc(SCALAR, 1)

                    conv_begin(None, None, 0)
                    silus(None, None, 0)
                    copy_dbc(None, None)
                    softplus(None, None, 0)
                    for i in range(8):
                        copy_bc(None, None, 0, i)
                    act.wait_ge(SCALAR, LEAD + pre_left[SCALAR] - 1)
                    act.sem_inc(SCALAR, 1)
                    act.preload_act_table_set("natural_log_exp_and_others")
                    with act.Fori(0, 4) as l:
                        act.wait_ge(s_dec, at(l, 0, UN, 0))
                        act.wait_ge(s_cst, 16 * len(consts))
                        nc.scalar.activation(a_cur[:, :], a_all[:, bass.ds(l, 1), :].rearrange("p l u -> p (l u)"), ACT.Copy).then_inc(s_ac, 1)
                        act.wait_ge(s_ac, l + 1)
                        for b in range(NB):
                            for u in range(UN):
                                if u == 0:
                                    act.wait_ge(s_dtr[b % 2], l * 512 + 256 * (1 + b // 2))
                                act.wait_ge(s_sc, at(l, b, UN, u - 1))
                                nc.scalar.activation(dec_bank[u % 2][:, :], dtr[:, b % 2, u // 4, :], ACT.Exp, scale=a_cur[:, u:u + 1]).then_inc(s_dec, 1)
                                if u == 5:
                                    conv_begin(l, b, b + 1)
                                if u == 7 and b:
                                    copy_out(l, b - 1)
                                if u == 11:
                                    silus(l, b, b + 1)
                                if u == 15:
                                    copy_dbc(l, b)
                                if u == 20:
                                    softplus(l, b, b + 1)
                                if 22 <= u < 30:
                                    copy_bc(l, b, b + 1, u - 22)
                        copy_out(l, NB - 1)

                @block.vector
                def _(dve):
                    for s in (s_fV, s_bx, s_sc, s_cs, s_dt, s_dun, s_yd, s_yv):
                        dve.sem_inc(s, LEAD)

                    def conv(l, b, n):
                        for h in range(2):
                            sl = Slot(f"xi{h}", b, l)
                            dve.wait_ge(s_ci, at(l, n, 2, h + 1))
                            dve.wait_ge(s_wpre, 64 if l is None else l * 64 + 64 * (1 + n // 4))
                            for i, tap in enumerate((2, 1, 0)):
                                d = 3 - tap
                                if i:
                                    dve.wait_ge(s_cs, at(l, n, 6, 3 * h + i))
                                op = nc.vector.scalar_tensor_tensor(cacc[:, h, d:512], sl.bank[:, 0:512 - d], pre_cols[:, 4 * h + tap:4 * h + tap + 1],
                                                                    cacc[:, h, d:512], ALU.mult, ALU.add)
                                op.then_inc(s_cs, 1)
                            dve.wait_ge(s_cs, at(l, n, 6, 3 * h + 3))
                            dve.sem_inc(VECTOR, 1)

                    def make_dt(l, b, n):
                        dve.wait_ge(s_ln, at(l, n, 1, 1))
                        dve.wait_ge(SCALAR, Slot("dt1", b, l).left_at())
                        if l is None:
                            pass
                        else:
                            dve.wait_ge(s_dtr[(n + 1) % 2], l * 512 + 256 * (1 + (n - 1) // 2))
                        nc.vector.tensor_tensor(dt[:, :, :], spa[:, :, :], spr[:, :, :], ALU.add).then_inc(s_dt, 1)
                        dve.wait_ge(s_dt, at(l, n, 1, 1))
                        dve.wait_ge(s_xc, at(l, n, 2, 2))
                        nc.vector.tensor_tensor(du[:, n % 2, :, :], dt[:, :, :], xc[:, n % 2, :, :], ALU.mult).then_inc(s_dun, 1)

                    def gate_y(l, b, half):
                        sl = Slot(f"y{half}", b, l)
                        dve.wait_ge(s_yr, at(l, b, 8, 4 * half + 4))
                        dve.wait_ge(s_wpost, l * 32 + 32)
                        dve.wait_ge(s_yd, at(l, b, 2, half))
                        if half == 0:
                            dve.wait_ge(SCALAR, Slot("out", b - 1, l).left_at() if b else l * per[SCALAR] + (LEAD + pre_left[SCALAR]))
                        nc.vector.scalar_tensor_tensor(yv[:, half, :], xc[:, b % 2, half, :], d_col[:, half:half + 1], sl.bank[:, :],
                                                       ALU.mult, ALU.add).then_inc(s_yd, 1)
                        dve.wait_ge(s_yd, at(l, b, 2, half + 1))
                        dve.sem_inc(VECTOR, 1)
                        nc.vector.tensor_tensor(yv[:, half, :], yv[:, half, :], zs[:, b % 2, half, :], ALU.mult).then_inc(s_yv, 1)

                    conv(None, None, 0)
                    make_dt(None, None, 0)
                    dve.sem_inc(VECTOR, 1)
                    with dve.Fori(0, 4) as l:
                        for b in range(NB):
                            for u in range(UN):
                                g, k = u // 4, u % 4
                                if k == 0:
                                    dve.wait_ge(s_du, at(l, b, 8, g + 1))
                                if u == 0:
                                    dve.wait_ge(SCALAR, Slot("bc7", b - 1, l).left_at() if b else last_bc(l))
                                dve.wait_ge(s_sc, at(l, b, UN, u - 1))
                                nc.vector.tensor_tensor(dbx[:, u % 2, :], du_bank[g % 2][:, :], bc[:, b % 2, k, :], ALU.mult).then_inc(s_bx, 1)
                                dve.wait_ge(s_dec, at(l, b, UN, u + 1))
                                dve.wait_ge(s_hc, at(l, b, UN, u - 3))
                                dve.wait_ge(s_bx, at(l, b, UN, u + 1))
                                nc.vector.tensor_tensor_scan(hs[:, u % 4, :], dec_bank[u % 2][:, :], dbx[:, u % 2, :], 0.0, ALU.mult, ALU.add).then_inc(s_sc, 1)
                                if u == 3 and b:
                                    gate_y(l, b - 1, 1)
                                if u == 8:
                                    conv(l, b, b + 1)
                                if u == 18:
                                    gate_y(l, b, 0)
                                if u == 23:
                                    make_dt(l, b, b + 1)
                        gate_y(l, NB - 1, 1)
        st6 = ExitStack()
        with st6:
            bank = [st6.enter_context(nc.psum_tensor(f"s6_bank{i}", [P, 4, D], fp32)) for i in range(4)]
            sem = lambda name: st6.enter_context(nc.semaphore(name))
            s_t6, s_m6, s_r6, s_o6 = map(sem, ("s_by_token", "s_gated", "x_done", "out_stored"))
            with nc.Block() as block:
                @block.tensor
                def _(pe):
                    for b in range(B):
                        for t in range(4):
                            last = nc.tensor.transpose(bank[b][:, t, :], XT[:, b, P * t:P * t + P], ident[:, :])
                        last.then_inc(s_t6, 1)

                @block.vector
                def _(dve):
                    for b in range(B):
                        tl = slice(4 * b, 4 * b + 4)
                        dve.wait_ge(s_t6, b + 1)
                        nc.vector.tensor_tensor(GATE[:, tl, :], bank[b][:, :, :], GATE[:, tl, :], ALU.mult).then_inc(s_m6, 1)
                        dve.wait_ge(s_m6, b + 1)
                        nc.vector.tensor_tensor(X[:, tl, :], X[:, tl, :], GATE[:, tl, :], ALU.add).then_inc(s_r6, 1)

                @block.sync
                def _(sp):
                    for b in range(B):
                        sp.wait_ge(s_r6, b + 1)
                        sp.dma_start(out[b].rearrange("(k p) d -> p k d", p=P), X[:, 4 * b:4 * b + 4, :]).then_inc(s_o6, 16)
                    sp.wait_ge(s_o6, 16 * B)


def laid_out(i):
    import numpy as np

    f = lambda name: np.asarray(i[name])
    row = lambda name: np.ascontiguousarray(f(name).reshape(-1))
    t2 = lambda a: np.ascontiguousarray(np.swapaxes(a, -1, -2))
    L = 4
    wrap = lambda a, n=1: np.concatenate([a, a[:n]], 0)
    part = np.arange(128)
    spread = np.stack([(np.arange(128)[:, None] == 32 * j + part[None] % 32) for j in range(4)], 1).astype(np.float32)
    pick = np.stack([np.arange(40)[:, None] == 8 + 16 * (i // 4) + 4 * (i % 4) + part[None] // 32 for i in range(8)], 1).astype(np.float32)
    a = {
        "x": f("L0_attn_x"),
        "w_att": np.concatenate([f("L0_attn_Wq").T, f("L0_attn_Wk").T, f("L0_attn_Wv").T], 1),
        "w_mha": t2(f("L0_ffn_Wqkv")), "b_mha": row("L0_ffn_bqkv"), "w_mo": t2(f("L0_ffn_Wo")), "b_mo": row("L0_ffn_bo"),
        "w_gate0": t2(f("L0_ffn_Wg")), "g1": row("L0_ffn_g1"), "be1": row("L0_ffn_be1"), "g2": row("L0_ffn_g2"), "be2": row("L0_ffn_be2"),
        "cos_head_delta": row("L0_attn_cos_head_delta"), "cos_raw": row("L0_attn_cos_logit_scale_raw"), "delta_gain": row("L0_attn_delta_gain"),
        "bo": row("L0_attn_bo"), "subln": row("L0_attn_subln_weight"), "wo_att": t2(f("L0_attn_Wo")),
        "lq1": row("L0_attn_lambda_q1"), "lk1": row("L0_attn_lambda_k1"), "lq2": row("L0_attn_lambda_q2"), "lk2": row("L0_attn_lambda_k2"),
        "w1": f("L0_ffn_W1"), "w2": f("L0_ffn_W2"), "b2": f("L0_ffn_b2"),
        "b1": t2(f("L0_ffn_b1").reshape(8, 4, 128)),
        "ident": np.eye(128, dtype=np.float32),
        "w_in": wrap(t2(f("L1_attn_in_proj_w"))),
        "w_xp": wrap(t2(f("L1_attn_x_proj_w")).reshape(L, 2, 128, 40).transpose(0, 2, 1, 3)),
        "w_dt": wrap(t2(f("L1_attn_dt_proj_w"))),
        "pre_cols": wrap(np.concatenate([f("L1_attn_conv_w").reshape(L, 2, 128, 4).transpose(0, 2, 1, 3).reshape(L, 128, 8),
                                    t2(f("L1_attn_conv_b").reshape(L, 2, 128)), t2(f("L1_attn_dt_proj_b").reshape(L, 2, 128))], 2)),
        "w_out": t2(f("L1_attn_out_proj_w")).reshape(L, 2, 128, 128).transpose(0, 2, 1, 3),
        "d_col": t2(f("L1_attn_D").reshape(L, 2, 128)),
        "a_log": f("L1_attn_A_log").reshape(L, 8, 32, 4, 4).transpose(4, 2, 0, 1, 3).reshape(128, L, 32),
        "spread": spread, "pick": pick, "fold": np.tile(np.eye(32, dtype=np.float32), (4, 1)),
        "w_router": t2(f("L1_ffn_router_w")), "below": np.triu(np.ones((128, 128), np.float32), 1),
        "w_sg": f("L1_ffn_sg"), "w_su": f("L1_ffn_su"), "w_sd": f("L1_ffn_sd").reshape(8, 128, 128).transpose(1, 0, 2),
        "w_rg": f("L1_ffn_rg"), "w_ru": f("L1_ffn_ru"), "w_rd": f("L1_ffn_rd"),
    }
    return {k: np.ascontiguousarray(v) for k, v in a.items()}


def kernel(**inputs):
    import concourse.bacc as _bacc
    from concourse.bass_utils import run_bass_kernel_spmd as _run

    nc = _bacc.Bacc("TRN2", target_bir_lowering=False, num_devices=1)
    arrays, aps = {}, {}
    for name, a in laid_out(inputs).items():
        arrays[f"in_{name}"] = a
        aps[name] = nc.dram_tensor(f"in_{name}", list(a.shape), mybir.dt.from_np(a.dtype), kind="ExternalInput").ap()
    out = nc.dram_tensor("out_x", [B, N, D], fp32, kind="ExternalOutput").ap()
    build_stages(nc, aps, out)
    r = _run(nc, [arrays], core_ids=[0])
    return r.results[0]["out_x"]
```

```python
import concourse.bass as bass
from concourse import mybir
from contextlib import ExitStack

fp32 = mybir.dt.float32
bf16 = mybir.dt.bfloat16
u32 = mybir.dt.uint32
ALU = mybir.AluOpType
ACT = mybir.ActivationFunctionType
AX = mybir.AxisListType

P = 128
B, N, D = 4, 512, 128
T = B * N
NT = T // P
NH = 8
NE = 8
EPS = 1e-5


class Chain:

    def __init__(self, engine, semaphore, start=0):
        self.engine, self.semaphore, self.done = engine, semaphore, start

    def __call__(self, instruction, then=None):
        self.done += 1
        instruction.then_inc(self.semaphore, 1)
        self.engine.wait_ge(self.semaphore, self.done)
        if then is not None:
            self.engine.sem_inc(then, 1)


def first_max(nc, link, lg, cand, lmax, source, rank_desc, onehot):
    link(nc.vector.tensor_copy(lg[:, :, :], source))
    link(nc.vector.tensor_reduce(lmax[:, :], lg[:, :, :], AX.X, ALU.max))
    link(nc.vector.tensor_tensor(cand[:, :, :], lg[:, :, :], lmax[:, :].unsqueeze(2).broadcast_to([P, NT, NE]), ALU.is_ge))
    link(nc.vector.tensor_tensor(cand[:, :, :], cand[:, :, :], rank_desc[:, :, :], ALU.mult))
    link(nc.vector.tensor_reduce(lmax[:, :], cand[:, :, :], AX.X, ALU.max))
    link(nc.vector.tensor_tensor(onehot[:, :, :], cand[:, :, :], lmax[:, :].unsqueeze(2).broadcast_to([P, NT, NE]), ALU.is_equal))




def build_stages(nc, A, out):
    keep = ExitStack()
    with keep:
        def sb(stack, name, shape, dtype=fp32):
            return stack.enter_context(nc.sbuf_tensor(name, shape, dtype))

        XT = sb(keep, "XT", [P, B, 512])
        ident = sb(keep, "ident_sb", [P, P])
        rank_desc = sb(keep, "rank_desc", [P, NT, NE])
        GATE = sb(keep, "GATE", [P, NT, D])
        rows_u = [sb(keep, f"rows_u{i}", [P, NT], u32) for i in range(2)]
        share = sb(keep, "share", [P, 2, NT])
        eo_dram = nc.dram_tensor("expert_outs", [NE * (5 * T // (4 * NE)), D], fp32).ap()
        x_dram = nc.dram_tensor("x_kept", [P, NT, D], fp32).ap()
        keepx = ExitStack()
        X = sb(keepx, "X", [P, NT, D])
        XN = sb(keepx, "XN", [P, NT, D])
        keep0 = ExitStack()
        with keep0:
            Y1 = sb(keep0, "Y1", [P, NT, D])
            Y1T = sb(keep0, "Y1T", [P, T])
            ACC = sb(keep0, "ACC", [P, NT, D])
            v_tok = sb(keep0, "v_tok", [P, NT, D])
            mask0 = sb(keep0, "mask0", [P, NT, NE])
            ybig = sb(keep0, "ybig", [P, NT, NH * 34])
            delta_gain = sb(keep0, "delta_gain_sb", [P, NH])
            neg_lam = sb(keep0, "neg_lam", [P, 1])
            subln = sb(keep0, "subln_sb", [P, 16])
            bo_row = sb(keep0, "bo_row", [P, D])
            g2_row = sb(keep0, "g2_row", [P, D])
            be2_row = sb(keep0, "be2_row", [P, D])
            wo_att = sb(keep0, "wo_att_sb", [P, D])
            qk_dram = nc.dram_tensor("qk_parts", [2, 3, P, T], bf16).ap()
            st1 = ExitStack()
            with st1:
                psum = [st1.enter_context(nc.psum_tensor(f"s1_bank{i}", [P, 512], fp32)) for i in range(8)]
                w_att = sb(st1, "w_att", [P, 3 * D])
                w_mha = sb(st1, "w_mha", [P, 3 * D])
                w_mo = sb(st1, "w_mo", [P, D])
                w_gate = sb(st1, "w_gate", [P, NE])
                b_mha = sb(st1, "b_mha", [P, 3 * D])
                b_mo = sb(st1, "b_mo", [P, D])
                g1_row = sb(st1, "g1_row", [P, D])
                be1_row = sb(st1, "be1_row", [P, D])
                chd = sb(st1, "chd", [P, NH])
                craw = sb(st1, "craw", [P, 1])
                lam_in = sb(st1, "lam_in", [P, 4, 8])
                stats = sb(st1, "stats", [P, NT, 6])
                mv = sb(st1, "mv", [P, NT, 2])
                rstd = sb(st1, "rstd", [P, NT])
                neghalf = sb(st1, "neghalf", [P, 512])
                qkv = sb(st1, "qkv", [P, NT, 3 * D])
                sq = sb(st1, "sq", [P, 4, 2 * D])
                ss = sb(st1, "ss", [P, NT, 32])
                cosb = sb(st1, "cosb", [P, 16])
                xnT = sb(st1, "xnT", [P, T])
                parts = {(w, i): sb(st1, f"part_{w}{i}", [P, T], bf16) for w in "qk" for i in range(3)}
                rest = {w: sb(st1, f"rest_{w}", [P, 512]) for w in "qk"}
                prod = sb(st1, "prod", [P, 2, 4, D])
                att = sb(st1, "att", [P, 4, 4, 4, 4])
                amax = sb(st1, "amax", [P, 64])
                mo = sb(st1, "mo", [P, NT, D])
                mh = sb(st1, "mh", [P, NT, 3 * D])
                smalls = sb(st1, "smalls", [P, 64])
                lg = sb(st1, "lg", [P, NT, NE])
                lgt = sb(st1, "lgt", [P, NT, NE])
                lmax = sb(st1, "lmax", [P, NT])

                sem = lambda name: st1.enter_context(nc.semaphore(name))
                s_x = [sem(f"x_loaded{b}") for b in range(B)]
                s_w = sem("weights_loaded")
                s_stat, s_rstd, s_xn, s_xnt_ps, s_xnt = map(sem, ("stats_ready", "rstd_ready", "xn_ready", "xnT_in_psum", "xnT_ready"))
                s_proj, s_qkv, s_mh = map(sem, ("proj_in_psum", "qkv_ready", "mha_in_ready"))
                s_sq, s_ss, s_rn, s_nrm, s_qkn = map(sem, ("squares_ready", "sumsq_ready", "sumsq_bounded", "norms_ready", "qk_normed"))
                s_qkt, s_hi, s_r1, s_mid, s_lo, s_qkst = map(sem, ("qkT_in_psum", "hi_ready", "rest_ready", "mid_ready", "lo_ready", "parts_stored"))
                s_cos, s_act, s_nh = map(sem, ("cos_steps", "act_steps", "neghalf_ready"))
                s_pr, s_sc, s_ex, s_at, s_pv, s_o = map(sem, ("qk_products", "scores_ready", "exps_ready", "att_ready", "pv_products", "mha_out"))
                s_ot_ps, s_ot, s_wo, s_y0, s_ys, s_yr, s_y1 = map(sem, ("oT_in_psum", "oT_ready", "wo_in_psum", "y_summed", "y_stats", "y_rstd", "y_normed"))
                s_yt_ps, s_yt, s_lgp, s_dch, s_pch, s_ach = map(sem, ("yT_in_psum", "yT_ready", "logits_in_psum", "vector_steps", "pool_steps", "scalar_steps"))
                NW = 0

                with nc.Block() as block:
                    loads = [(ident[:, :], A["ident"]), (w_att[:, :], A["w_att"]), (w_mha[:, :], A["w_mha"]), (w_mo[:, :], A["w_mo"]),
                             (w_gate[:, :], A["w_gate0"]), (b_mha[:, :], A["b_mha"].partition_broadcast(P)),
                             (b_mo[:, :], A["b_mo"].partition_broadcast(P)), (g1_row[:, :], A["g1"].partition_broadcast(P)),
                             (be1_row[:, :], A["be1"].partition_broadcast(P)), (chd[:, :], A["cos_head_delta"].partition_broadcast(P)),
                             (craw[:, :], A["cos_raw"].partition_broadcast(P)), (delta_gain[:, :], A["delta_gain"].partition_broadcast(P)),
                             (bo_row[:, :], A["bo"].partition_broadcast(P)), (subln[:, :], A["subln"].partition_broadcast(P)),
                             (g2_row[:, :], A["g2"].partition_broadcast(P)), (be2_row[:, :], A["be2"].partition_broadcast(P)),
                             (wo_att[:, :], A["wo_att"])]
                    loads += [(lam_in[:, i, :], A[n].partition_broadcast(P)) for i, n in enumerate(("lq1", "lk1", "lq2", "lk2"))]
                    ALL_W = 16 * len(loads)

                    @block.sync
                    def _(sp):
                        for b in range(B):
                            sp.dma_start(X[:, 4 * b:4 * b + 4, :], A["x"][b].rearrange("(k p) d -> p k d", p=P)).then_inc(s_x[b], 16)
                        for dst, src in loads:
                            sp.dma_start(dst, src).then_inc(s_w, 16)
                        for b in range(B):
                            sp.wait_ge(s_mid, 2 * b + 2)
                            sp.wait_ge(s_lo, 2 * b + 2)
                            for n, w in enumerate("qk"):
                                for i in range(3):
                                    sp.dma_start(qk_dram[n, i, :, 512 * b:512 * b + 512], parts[w, i][:, 512 * b:512 * b + 512]).then_inc(s_qkst, 16)
                        sp.wait_ge(s_qkst, 16 * 6 * B)

                    @block.vector
                    def _(dve):
                        link = Chain(dve, s_dch)
                        nc.vector.memset(neghalf[:, :], -0.5).then_inc(s_nh, 1)
                        for b in range(B):
                            dve.wait_ge(s_x[b], 16)
                            for t in range(4 * b, 4 * b + 4):
                                last = nc.vector.bn_stats(stats[:, t, :], X[:, t, :])
                            link(last)
                            for t in range(4 * b, 4 * b + 4):
                                last = nc.vector.bn_aggr(mv[:, t, :], stats[:, t, :])
                            last.then_inc(s_stat, 1)
                        for b in range(B):
                            dve.wait_ge(s_rstd, b + 1)
                            for t in range(4 * b, 4 * b + 4):
                                last = nc.vector.tensor_scalar(XN[:, t, :], X[:, t, :], mv[:, t, 0:1], rstd[:, t:t + 1], ALU.subtract, ALU.mult)
                            last.then_inc(s_xn, 1)
                        dve.wait_ge(s_w, ALL_W)
                        link(nc.vector.tensor_reduce(smalls[:, 0:1], chd[:, :], AX.X, ALU.add))
                        link(nc.vector.tensor_scalar(smalls[:, 1:2], smalls[:, 0:1], 1.0 / NH, None, ALU.mult))
                        nc.vector.tensor_scalar(smalls[:, 8:16], chd[:, :], smalls[:, 1:2], None, ALU.subtract).then_inc(s_cos, 1)
                        link(nc.vector.tensor_tensor(smalls[:, 16:24], lam_in[:, 0, :], lam_in[:, 1, :], ALU.mult))
                        link(nc.vector.tensor_tensor(smalls[:, 24:32], lam_in[:, 2, :], lam_in[:, 3, :], ALU.mult))
                        nc.vector.tensor_reduce(smalls[:, 2:4], smalls[:, 16:32].rearrange("p (a b) -> p a b", b=8), AX.X, ALU.add).then_inc(s_cos, 1)
                        dve.wait_ge(s_act, 3)
                        link(nc.vector.tensor_scalar(smalls[:, 6:7], smalls[:, 4:5], 1.0, None, ALU.add))
                        link(nc.vector.reciprocal(smalls[:, 7:8], smalls[:, 6:7]))
                        link(nc.vector.tensor_scalar(smalls[:, 40:48], smalls[:, 32:40], 0.5, 1.0, ALU.mult, ALU.add))
                        link(nc.vector.tensor_scalar(smalls[:, 48:56], smalls[:, 40:48], smalls[:, 7:8], 15.0, ALU.mult, ALU.mult))
                        cv = cosb[:, :].rearrange("p (h s) -> p h s", s=2)
                        link(nc.vector.tensor_scalar(cv[:, :, 0], smalls[:, 48:56], 1.0, None, ALU.mult))
                        link(nc.vector.tensor_scalar(cv[:, :, 1], smalls[:, 48:56], -1.0, None, ALU.mult))
                        link(nc.vector.tensor_tensor(smalls[:, 56:57], smalls[:, 59:60], smalls[:, 58:59], ALU.subtract))
                        link(nc.vector.tensor_scalar(neg_lam[:, :], smalls[:, 56:57], 0.5, None, ALU.subtract))
                        def norm_and_split(b):
                            dve.wait_ge(s_sq, b + 1)
                            ssb = ss[:, 4 * b:4 * b + 4, :]
                            nc.vector.tensor_reduce(ssb.rearrange("p t g -> p (t g)"), sq[:, :, :].rearrange("p t (g d) -> p (t g) d", d=8),
                                                    AX.X, ALU.add).then_inc(s_ss, 1)
                            dve.wait_ge(s_nrm, b + 1)
                            link(nc.vector.reciprocal(ssb.rearrange("p t g -> p (t g)"), ssb.rearrange("p t g -> p (t g)")))
                            link(nc.vector.tensor_tensor(ssb[:, :, 0:16], ssb[:, :, 0:16], cosb[:, :].unsqueeze(1).broadcast_to([P, 4, 16]), ALU.mult))
                            qk = qkv[:, 4 * b:4 * b + 4, 0:2 * D].rearrange("p t (g d) -> p t g d", d=8)
                            nc.vector.tensor_tensor(qk, qk, ssb.unsqueeze(3).broadcast_to([P, 4, 32, 8]), ALU.mult).then_inc(s_qkn, 1)
                            for n, w in enumerate("qk"):
                                c = slice(512 * b, 512 * b + 512)
                                dve.wait_ge(s_hi, 2 * b + n + 1)
                                if b:
                                    dve.wait_ge(s_lo, 2 * b + n - 1)
                                    dve.wait_ge(s_mid, 2 * b + n - 1)
                                nc.vector.tensor_tensor(rest[w][:, :], psum[4 + n][:, :], parts[w, 0][:, c], ALU.subtract).then_inc(s_r1, 1)
                                dve.wait_ge(s_mid, 2 * b + n + 1)
                                nc.vector.tensor_tensor(parts[w, 2][:, c], rest[w][:, :], parts[w, 1][:, c], ALU.subtract).then_inc(s_lo, 1)
                        for b in range(B):
                            for t in range(4 * b, 4 * b + 4):
                                dve.wait_ge(s_proj, t + 1)
                                nc.vector.tensor_tensor(mh[:, t, :], psum[2 * (t % 2) + 1][:, 0:3 * D], b_mha[:, :], ALU.add).then_inc(s_mh, 1)
                            if b:
                                norm_and_split(b - 1)
                        norm_and_split(B - 1)
                        for u in range(16):
                            nb, b1 = u // 4, u % 4
                            dve.wait_ge(s_pr, u + 1)
                            nc.vector.tensor_reduce(att[:, nb, b1, :, :].rearrange("p k h -> p (k h)"),
                                                    prod[:, u % 2, :, :].rearrange("p k (h d) -> p (k h) d", d=32), AX.X, ALU.add).then_inc(s_sc, 1)
                        a_kh = att[:, :, :, :, :].rearrange("p n q k h -> p (n q) k h")
                        a_hk = att[:, :, :, :, :].rearrange("p n q k h -> p (n q) h k")
                        am = amax[:, :].rearrange("p (a h) -> p a h", h=4)
                        dve.wait_ge(s_sc, 16)
                        link(nc.vector.tensor_reduce(am, a_hk, AX.X, ALU.max))
                        nc.vector.tensor_tensor(a_kh, a_kh, am.unsqueeze(2).broadcast_to([P, 16, 4, 4]), ALU.subtract).then_inc(s_sc, 1)
                        dve.wait_ge(s_ex, 1)
                        link(nc.vector.tensor_reduce(am, a_hk, AX.X, ALU.add))
                        link(nc.vector.reciprocal(amax[:, :], amax[:, :]))
                        nc.vector.tensor_tensor(a_kh, a_kh, am.unsqueeze(2).broadcast_to([P, 16, 4, 4]), ALU.mult).then_inc(s_at, 1)
                        for u in range(16):
                            nb, b1 = u // 4, u % 4
                            dve.wait_ge(s_pv, u + 1)
                            nc.vector.tensor_reduce(mo[:, 4 * b1 + nb, :], prod[:, u % 2, :, :].rearrange("p k d -> p d k"), AX.X, ALU.add).then_inc(s_o, 1)
                        for b in range(B):
                            dve.wait_ge(s_wo, b + 1)
                            tl = slice(4 * b, 4 * b + 4)
                            link(nc.vector.tensor_tensor(Y1[:, tl, :], psum[6 + b % 2][:, :].rearrange("p (t d) -> p t d", d=D), XN[:, tl, :], ALU.add))
                            nc.vector.tensor_tensor(Y1[:, tl, :], Y1[:, tl, :], b_mo[:, :].unsqueeze(1).broadcast_to([P, 4, D]), ALU.add).then_inc(s_y0, 1)
                            dve.wait_ge(s_y0, b + 1)
                            for t in range(4 * b, 4 * b + 4):
                                last = nc.vector.bn_stats(stats[:, t, :], Y1[:, t, :])
                            link(last)
                            for t in range(4 * b, 4 * b + 4):
                                last = nc.vector.bn_aggr(mv[:, t, :], stats[:, t, :])
                            last.then_inc(s_ys, 1)
                        for b in range(B):
                            tl = slice(4 * b, 4 * b + 4)
                            dve.wait_ge(s_yr, b + 1)
                            for t in range(4 * b, 4 * b + 4):
                                last = nc.vector.tensor_scalar(Y1[:, t, :], Y1[:, t, :], mv[:, t, 0:1], rstd[:, t:t + 1], ALU.subtract, ALU.mult)
                            link(last)
                            link(nc.vector.tensor_tensor(Y1[:, tl, :], Y1[:, tl, :], g1_row[:, :].unsqueeze(1).broadcast_to([P, 4, D]), ALU.mult))
                            nc.vector.tensor_tensor(Y1[:, tl, :], Y1[:, tl, :], be1_row[:, :].unsqueeze(1).broadcast_to([P, 4, D]), ALU.add).then_inc(s_y1, 1)
                        dve.wait_ge(s_lgp, 1)
                        first_max(nc, link, lg, lgt, lmax, psum[0][:, 0:NT * NE].rearrange("p (t e) -> p t e", e=NE), rank_desc, mask0)

                    @block.gpsimd
                    def _(pool):
                        link = Chain(pool, s_pch)
                        pool.wait_ge(s_nh, 1)
                        for e in range(NE):
                            link(nc.gpsimd.memset(rank_desc[:, :, e:e + 1], float(NE - e)))
                        for b in range(B):
                            pool.wait_ge(s_stat, b + 1)
                            link(nc.gpsimd.tensor_scalar(rstd[:, 4 * b:4 * b + 4], mv[:, 4 * b:4 * b + 4, 1], EPS, None, ALU.add))
                            nc.gpsimd.tensor_tensor(rstd[:, 4 * b:4 * b + 4], rstd[:, 4 * b:4 * b + 4], neghalf[:, 0:4], ALU.pow).then_inc(s_rstd, 1)
                        for b in range(B):
                            tl = slice(4 * b, 4 * b + 4)
                            pool.wait_ge(s_qkv, 4 * b + 4)
                            if b:
                                pool.wait_ge(s_ss, b)
                            nc.gpsimd.tensor_tensor(sq[:, :, :], qkv[:, tl, 0:2 * D], qkv[:, tl, 0:2 * D], ALU.mult).then_inc(s_sq, 1)
                            pool.wait_ge(s_ss, b + 1)
                            ssb = ss[:, tl, :].rearrange("p t g -> p (t g)")
                            nc.gpsimd.tensor_scalar(ssb, ssb, 1e-12, None, ALU.max).then_inc(s_rn, 1)
                        pool.wait_ge(s_mh, NT)
                        mt = mh[:, :, :].rearrange("p (b n) c -> p n b c", n=4)
                        for u in range(16):
                            nb, b1 = u // 4, u % 4
                            if u >= 2:
                                pool.wait_ge(s_sc, u - 1)
                            nc.gpsimd.tensor_tensor(prod[:, u % 2, :, :], mt[:, nb, b1, 0:D].unsqueeze(1).broadcast_to([P, 4, D]),
                                                    mt[:, nb, :, D:2 * D], ALU.mult).then_inc(s_pr, 1)
                        pool.wait_ge(s_at, 1)
                        for u in range(16):
                            nb, b1 = u // 4, u % 4
                            if u >= 2:
                                pool.wait_ge(s_o, u - 1)
                            for b2 in range(4):
                                last = nc.gpsimd.tensor_tensor(prod[:, u % 2, b2, :].rearrange("p (h d) -> p h d", d=32),
                                                    mt[:, nb, b2, 2 * D:3 * D].rearrange("p (h d) -> p h d", d=32),
                                                    att[:, nb, b1, b2, :].unsqueeze(2).broadcast_to([P, 4, 32]), ALU.mult)
                            last.then_inc(s_pv, 1)
                        for b in range(B):
                            pool.wait_ge(s_ys, b + 1)
                            link(nc.gpsimd.tensor_scalar(rstd[:, 4 * b:4 * b + 4], mv[:, 4 * b:4 * b + 4, 1], EPS, None, ALU.add))
                            nc.gpsimd.tensor_tensor(rstd[:, 4 * b:4 * b + 4], rstd[:, 4 * b:4 * b + 4], neghalf[:, 0:4], ALU.pow).then_inc(s_yr, 1)

                    @block.scalar
                    def _(act):
                        act.preload_act_table_set("exp_and_others")

                        def parts_of(b):
                            act.wait_ge(s_rn, b + 1)
                            ssb = ss[:, 4 * b:4 * b + 4, :].rearrange("p t g -> p (t g)")
                            nc.scalar.activation(ssb, ssb, ACT.Sqrt).then_inc(s_nrm, 1)
                            c = slice(512 * b, 512 * b + 512)
                            for n, w in enumerate("qk"):
                                act.wait_ge(s_qkt, 2 * b + n + 1)
                                nc.scalar.activation(parts[w, 0][:, c], psum[4 + n][:, :], ACT.Copy).then_inc(s_hi, 1)
                            for n, w in enumerate("qk"):
                                act.wait_ge(s_r1, 2 * b + n + 1)
                                nc.scalar.activation(parts[w, 1][:, c], rest[w][:, :], ACT.Copy).then_inc(s_mid, 1)

                        for b in range(B):
                            act.wait_ge(s_xnt_ps, b + 1)
                            nc.scalar.activation(xnT[:, 512 * b:512 * b + 512], psum[6 + b % 2][:, :], ACT.Copy).then_inc(s_xnt, 1)
                            if b == 0:
                                act.wait_ge(s_w, ALL_W)
                                nc.scalar.activation(smalls[:, 4:5], craw[:, :], ACT.Exp, scale=-1.0).then_inc(s_act, 1)
                                act.wait_ge(s_cos, 2)
                                nc.scalar.activation(smalls[:, 32:40], smalls[:, 8:16], ACT.Tanh).then_inc(s_act, 1)
                                nc.scalar.activation(smalls[:, 58:60], smalls[:, 2:4], ACT.Exp).then_inc(s_act, 1)
                            for t in range(4 * b, 4 * b + 4):
                                act.wait_ge(s_proj, t + 1)
                                nc.scalar.activation(qkv[:, t, :], psum[2 * (t % 2)][:, 0:3 * D], ACT.Copy).then_inc(s_qkv, 1)
                            if b:
                                parts_of(b - 1)
                        parts_of(B - 1)
                        nc.scalar.activation(v_tok[:, :, :], qkv[:, :, 2 * D:3 * D], ACT.Copy).then_inc(s_ach, 1)
                        act.wait_ge(s_sc, 17)
                        af = att[:, :, :, :, :].rearrange("p n q k h -> p (n q k h)")
                        nc.scalar.activation(af, af, ACT.Exp, scale=32.0 ** -0.5).then_inc(s_ex, 1)
                        for b in range(B):
                            act.wait_ge(s_ot_ps, b + 1)
                            nc.scalar.activation(xnT[:, 512 * b:512 * b + 512], psum[b % 2][:, :], ACT.Copy).then_inc(s_ot, 1)
                        for b in range(B):
                            act.wait_ge(s_yt_ps, b + 1)
                            nc.scalar.activation(Y1T[:, 512 * b:512 * b + 512], psum[2 + b % 2][:, :], ACT.Copy).then_inc(s_yt, 1)

                    @block.tensor
                    def _(pe):
                        pe.wait_ge(s_w, ALL_W)

                        def qk_transposes(b):
                            pe.wait_ge(s_qkn, b + 1)
                            for n in range(2):
                                if b:
                                    pe.wait_ge(s_r1, 2 * b + n - 1)
                                for t in range(4):
                                    last = nc.tensor.transpose(psum[4 + n][:, P * t:P * t + P], qkv[:, 4 * b + t, n * D:n * D + D], ident[:, :])
                                last.then_inc(s_qkt, 1)

                        for b in range(B):
                            pe.wait_ge(s_xn, b + 1)
                            if b >= 2:
                                pe.wait_ge(s_xnt, b - 1)
                            for t in range(4):
                                last = nc.tensor.transpose(psum[6 + b % 2][:, P * t:P * t + P], XN[:, 4 * b + t, :], ident[:, :])
                            last.then_inc(s_xnt_ps, 1)
                            pe.wait_ge(s_xnt, b + 1)
                            for t in range(4 * b, 4 * b + 4):
                                if t >= 2:
                                    pe.wait_ge(s_qkv, t - 1)
                                    pe.wait_ge(s_mh, t - 1)
                                nc.tensor.matmul(psum[2 * (t % 2)][:, 0:3 * D], xnT[:, P * t:P * t + P], w_att[:, :], start=True, stop=True)
                                nc.tensor.matmul(psum[2 * (t % 2) + 1][:, 0:3 * D], xnT[:, P * t:P * t + P], w_mha[:, :], start=True, stop=True).then_inc(s_proj, 1)
                            if b:
                                qk_transposes(b - 1)
                        qk_transposes(B - 1)
                        for b in range(B):
                            pe.wait_ge(s_o, 12 + b + 1)
                            pe.wait_ge(s_qkv, NT)
                            pe.wait_ge(s_mh, NT)
                            if b >= 2:
                                pe.wait_ge(s_ot, b - 1)
                            for t in range(4):
                                last = nc.tensor.transpose(psum[b % 2][:, P * t:P * t + P], mo[:, 4 * b + t, :], ident[:, :])
                            last.then_inc(s_ot_ps, 1)
                        for b in range(B):
                            pe.wait_ge(s_ot, b + 1)
                            if b >= 2:
                                pe.wait_ge(s_y0, b - 1)
                            for t in range(4):
                                last = nc.tensor.matmul(psum[6 + b % 2][:, P * t:P * t + P], xnT[:, 512 * b + P * t:512 * b + P * t + P], w_mo[:, :], start=True, stop=True)
                            last.then_inc(s_wo, 1)
                        for b in range(B):
                            pe.wait_ge(s_y1, b + 1)
                            if b >= 2:
                                pe.wait_ge(s_yt, b - 1)
                            for t in range(4):
                                last = nc.tensor.transpose(psum[2 + b % 2][:, P * t:P * t + P], Y1[:, 4 * b + t, :], ident[:, :])
                            last.then_inc(s_yt_ps, 1)
                        pe.wait_ge(s_yt, B)
                        pe.wait_ge(s_ot, B)
                        for t in range(NT):
                            last = nc.tensor.matmul(psum[0][:, NE * t:NE * t + NE], Y1T[:, P * t:P * t + P], w_gate[:, :], start=True, stop=True)
                        last.then_inc(s_lgp, 1)
            st2 = ExitStack()
            with st2:
                bank_d = st2.enter_context(nc.psum_tensor("bank_d", [P, 512], fp32))
                bank_l = [st2.enter_context(nc.psum_tensor(f"bank_l{i}", [P, 2, 512], fp32)) for i in range(2)]
                bank_pv = st2.enter_context(nc.psum_tensor("bank_pv", [P, 512], fp32))
                bank_h = st2.enter_context(nc.psum_tensor("bank_h", [P, 512], fp32))
                bank_o = st2.enter_context(nc.psum_tensor("bank_o", [P, 4, D], fp32))
                kst = [sb(st2, f"k_stack{i}", [112, T], bf16) for i in range(2)]
                qst = [sb(st2, f"q_stack{i}", [112, T], bf16) for i in range(2)]
                w1 = [sb(st2, f"w1_{i}", [P, 512]) for i in range(2)]
                w2 = [sb(st2, f"w2_{i}", [P, 4, D]) for i in range(2)]
                b1 = [sb(st2, f"b1_{i}", [P, 4]) for i in range(2)]
                vh = [sb(st2, f"v_head{i}", [P, NT, 32]) for i in range(2)]
                dgh = sb(st2, "dgh", [P, 2])
                gt = sb(st2, "gt", [P, 2, 512])
                tt = sb(st2, "tt", [P, 2, 2, 512])
                ex = sb(st2, "ex", [P, 2, 4, 2, 512])
                hid = sb(st2, "hid", [P, 2, 4, 512])
                pvs = sb(st2, "pvs", [P, 512])
                tmp = sb(st2, "tmp", [P, 4, D])

                sem = lambda name: st2.enter_context(nc.semaphore(name))
                s_ld = [sem(f"head_loaded{i}") for i in range(2)]
                s_z, s_vh, s_dg = sem("stacks_cleared"), sem("v_head_ready"), sem("gain_of_head")
                s_D, s_L, s_G, s_T, s_E = map(sem, ("diff_in_psum", "logits_in_psum2", "gate_ready", "sums_ready", "exp_ready"))
                s_pvd, s_pvs, s_pvt, s_yb = map(sem, ("pv_done", "pv_copied", "pv_turned", "pv_kept"))
                s_h, s_relu, s_dn, s_acc, s_dch = map(sem, ("hidden_in_psum", "hidden_ready", "expert_out", "expert_added", "vector_steps2"))
                LEAD, STEPS, UNITS, LOADS = 2, 32, 8, 15
                step = lambda q, n: LEAD + STEPS * q + n
                unit = lambda q, n: LEAD + UNITS * q + n

                with nc.Block() as block:
                    def load_head(sp, h, i):
                        for s in range(2):
                            rows = bass.ds(h * 16 + 8 * s, 8)
                            for n, (stack, order) in enumerate(((qst[i], (0, 1, 2, 0, 1, 0)), (kst[i], (0, 0, 0, 1, 1, 2)))):
                                if n == 0:
                                    groups = [(0, 0, 3), (3, 0, 2), (5, 0, 1)]
                                    for at, part, k in groups:
                                        sp.dma_start(stack[64 * s + 8 * at:64 * s + 8 * (at + k), :], qk_dram[0, part:part + k, rows, :]).then_inc(s_ld[i], 16)
                                else:
                                    groups = [(0, 0, 3), (3, 1, 2), (5, 2, 1)]
                                    for at, part, k in groups:
                                        sp.dma_start(stack[64 * s + 8 * at:64 * s + 8 * (at + k), :],
                                                     qk_dram[1, part:part + 1, rows, :].broadcast_to([k, 8, T])).then_inc(s_ld[i], 16)
                        sp.dma_start(w1[i][:, :], A["w1"][bass.ds(h, 1), :, :].rearrange("o p f -> p (o f)")).then_inc(s_ld[i], 16)
                        sp.dma_start(w2[i][:, :, :], A["w2"][bass.ds(h, 1), :, :].rearrange("o (k p) d -> p (o k) d", p=P)).then_inc(s_ld[i], 16)
                        sp.dma_start(b1[i][:, :], A["b1"][bass.ds(h, 1), :, :].rearrange("o p k -> p (o k)")).then_inc(s_ld[i], 16)

                    @block.sync
                    def _(sp):
                        sp.wait_ge(s_z, 4)
                        for i in range(2):
                            load_head(sp, i, i)
                        with sp.Fori(0, 3) as q:
                            for i in range(2):
                                sp.wait_ge(s_dn, unit(q, 4 * i + 4))
                                sp.wait_ge(s_z, 4)
                                load_head(sp, q * 2 + (2 + i), i)

                    @block.gpsimd
                    def _(pool):
                        for t in (kst[0], kst[1], qst[0], qst[1]):
                            nc.gpsimd.memset(t[:, :], 0.0).then_inc(s_z, 1)
                        nc.gpsimd.memset(ACC[:, :, :], 0.0).then_inc(s_z, 1)
                        for i in range(2):
                            nc.gpsimd.memset(vh[i][:, :, :], 0.0).then_inc(s_z, 1)
                        pool.wait_ge(s_z, 7)
                        for i in range(2):
                            nc.gpsimd.memset(vh[i][:, :, 16:17], 1.0).then_inc(s_z, 1)

                        def copy_v(h, i):
                            nc.gpsimd.tensor_copy(dgh[:, i:i + 1], delta_gain[:, bass.ds(h, 1)]).then_inc(s_dg, 1)
                            nc.gpsimd.tensor_copy(vh[i][:, :, 0:16], v_tok[:, :, bass.ds(h * 16, 16)]).then_inc(s_vh, 1)

                        for i in range(2):
                            copy_v(i, i)
                        with pool.Fori(0, 3) as q:
                            for i in range(2):
                                pool.wait_ge(s_pvd, unit(q, 4 * i + 4))
                                copy_v(q * 2 + (2 + i), i)

                    @block.tensor
                    def _(pe):
                        for s in (s_D, s_L, s_pvd, s_pvt, s_h, s_dn):
                            pe.sem_inc(s, LEAD)
                        pe.wait_ge(s_z, 9)

                        def scores(q, st):
                            u, mb = st // 4, st % 4
                            i, b = u // 4, u % 4
                            if st % 16 == 0:
                                pe.wait_ge(s_ld[i], q * (16 * LOADS) + 16 * LOADS)
                            k = slice(512 * b + P * mb, 512 * b + P * mb + P)
                            n = slice(512 * b, 512 * b + 512)
                            pe.wait_ge(s_G, step(q, st))
                            nc.tensor.matmul(bank_d[:, :], kst[i][:, k], qst[i][:, n], start=True, stop=True).then_inc(s_D, 1)
                            pe.wait_ge(s_T, step(q, st - 1))
                            nc.tensor.matmul(bank_l[st % 2][:, 0, :], kst[i][0:48, k], qst[i][0:48, n], start=True, stop=True)
                            nc.tensor.matmul(bank_l[st % 2][:, 1, :], kst[i][64:112, k], qst[i][64:112, n], start=True, stop=True).then_inc(s_L, 1)

                        def hidden(q, st):
                            u, f = st // 4, st % 4
                            i, b = u // 4, u % 4
                            pe.wait_ge(s_relu, step(q, st))
                            nc.tensor.matmul(bank_h[:, :], w1[i][:, P * f:P * f + P], Y1T[:, 512 * b:512 * b + 512], start=True, stop=True).then_inc(s_h, 1)

                        def weigh(q, u, pair):
                            i, b = u // 4, u % 4
                            if pair == 0:
                                pe.wait_ge(s_yb, unit(q, u))
                                pe.wait_ge(s_vh, q * 2 + (i + 1))
                            pe.wait_ge(s_E, step(q, 4 * u + 2 * pair + 2))
                            for m in range(2):
                                for s in range(2):
                                    j = 2 * s + m
                                    mb = 2 * pair + m
                                    last = nc.tensor.matmul(bank_pv[32 * j:32 * j + 32, :], vh[i][:, 4 * b + mb, :], ex[:, u % 2, mb, s, :],
                                                            start=(pair == 0), stop=(pair == 1), tile_position=(0, 32 * j), skip_group_check=True)
                            if pair == 1:
                                last.then_inc(s_pvd, 1)

                        def turn(q, u):
                            pe.wait_ge(s_pvs, unit(q, u + 1))
                            for t in range(4):
                                last = nc.tensor.transpose(bank_pv[:, P * t:P * t + P], pvs[:, P * t:P * t + P], ident[:, :])
                            last.then_inc(s_pvt, 1)

                        def expert_out(q, u):
                            i, b = u // 4, u % 4
                            pe.wait_ge(s_relu, step(q, 4 * u + 4))
                            pe.wait_ge(s_acc, unit(q, u))
                            for t in range(4):
                                for f in range(4):
                                    last = nc.tensor.matmul(bank_o[:, t, :], hid[:, u % 2, f, P * t:P * t + P], w2[i][:, f, :], start=(f == 0), stop=(f == 3))
                            last.then_inc(s_dn, 1)

                        with pe.Fori(0, 4) as q:
                            scores(q, 0)
                            for st in range(STEPS):
                                u, mb = st // 4, st % 4
                                if st < STEPS - 1:
                                    scores(q, st + 1)
                                hidden(q, st)
                                if mb == 1 and u:
                                    weigh(q, u - 1, 1)
                                if mb == 2 and u:
                                    expert_out(q, u - 1)
                                    turn(q, u - 1)
                                if mb == 3:
                                    weigh(q, u, 0)
                            weigh(q, UNITS - 1, 1)
                            expert_out(q, UNITS - 1)
                            turn(q, UNITS - 1)

                    @block.scalar
                    def _(act):
                        act.preload_act_table_set("exp_and_others")
                        for s in (s_G, s_E, s_pvs):
                            act.sem_inc(s, LEAD)
                        with act.Fori(0, 4) as q:
                            def gate(st):
                                if st % 16 == 0:
                                    act.wait_ge(s_dg, q * 2 + (st // 16 + 1))
                                act.wait_ge(s_D, step(q, st + 1))
                                act.wait_ge(s_T, step(q, st - 1))
                                nc.scalar.activation(gt[:, st % 2, :], bank_d[:, :], ACT.Tanh, scale=dgh[:, st // 16:st // 16 + 1]).then_inc(s_G, 1)

                            def exps(st):
                                act.wait_ge(s_T, step(q, st + 1))
                                if st % 4 == 0:
                                    act.wait_ge(s_pvd, unit(q, st // 4 - 1))
                                nc.scalar.activation(ex[:, (st // 4) % 2, st % 4, :, :], tt[:, st % 2, :, :], ACT.Exp).then_inc(s_E, 1)

                            def keep(u):
                                act.wait_ge(s_pvd, unit(q, u + 1))
                                act.wait_ge(s_pvt, unit(q, u))
                                nc.scalar.activation(pvs[:, :], bank_pv[:, :], ACT.Copy).then_inc(s_pvs, 1)

                            gate(0)
                            for st in range(1, STEPS):
                                gate(st)
                                exps(st - 1)
                                if st % 4 == 2 and st > 4:
                                    keep(st // 4 - 1)
                            exps(STEPS - 1)
                            keep(UNITS - 1)

                    @block.vector
                    def _(dve):
                        for s in (s_T, s_yb, s_relu, s_acc):
                            dve.sem_inc(s, LEAD)
                        dve.wait_ge(s_z, 9)
                        with dve.Fori(0, 4) as q:
                            def settle(u):
                                b = u % 4
                                e = q * 2 + u // 4
                                dve.wait_ge(s_dn, unit(q, u + 1))
                                nc.vector.tensor_tensor(tmp[:, :, :], bank_o[:, :, :], mask0[:, 4 * b:4 * b + 4, bass.ds(e, 1)].broadcast_to([P, 4, D]),
                                                        ALU.mult).then_inc(s_dch, 1)
                                dve.wait_ge(s_dch, UNITS * q + (u + 1))
                                nc.vector.tensor_tensor(ACC[:, 4 * b:4 * b + 4, :], ACC[:, 4 * b:4 * b + 4, :], tmp[:, :, :], ALU.add).then_inc(s_acc, 1)
                                dve.wait_ge(s_pvt, unit(q, u + 1))
                                nc.vector.tensor_reduce(ybig[:, 4 * b:4 * b + 4, bass.ds(e * 34, 34)].rearrange("p t (s c) -> p t s c", s=2),
                                                        bank_pv[:, :].rearrange("p (t s m c) -> p t s c m", t=4, s=2, m=2)[:, :, :, 0:17, :],
                                                        AX.X, ALU.add).then_inc(s_yb, 1)

                            for st in range(STEPS):
                                u, mb = st // 4, st % 4
                                i = u // 4
                                dve.wait_ge(s_L, step(q, st + 1))
                                dve.wait_ge(s_G, step(q, st + 1))
                                dve.wait_ge(s_E, step(q, st - 1))
                                nc.vector.tensor_tensor(tt[:, st % 2, 0, :], bank_l[st % 2][:, 0, :], gt[:, st % 2, :], ALU.add)
                                nc.vector.scalar_tensor_tensor(tt[:, st % 2, 1, :], bank_l[st % 2][:, 1, :], -1.0, gt[:, st % 2, :],
                                                               ALU.mult, ALU.subtract).then_inc(s_T, 1)
                                dve.wait_ge(s_h, step(q, st + 1))
                                if mb == 0:
                                    dve.wait_ge(s_dn, unit(q, u - 1))
                                if mb == 0 and u % 4 == 0:
                                    dve.wait_ge(s_ld[i], q * (16 * LOADS) + 16 * LOADS)
                                nc.vector.tensor_scalar(hid[:, u % 2, mb, :], bank_h[:, :], b1[i][:, mb:mb + 1], 0.0, ALU.add, ALU.max).then_inc(s_relu, 1)
                                if mb == 3 and u:
                                    settle(u - 1)
                            settle(UNITS - 1)
            st3 = ExitStack()
            with st3:
                bank = [st3.enter_context(nc.psum_tensor(f"s3_bank{i}", [P, 4, D], fp32)) for i in range(8)]
                b2blk = sb(st3, "b2blk", [P, NT, D])
                rs = sb(st3, "rs", [P, NT * NH * 2])
                yv = sb(st3, "yv", [P, NT, D])
                y2 = sb(st3, "y2", [P, NT, D])
                ms = sb(st3, "ms", [P, NT * NH])
                yT = sb(st3, "yT", [P, T])
                maskT = sb(st3, "maskT", [P, P])
                z = sb(st3, "z", [P, NT, D])
                gg = sb(st3, "gg", [P, NT, D])
                stats = sb(st3, "stats3", [P, NT, 6])
                mv = sb(st3, "mv3", [P, NT, 2])
                mw = sb(st3, "mw3", [P, NT, 2])
                rstd = sb(st3, "rstd3", [P, NT])
                rstw = sb(st3, "rstw3", [P, NT])
                neghalf = sb(st3, "neghalf3", [P, P])
                sem = lambda name: st3.enter_context(nc.semaphore(name))
                s_b2, s_dch, s_pch, s_z0 = map(sem, ("b2_loaded", "vector_steps3", "pool_steps3", "b2_cleared"))
                s_ms, s_rms, s_yv, s_yt_ps, s_yt, s_so = map(sem, ("meansq3", "rms3", "y_ready3", "yT_in_psum3", "yT_ready3", "attention_out"))
                s_mt_ps, s_mt, s_b2o, s_zst, s_zr, s_zz, s_gg = map(sem, ("maskT_in_psum", "maskT_ready", "b2_in_psum", "z_stats", "z_rstd", "z_ready", "gate_done"))
                s_xst, s_xr, s_xn, s_xt_ps, s_xt = map(sem, ("x_stats", "x_rstd", "xn_ready3", "xT_in_psum", "xT_ready"))

                with nc.Block() as block:
                    @block.sync
                    def _(sp):
                        sp.wait_ge(s_z0, 1)
                        for t in range(NT):
                            sp.dma_start(b2blk[NE * t:NE * t + NE, t, :], A["b2"]).then_inc(s_b2, 16)

                    @block.gpsimd
                    def _(pool):
                        link = Chain(pool, s_pch)
                        nc.gpsimd.memset(b2blk[:, :, :], 0.0).then_inc(s_z0, 1)
                        link(nc.gpsimd.memset(neghalf[:, :], -0.5))
                        pool.wait_ge(s_ms, 1)
                        link(nc.gpsimd.tensor_scalar(ms[:, :], ms[:, :], 1.0 / 16, 1e-5, ALU.mult, ALU.add))
                        nc.gpsimd.tensor_tensor(ms[:, :], ms[:, :], neghalf[:, :], ALU.pow).then_inc(s_rms, 1)
                        pool.wait_ge(s_zst, 1)
                        link(nc.gpsimd.tensor_scalar(rstd[:, :], mv[:, :, 1], EPS, None, ALU.add))
                        nc.gpsimd.tensor_tensor(rstd[:, :], rstd[:, :], neghalf[:, 0:NT], ALU.pow).then_inc(s_zr, 1)
                        pool.wait_ge(s_xst, 1)
                        link(nc.gpsimd.tensor_scalar(rstw[:, :], mw[:, :, 1], EPS, None, ALU.add))
                        nc.gpsimd.tensor_tensor(rstw[:, :], rstw[:, :], neghalf[:, 0:NT], ALU.pow).then_inc(s_xr, 1)

                    @block.scalar
                    def _(act):
                        act.wait_ge(s_mt_ps, 1)
                        nc.scalar.activation(maskT[:, :], bank[0][:, 0, :], ACT.Copy).then_inc(s_mt, 1)
                        for b in range(B):
                            act.wait_ge(s_yt_ps, b + 1)
                            nc.scalar.activation(yT[:, 512 * b:512 * b + 512], bank[b % 2][:, :, :].rearrange("p t d -> p (t d)"), ACT.Copy).then_inc(s_yt, 1)
                        act.wait_ge(s_zz, 1)
                        nc.scalar.activation(gg[:, :, :], z[:, :, :], ACT.Silu).then_inc(s_gg, 1)
                        for b in range(B):
                            act.wait_ge(s_xt_ps, b + 1)
                            nc.scalar.activation(XT[:, b, :], bank[4 + b][:, :, :].rearrange("p t d -> p (t d)"), ACT.Copy).then_inc(s_xt, 1)

                    @block.tensor
                    def _(pe):
                        nc.tensor.transpose(bank[0][:, 0, :], mask0[:, :, :].rearrange("p t e -> p (t e)"), ident[:, :]).then_inc(s_mt_ps, 1)
                        pe.wait_ge(s_mt, 1)
                        pe.wait_ge(s_b2, 16 * NT)
                        for t in range(NT):
                            last = nc.tensor.matmul(bank[4 + t // 4][:, t % 4, :], maskT[:, :], b2blk[:, t, :], start=True, stop=True)
                        last.then_inc(s_b2o, 1)
                        pe.wait_ge(s_yv, 1)
                        for b in range(B):
                            if b >= 2:
                                pe.wait_ge(s_yt, b - 1)
                            for t in range(4):
                                last = nc.tensor.transpose(bank[b % 2][:, t, :], yv[:, 4 * b + t, :], ident[:, :])
                            last.then_inc(s_yt_ps, 1)
                        pe.wait_ge(s_yt, B)
                        for b in range(B):
                            for t in range(4):
                                last = nc.tensor.matmul(bank[b][:, t, :], yT[:, P * (4 * b + t):P * (4 * b + t) + P], wo_att[:, :], start=True, stop=True)
                        last.then_inc(s_so, 1)
                        pe.wait_ge(s_xn, 1)
                        for b in range(B):
                            for t in range(4):
                                last = nc.tensor.transpose(bank[4 + b][:, t, :], XN[:, 4 * b + t, :], ident[:, :])
                            last.then_inc(s_xt_ps, 1)

                    @block.vector
                    def _(dve):
                        link = Chain(dve, s_dch)
                        yb = ybig[:, :, :].rearrange("p t (h s c) -> p (t h s) c", s=2, c=17)
                        link(nc.vector.reciprocal(rs[:, :].unsqueeze(2), yb[:, :, 16:17]))
                        rv = rs[:, :].rearrange("p (a s) -> p a s", s=2)
                        link(nc.vector.tensor_scalar(rv[:, :, 1], rv[:, :, 1], neg_lam[:, :], None, ALU.mult))
                        link(nc.vector.tensor_scalar(subln[:, :], subln[:, :], 0.5, None, ALU.mult))
                        link(nc.vector.tensor_tensor(yb[:, :, 0:16], yb[:, :, 0:16], rs[:, :].unsqueeze(2).broadcast_to([P, NT * NH * 2, 16]), ALU.mult))
                        y4 = ybig[:, :, :].rearrange("p t (h s c) -> p (t h) s c", s=2, c=17)
                        yf = yv[:, :, :].rearrange("p t (h d) -> p (t h) d", d=16)
                        y2f = y2[:, :, :].rearrange("p t (h d) -> p (t h) d", d=16)
                        link(nc.vector.tensor_tensor(yf, y4[:, :, 0, 0:16], y4[:, :, 1, 0:16], ALU.add))
                        link(nc.vector.tensor_tensor(y2[:, :, :], yv[:, :, :], yv[:, :, :], ALU.mult))
                        nc.vector.tensor_reduce(ms[:, :], y2f, AX.X, ALU.add).then_inc(s_ms, 1)
                        dve.wait_ge(s_b2o, 1)
                        link(nc.vector.tensor_tensor(z[:, :, :], ACC[:, :, :], Y1[:, :, :], ALU.add))
                        for b in range(B):
                            last = nc.vector.tensor_tensor(z[:, 4 * b:4 * b + 4, :], z[:, 4 * b:4 * b + 4, :], bank[4 + b][:, :, :], ALU.add)
                        link(last)
                        for t in range(NT):
                            last = nc.vector.bn_stats(stats[:, t, :], z[:, t, :])
                        link(last)
                        for t in range(NT):
                            last = nc.vector.bn_aggr(mv[:, t, :], stats[:, t, :])
                        last.then_inc(s_zst, 1)
                        dve.wait_ge(s_rms, 1)
                        link(nc.vector.tensor_tensor(yf, yf, ms[:, :].unsqueeze(2).broadcast_to([P, NT * NH, 16]), ALU.mult))
                        nc.vector.tensor_tensor(yf, yf, subln[:, :].unsqueeze(1).broadcast_to([P, NT * NH, 16]), ALU.mult).then_inc(s_yv, 1)
                        dve.wait_ge(s_zr, 1)
                        for t in range(NT):
                            last = nc.vector.tensor_scalar(z[:, t, :], z[:, t, :], mv[:, t, 0:1], rstd[:, t:t + 1], ALU.subtract, ALU.mult)
                        link(last)
                        link(nc.vector.tensor_tensor(z[:, :, :], z[:, :, :], g2_row[:, :].unsqueeze(1).broadcast_to([P, NT, D]), ALU.mult))
                        nc.vector.tensor_tensor(z[:, :, :], z[:, :, :], be2_row[:, :].unsqueeze(1).broadcast_to([P, NT, D]), ALU.add).then_inc(s_zz, 1)
                        dve.wait_ge(s_so, 1)
                        for b in range(B):
                            last = nc.vector.tensor_tensor(y2[:, 4 * b:4 * b + 4, :], bank[b][:, :, :], bo_row[:, :].unsqueeze(1).broadcast_to([P, 4, D]), ALU.add)
                        link(last)
                        dve.wait_ge(s_gg, 1)
                        link(nc.vector.tensor_tensor(y2[:, :, :], y2[:, :, :], gg[:, :, :], ALU.mult))
                        link(nc.vector.tensor_tensor(X[:, :, :], X[:, :, :], y2[:, :, :], ALU.add))
                        for t in range(NT):
                            last = nc.vector.bn_stats(stats[:, t, :], X[:, t, :])
                        link(last)
                        for t in range(NT):
                            last = nc.vector.bn_aggr(mw[:, t, :], stats[:, t, :])
                        last.then_inc(s_xst, 1)
                        dve.wait_ge(s_xr, 1)
                        for t in range(NT):
                            last = nc.vector.tensor_scalar(XN[:, t, :], X[:, t, :], mw[:, t, 0:1], rstw[:, t:t + 1], ALU.subtract, ALU.mult)
                        last.then_inc(s_xn, 1)
        st4 = ExitStack()
        with st4:
            CAP = int(1.25 * T / NE)
            ROWS = NE * CAP
            FAR = 1.0e6
            g_bank = [st4.enter_context(nc.psum_tensor(f"g_bank{i}", [P, 512], fp32)) for i in range(2)]
            u_bank = [st4.enter_context(nc.psum_tensor(f"u_bank{i}", [P, 512], fp32)) for i in range(2)]
            o_bank = st4.enter_context(nc.psum_tensor("o_bank4", [P, 4, D], fp32))
            e_bank = st4.enter_context(nc.psum_tensor("e_bank4", [P, 4, D], fp32))
            x_bank = st4.enter_context(nc.psum_tensor("x_bank4", [P, 512], fp32))
            r_bank = st4.enter_context(nc.psum_tensor("r_bank4", [P, 512], fp32))
            xg_dram = nc.dram_tensor("expert_rows", [ROWS, D], fp32).ap()
            w_r = sb(st4, "w_r", [P, NE])
            w_sg = sb(st4, "w_sg", [P, 1024])
            w_su = sb(st4, "w_su", [P, 1024])
            w_sd = sb(st4, "w_sd", [P, 8, D])
            w_rg = [sb(st4, f"w_rg{i}", [P, 512]) for i in range(2)]
            w_ru = [sb(st4, f"w_ru{i}", [P, 512]) for i in range(2)]
            w_rd = [sb(st4, f"w_rd{i}", [P, 4, D]) for i in range(2)]
            below = sb(st4, "below_sb", [P, P])
            ones = sb(st4, "ones4", [P, P])
            zeros = sb(st4, "zeros4", [P, 20, D])
            neghalf = sb(st4, "neghalf4", [P, NT])
            base_row = sb(st4, "base_row", [P, NT, NE])
            sq = sb(st4, "sq4", [P, NT, D])
            pr = sb(st4, "pr", [P, NT, NE])
            p2 = sb(st4, "p2", [P, NT, NE])
            cand = sb(st4, "cand4", [P, NT, NE])
            oh = [sb(st4, f"oh{i}", [P, NT, NE]) for i in range(2)]
            sel = sb(st4, "sel", [P, NT, NE])
            cum = [sb(st4, f"cum{i}", [P, NT + 1, NE]) for i in range(2)]
            kept = sb(st4, "kept", [P, NT, NE])
            row = sb(st4, "row4", [P, NT, NE])
            cols = sb(st4, "cols4", [P, 12, NT])
            hid = sb(st4, "hid4", [P, 2, 8, 512])
            sil = sb(st4, "sil4", [P, 2, 512])
            xg = [sb(st4, f"xg{i}", [P, 3, D]) for i in range(2)]
            xgT = sb(st4, "xgT", [P, 2, CAP])
            eo = sb(st4, "eo", [P, 2, 3, D])

            sem = lambda name: st4.enter_context(nc.semaphore(name))
            s_w4, s_w8 = sem("shared_loaded"), [sem(f"expert_loaded{i}") for i in range(2)]
            s_xg = [sem(f"rows_loaded{i}") for i in range(2)]
            s_lg4, s_sq4, s_ms4, s_rn4, s_x4, s_e4, s_sel, s_rk, s_rows = map(sem, ("logits4", "squares4", "meansq4", "rnorm4", "logits_shifted", "exps4", "selected", "ranks", "rows_known"))
            s_dch, s_pch, s_clr, s_zf, s_scat = map(sem, ("vector_steps4", "pool_steps4", "cleared4", "rows_cleared_x_stored", "scattered"))
            s_gu, s_si, s_hd, s_od, s_oc = map(sem, ("gate_up_in_psum", "silu_done", "hidden_done", "shared_out_in_psum", "shared_out_kept"))
            s_tp, s_tc, s_gu8, s_si8, s_hd8, s_ed, s_ec = map(sem, ("rowsT_in_psum", "rowsT_kept", "gate_up_in_psum8", "silu_done8", "hidden_done8", "expert_out_in_psum", "expert_out_kept"))
            s_es = [sem(f"expert_out_stored{i}") for i in range(2)]
            LEAD = 4
            at = lambda i, per, k: i * per + (LEAD + k)

            with nc.Block() as block:
                @block.sync
                def _(sp):
                    for dst, src in ((w_r[:, :], A["w_router"]), (below[:, :], A["below"]), (w_sg[:, :], A["w_sg"]), (w_su[:, :], A["w_su"]), (w_sd[:, :, :], A["w_sd"])):
                        sp.dma_start(dst, src).then_inc(s_w4, 16)
                    sp.dma_start(x_dram, X[:, :, :]).then_inc(s_zf, 16)
                    sp.wait_ge(s_clr, 1)
                    sp.dma_start(xg_dram.rearrange("(p k) d -> p k d", p=P), zeros[:, :, :]).then_inc(s_zf, 16)

                    def load_weights(e, i):
                        one = lambda x: x[bass.ds(e, 1)]
                        sp.dma_start(w_rg[i][:, :], one(A["w_rg"]).rearrange("o p f -> p (o f)")).then_inc(s_w8[i], 16)
                        sp.dma_start(w_ru[i][:, :], one(A["w_ru"]).rearrange("o p f -> p (o f)")).then_inc(s_w8[i], 16)
                        sp.dma_start(w_rd[i][:, :, :], one(A["w_rd"]).rearrange("o (k p) d -> p (o k) d", p=P)).then_inc(s_w8[i], 16)

                    def load_rows(e, i):
                        for k in range(3):
                            n = min(P, CAP - P * k)
                            sp.dma_start(xg[i][0:n, k, :], xg_dram[bass.ds(e * CAP + P * k, n), :]).then_inc(s_xg[i], 16)

                    for i in range(2):
                        load_weights(i, i)
                    sp.wait_ge(s_scat, 16 * 2 * NT)
                    for i in range(2):
                        load_rows(i, i)
                    def turn(q, more):
                        for i in range(2):
                            sp.wait_ge(s_ec, at(q, 2, i + 1))
                            sp.wait_ge(s_clr, 1)
                            for k in range(3):
                                n = min(P, CAP - P * k)
                                sp.dma_start(eo_dram[bass.ds((q * 2 + i) * CAP + P * k, n), :], eo[0:n, i, k, :]).then_inc(s_es[i], 16)
                            if more:
                                load_weights(q * 2 + (2 + i), i)
                                load_rows(q * 2 + (2 + i), i)

                    with sp.Fori(0, 3) as q:
                        turn(q, True)
                    turn(3, False)
                    for i in range(2):
                        sp.wait_ge(s_es[i], 16 + 4 * 48)

                @block.gpsimd
                def _(pool):
                    link = Chain(pool, s_pch)
                    nc.gpsimd.memset(zeros[:, :, :], 0.0).then_inc(s_clr, 1)
                    link(nc.gpsimd.memset(neghalf[:, :], -0.5))
                    nc.gpsimd.tensor_tensor(sq[:, :, :], XN[:, :, :], XN[:, :, :], ALU.mult).then_inc(s_sq4, 1)
                    for e in range(NE):
                        nc.gpsimd.memset(base_row[:, :, e:e + 1], float(CAP * e)).then_inc(s_clr, 1)
                    nc.gpsimd.memset(ones[:, :], 1.0).then_inc(s_clr, 1)
                    pool.wait_ge(s_ms4, 1)
                    link(nc.gpsimd.tensor_scalar(cols[:, 0, :], cols[:, 0, :], 1.0 / D, 1.1920929e-07, ALU.mult, ALU.add))
                    nc.gpsimd.tensor_tensor(cols[:, 0, :], cols[:, 0, :], neghalf[:, :], ALU.pow).then_inc(s_rn4, 1)
                    pool.wait_ge(s_rows, 1)
                    pool.wait_ge(s_zf, 32)
                    for t in range(NT):
                        for i in range(2):
                            nc.gpsimd.indirect_dma_start(xg_dram[:, :], bass.IndirectOffsetOnAxis(ap=rows_u[i][:, t:t + 1], axis=0), XN[:, t, :], None,
                                                         bounds_check=ROWS - 1, oob_is_err=False).then_inc(s_scat, 16)

                @block.tensor
                def _(pe):
                    for s in (s_gu, s_od, s_tp, s_gu8, s_ed):
                        pe.sem_inc(s, LEAD)
                    mm = nc.tensor.matmul
                    pe.wait_ge(s_w4, 16 * 5)
                    for t in range(NT):
                        last = mm(r_bank[:, NE * t:NE * t + NE], XT[:, t // 4, P * (t % 4):P * (t % 4) + P], w_r[:, :], start=True, stop=True)
                    last.then_inc(s_lg4, 1)

                    def shared(c):
                        for f in range(8):
                            pe.wait_ge(s_hd, at(c, 8, f - 1))
                            mm(g_bank[f % 2][:, :], w_sg[:, P * f:P * f + P], XT[:, bass.ds(c, 1), :], start=True, stop=True)
                            mm(u_bank[f % 2][:, :], w_su[:, P * f:P * f + P], XT[:, bass.ds(c, 1), :], start=True, stop=True).then_inc(s_gu, 1)

                    def shared_down(c):
                        pe.wait_ge(s_hd, at(c, 8, 8))
                        pe.wait_ge(s_oc, at(c, 1, 0))
                        for t in range(4):
                            for f in range(8):
                                last = mm(o_bank[:, t, :], hid[:, 0, f, P * t:P * t + P], w_sd[:, f, :], start=(f == 0), stop=(f == 7))
                        last.then_inc(s_od, 1)

                    pe.wait_ge(s_clr, 10)
                    pe.wait_ge(s_sel, 1)
                    mm(x_bank[:, 0:P], below[:, :], sel[:, :, :].rearrange("p t e -> p (t e)"), start=True, stop=False)
                    mm(x_bank[:, 0:P], ones[:, :], cum[0][:, 0:NT, :].rearrange("p t e -> p (t e)"), start=False, stop=True).then_inc(s_rk, 1)
                    with pe.Fori(0, 4) as c:
                        shared(c)
                        shared_down(c)
                    pe.wait_ge(s_rows, 1)
                    with pe.Fori(0, 4) as q:
                        for i in range(2):
                            n = lambda per, k: at(q, 2 * per, i * per + k)
                            pe.wait_ge(s_xg[i], q * 48 + 48)
                            pe.wait_ge(s_tc, n(1, 0))
                            for k in range(3):
                                r = min(P, CAP - P * k)
                                last = nc.tensor.transpose(x_bank[:, P * k:P * k + r], xg[i][0:r, k, :], ident[0:r, 0:r])
                            last.then_inc(s_tp, 1)
                            pe.wait_ge(s_tc, n(1, 1))
                            pe.wait_ge(s_w8[i], q * 48 + 48)
                            for f in range(4):
                                pe.wait_ge(s_hd8, n(4, f - 1))
                                mm(g_bank[f % 2][:, 0:CAP], w_rg[i][:, P * f:P * f + P], xgT[:, i, :], start=True, stop=True)
                                mm(u_bank[f % 2][:, 0:CAP], w_ru[i][:, P * f:P * f + P], xgT[:, i, :], start=True, stop=True).then_inc(s_gu8, 1)
                            pe.wait_ge(s_hd8, n(4, 4))
                            pe.wait_ge(s_ec, n(1, 0))
                            for k in range(3):
                                r = min(P, CAP - P * k)
                                for f in range(4):
                                    last = mm(e_bank[0:r, k, :], hid[:, i, f, P * k:P * k + r], w_rd[i][:, f, :], start=(f == 0), stop=(f == 3))
                            last.then_inc(s_ed, 1)

                @block.scalar
                def _(act):
                    for s in (s_si, s_oc, s_tc, s_si8, s_ec):
                        act.sem_inc(s, LEAD)
                    for s in s_es:
                        act.sem_inc(s, 16)
                    act.wait_ge(s_x4, 1)
                    nc.scalar.activation(pr[:, :, :], pr[:, :, :], ACT.Exp).then_inc(s_e4, 1)
                    act.preload_act_table(ACT.Silu)
                    with act.Fori(0, 4) as c:
                        for f in range(8):
                            act.wait_ge(s_gu, at(c, 8, f + 1))
                            act.wait_ge(s_hd, at(c, 8, f - 1))
                            nc.scalar.activation(sil[:, f % 2, :], g_bank[f % 2][:, :], ACT.Silu).then_inc(s_si, 1)
                        act.wait_ge(s_od, at(c, 1, 1))
                        nc.scalar.activation(GATE[:, bass.ds(c * 4, 4), :], o_bank[:, :, :], ACT.Copy).then_inc(s_oc, 1)
                    with act.Fori(0, 4) as q:
                        for i in range(2):
                            n = lambda per, k: at(q, 2 * per, i * per + k)
                            act.wait_ge(s_tp, n(1, 1))
                            act.wait_ge(s_ed, n(1, -1))
                            nc.scalar.activation(xgT[:, i, :], x_bank[:, 0:CAP], ACT.Copy).then_inc(s_tc, 1)
                            for f in range(4):
                                act.wait_ge(s_gu8, n(4, f + 1))
                                act.wait_ge(s_hd8, n(4, f - 1))
                                nc.scalar.activation(sil[:, f % 2, 0:CAP], g_bank[f % 2][:, 0:CAP], ACT.Silu).then_inc(s_si8, 1)
                            act.wait_ge(s_ed, n(1, 1))
                            act.wait_ge(s_es[i], q * 48 + 16)
                            nc.scalar.activation(eo[:, i, 0:2, :], e_bank[:, 0:2, :], ACT.Copy)
                            nc.scalar.activation(eo[0:CAP - 2 * P, i, 2, :], e_bank[0:CAP - 2 * P, 2, :], ACT.Copy).then_inc(s_ec, 1)

                @block.vector
                def _(dve):
                    link = Chain(dve, s_dch)
                    for s in (s_hd, s_hd8):
                        dve.sem_inc(s, LEAD)
                    TT = nc.vector.tensor_tensor
                    wide = lambda col: col.unsqueeze(2).broadcast_to([P, NT, NE])
                    dve.wait_ge(s_sq4, 1)
                    nc.vector.tensor_reduce(cols[:, 0, :], sq[:, :, :], AX.X, ALU.add).then_inc(s_ms4, 1)
                    dve.wait_ge(s_rn4, 1)
                    dve.wait_ge(s_lg4, 1)
                    link(TT(pr[:, :, :], r_bank[:, 0:NT * NE].rearrange("p (t e) -> p t e", e=NE), wide(cols[:, 0, :]), ALU.mult))
                    link(nc.vector.tensor_reduce(cols[:, 1, :], pr[:, :, :], AX.X, ALU.max))
                    TT(pr[:, :, :], pr[:, :, :], wide(cols[:, 1, :]), ALU.subtract).then_inc(s_x4, 1)
                    dve.wait_ge(s_e4, 1)
                    link(nc.vector.tensor_reduce(cols[:, 2, :], pr[:, :, :], AX.X, ALU.add))
                    link(nc.vector.reciprocal(cols[:, 2, :], cols[:, 2, :]))
                    link(TT(pr[:, :, :], pr[:, :, :], wide(cols[:, 2, :]), ALU.mult))
                    for i, src in enumerate((pr, p2)):
                        link(nc.vector.tensor_reduce(cols[:, 3 + i, :], src[:, :, :], AX.X, ALU.max))
                        link(TT(cand[:, :, :], src[:, :, :], wide(cols[:, 3 + i, :]), ALU.is_ge))
                        link(TT(cand[:, :, :], cand[:, :, :], rank_desc[:, :, :], ALU.mult))
                        link(nc.vector.tensor_reduce(cols[:, 5, :], cand[:, :, :], AX.X, ALU.max))
                        link(TT(oh[i][:, :, :], cand[:, :, :], wide(cols[:, 5, :]), ALU.is_equal))
                        if i == 0:
                            link(nc.vector.scalar_tensor_tensor(p2[:, :, :], oh[0][:, :, :], -2.0, pr[:, :, :], ALU.mult, ALU.add))
                    link(TT(cols[:, 6, :], cols[:, 3, :], cols[:, 4, :], ALU.add))
                    link(nc.vector.reciprocal(cols[:, 6, :], cols[:, 6, :]))
                    link(TT(cols[:, 3:5, :], cols[:, 3:5, :], cols[:, 6, :].unsqueeze(1).broadcast_to([P, 2, NT]), ALU.mult))
                    link(TT(sel[:, :, :], oh[0][:, :, :], oh[1][:, :, :], ALU.add))
                    for c in range(2):
                        link(nc.vector.memset(cum[c][:, :, :], 0.0))
                    link(nc.vector.tensor_copy(cum[0][:, 1:NT + 1, :], sel[:, :, :]))
                    for n, step4 in enumerate((1, 2, 4, 8)):
                        a, z = cum[n % 2], cum[(n + 1) % 2]
                        link(nc.vector.tensor_copy(z[:, 0:step4, :], a[:, 0:step4, :]))
                        link(TT(z[:, step4:NT + 1, :], a[:, step4:NT + 1, :], a[:, 0:NT + 1 - step4, :], ALU.add), s_sel if n == 3 else None)

                    dve.wait_ge(s_rk, 1)
                    dve.wait_ge(s_clr, 10)
                    rk = x_bank[:, 0:P].rearrange("p (t e) -> p t e", e=NE)
                    link(nc.vector.tensor_scalar(kept[:, :, :], rk, float(CAP), None, ALU.is_lt))
                    link(TT(row[:, :, :], rk, base_row[:, :, :], ALU.add))
                    link(nc.vector.tensor_scalar(cand[:, :, :], kept[:, :, :], -FAR, FAR, ALU.mult, ALU.add))
                    link(TT(row[:, :, :], row[:, :, :], cand[:, :, :], ALU.add))
                    for i in range(2):
                        link(TT(cand[:, :, :], oh[i][:, :, :], row[:, :, :], ALU.mult))
                        link(nc.vector.tensor_reduce(cols[:, 7, :], cand[:, :, :], AX.X, ALU.add))
                        link(nc.vector.tensor_copy(rows_u[i][:, :], cols[:, 7, :]))
                        link(TT(cand[:, :, :], oh[i][:, :, :], kept[:, :, :], ALU.mult))
                        link(nc.vector.tensor_reduce(cols[:, 8 + i, :], cand[:, :, :], AX.X, ALU.add))
                    link(TT(share[:, :, :], cols[:, 3:5, :], cols[:, 8:10, :], ALU.mult), s_rows)

                    def shared(c):
                        for f in range(8):
                            dve.wait_ge(s_si, at(c, 8, f + 1))
                            if f == 0:
                                dve.wait_ge(s_od, at(c, 1, 0))
                            TT(hid[:, 0, f, :], sil[:, f % 2, :], u_bank[f % 2][:, :], ALU.mult).then_inc(s_hd, 1)

                    with dve.Fori(0, 4) as c:
                        shared(c)
                    with dve.Fori(0, 4) as q:
                        for i in range(2):
                            n = lambda per, k: at(q, 2 * per, i * per + k)
                            for f in range(4):
                                dve.wait_ge(s_si8, n(4, f + 1))
                                if f == 0:
                                    dve.wait_ge(s_ed, n(1, -1))
                                TT(hid[:, i, f, 0:CAP], sil[:, f % 2, 0:CAP], u_bank[f % 2][:, 0:CAP], ALU.mult).then_inc(s_hd8, 1)
        keepx.close()
        st5 = ExitStack()
        with st5:
            NB, GR, KS, UN = B, 8, 4, 32
            DR, XR, HR = 8, 4, 4
            slot_bank = [st5.enter_context(nc.psum_tensor(f"slot_bank{i}", [P, 512], fp32)) for i in range(4)]
            du_bank = [st5.enter_context(nc.psum_tensor(f"du_bank{i}", [P, 512], fp32)) for i in range(2)]
            dt_dram = nc.dram_tensor("dt_turn", [2, 256, 512], fp32).ap()
            bc_dram = nc.dram_tensor("bc_turn", [2, 32, 512], fp32).ap()
            w_in = sb(st5, "w_in", [P, 512])
            conv_row = sb(st5, "conv_row", [P, 4, 256])
            w_tap = sb(st5, "w_tap", [P, 4, 256])
            w_xp = sb(st5, "w_xp", [P, 2, 40])
            w_dt = sb(st5, "w_dt", [40, 256])
            pre_cols = sb(st5, "pre_cols", [P, 4])
            w_out = sb(st5, "w_out", [P, 2, D])
            d_col = sb(st5, "d_col", [P, 2])
            a_all = sb(st5, "a_all", [P, 4, UN])
            a_cur = sb(st5, "a_cur", [P, UN])
            spread = sb(st5, "spread_sb", [P, 4, P])
            fold = sb(st5, "fold_sb", [P, 32])
            bc = sb(st5, "bc", [P, 2, 8, 512])
            dtr = sb(st5, "dtr", [P, 2, GR, 512])
            xc = sb(st5, "xc", [P, 2, 2, 512])
            zs = sb(st5, "zs", [P, 2, 2, 512])
            du = sb(st5, "du", [P, 2, 2, 512])
            dt = sb(st5, "dt", [P, 2, 512])
            spa = sb(st5, "spa", [P, 2, 512])
            spr = sb(st5, "spr", [P, 2, 512])
            dbc = sb(st5, "dbc", [40, 512])
            dec = sb(st5, "decay", [P, DR, 512])
            dbx = sb(st5, "dbx", [P, XR, 512])
            hs = sb(st5, "hs", [P, HR, 512])
            hc = sb(st5, "hc", [P, 16, 512])
            back = [hc[:, 4 * i:4 * i + 4, :].rearrange("p a (b d) -> p (a b) d", d=D) for i in range(2)]
            yv = sb(st5, "yv5", [P, 2, 512])

            sem = lambda name: st5.enter_context(nc.semaphore(name))
            s_cst, s_wpre, s_wpost, s_zero, s_neg = map(sem, ("consts5", "pre_weights", "post_weights", "w_dt_cleared", "a_steps"))
            s_slot, s_fA, s_fV = map(sem, ("slot_written", "slot_left_by_scalar", "slot_left_by_vector"))
            s_du, s_dec, s_bx, s_sc, s_hc, s_yr = map(sem, ("du_spread", "decay_ready", "dbx_ready", "scan_done", "hc_ready", "round_summed"))
            s_win, s_wc = sem("in_weights"), sem("tap_weights")
            s_gz, s_gath, s_fin = map(sem, ("rows_cleared5", "rows_back", "mixture_steps"))
            s_xc, s_ln, s_dt, s_dun, s_yd, s_yv, s_ac = map(sem, ("xc_ready", "softplus_log", "dt_ready", "du_ready", "y_with_d", "yv_ready", "a_of_layer"))
            s_dtr = [sem(f"dt_spread{i}") for i in range(2)]
            s_bc = [sem(f"bc_spread{i}") for i in range(2)]
            s_dst, s_bst = sem("dt_stored"), sem("bc_stored")
            s_spx = sem("softplus_exp")

            ACT_AT = {"out": 9, "silus": 14, "dbc": 16, "softplus": 18}
            DVE_AT = {"y1": 5, "dt": 19, "du": 21, "y0": 28}
            LEAD = 64
            SCALAR, VECTOR = s_fA, s_fV
            PRE = [(name, SCALAR) for name in ("xi0", "xi1", "z0", "z1", "xp", "dt0", "dt1", "out")]
            order = []
            for b in range(NB):
                if b:
                    order.append(("y1", b - 1, VECTOR))
                order += [("xi0", b, SCALAR), ("xi1", b, SCALAR)]
                if b:
                    order.append(("out", b - 1, SCALAR))
                order += [("z0", b, SCALAR), ("z1", b, SCALAR), ("xp", b, SCALAR), ("dt0", b, SCALAR), ("dt1", b, SCALAR), ("y0", b, VECTOR)]
            order += [("y1", NB - 1, VECTOR), ("out", NB - 1, SCALAR)]
            place = {(name, b): n for n, (name, b, _) in enumerate(order)}
            left = lambda n, who: sum(1 for x in order[:n] if x[2] is who)
            per = {who: left(len(order), who) for who in (SCALAR, VECTOR)}
            assert len(order) % 4 == 0
            assert place["out", NB - 1] % 4 == (len(PRE) - 1) % 4
            pre_left = {SCALAR: len(PRE), VECTOR: 1}
            written_before = lambda n: sum(1 for x in order[:n] if x[0][0] != "y")

            class Slot:

                def __init__(self, name, b, l):
                    self.l = l
                    if l is None:
                        self.n = [x[0] for x in PRE].index(name)
                        self.who = PRE[self.n][1]
                    else:
                        self.n = place[name, b]
                        self.who = order[self.n][2]
                    self.bank = slot_bank[self.n % 4]

                def written(self):
                    if self.l is None:
                        return LEAD + self.n + 1
                    return self.l * written_before(len(order)) + (LEAD + len(PRE) + written_before(self.n + 1))

                def free(self, pe):
                    if self.l is None:
                        if self.n >= 4:
                            who = PRE[self.n - 4][1]
                            pe.wait_ge(who, LEAD + sum(1 for x in PRE[:self.n - 3] if x[1] is who))
                        return
                    m = self.n - 4
                    who = order[m][2]
                    count = left(m + 1, who) if m >= 0 else left(len(order) + m + 1, who) - per[who]
                    pe.wait_ge(who, self.l * per[who] + (LEAD + pre_left[who] + count))

                def left_at(self):
                    if self.l is None:
                        return LEAD + sum(1 for x in PRE[:self.n + 1] if x[1] is self.who)
                    return self.l * per[self.who] + (LEAD + pre_left[self.who] + left(self.n + 1, self.who))

            at = lambda l, b, per_turn, k: (0 if l is None else l) * (4 * per_turn) + (LEAD + per_turn * b + k)

            with nc.Block() as block:
                loaded = lambda l, n: l * 128 + 64 * (1 + n // 2)
                stored = lambda l, n: l * 64 + 16 * (n + 1)
                consts = [(spread[:, :, :], A["spread"]), (fold[:, :], A["fold"]), (a_all[:, :, :], A["a_log"])]

                @block.sync
                def _(sp):
                    def load_in(l):
                        one = lambda x: x[bass.ds(l, 1)]
                        sp.dma_start(w_in[:, :], one(A["w_in"]).rearrange("o p e -> p (o e)")).then_inc(s_win, 16)
                        sp.dma_start(conv_row[:, :, :], one(A["conv_row"]).broadcast_to([P, 4, 256])).then_inc(s_win, 16)

                    def load_pre(l):
                        one = lambda x: x[bass.ds(l, 1)]
                        sp.dma_start(w_xp[:, :, :], one(A["w_xp"]).rearrange("o p k e -> p (o k) e")).then_inc(s_wpre, 16)
                        sp.dma_start(w_dt[0:8, :], one(A["w_dt"]).rearrange("o p e -> p (o e)")).then_inc(s_wpre, 16)
                        sp.dma_start(pre_cols[:, :], one(A["pre_cols"]).rearrange("o p e -> p (o e)")).then_inc(s_wpre, 16)

                    def load_post(l):
                        one = lambda x: x[bass.ds(l, 1)]
                        sp.dma_start(w_out[:, :, :], one(A["w_out"]).rearrange("o p k e -> p (o k) e")).then_inc(s_wpost, 16)
                        sp.dma_start(d_col[:, :], one(A["d_col"]).rearrange("o p e -> p (o e)")).then_inc(s_wpost, 16)

                    def spread_dt(l, b, n):
                        sp.wait_ge(s_dt, at(l, n, 2, 2))
                        sp.dma_start(dt_dram[n % 2].rearrange("(h p) t -> p h t", p=P), dt[:, :, :]).then_inc(s_dst, 16)
                        sp.wait_ge(s_dst, stored(l, n))
                        for s in range(4):
                            sp.dma_start(dtr[32 * s:32 * s + 32, n % 2, :, :], dt_dram[n % 2].rearrange("(g c) t -> c g t", c=32)).then_inc(s_dtr[n % 2], 16)

                    def spread_bc(l, b, n):
                        sp.wait_ge(SCALAR, Slot("xp", b, l).left_at())
                        sp.dma_start(bc_dram[n % 2], dbc[8:40, :]).then_inc(s_bst, 16)
                        sp.wait_ge(s_bst, stored(0 if l is None else l, n))
                        for s in range(4):
                            sp.dma_start(bc[32 * s:32 * s + 32, n % 2, :, :],
                                         bc_dram[n % 2].rearrange("(i s) t -> s i t", s=4)[s:s + 1].broadcast_to([32, 8, 512])).then_inc(s_bc[n % 2], 16)

                    load_in(0)
                    for dst, src in consts:
                        sp.dma_start(dst, src).then_inc(s_cst, 16)
                    sp.wait_ge(s_zero, 1)
                    load_pre(0)
                    spread_bc(None, None, 0)
                    spread_dt(0, None, 0)
                    with sp.Fori(0, 4) as l:
                        for b in range(NB):
                            if b == 0:
                                sp.wait_ge(s_slot, Slot("out", NB - 1, l - 1).written())
                                sp.wait_ge(s_zero, 1)
                                load_post(l)
                            if b == 2:
                                sp.wait_ge(s_slot, Slot("z1", b, l).written())
                                sp.wait_ge(s_zero, 1)
                                load_in(l + 1)
                            if b == 3:
                                load_pre(l + 1)
                            spread_bc(l, b, b + 1)
                            spread_dt(l, b, b + 1)

                @block.gpsimd
                def _(pool):
                    nc.gpsimd.memset(w_dt[:, :], 0.0).then_inc(s_zero, 1)
                    pool.sem_inc(s_hc, LEAD)

                    def make_tap(tap):
                        nc.gpsimd.tensor_tensor(w_tap[:, tap, :], w_in[:, 0:256], conv_row[:, tap, :], ALU.mult).then_inc(s_wc, 1)

                    for i in range(2):
                        nc.gpsimd.memset(back[i][:, :, :], 0.0).then_inc(s_gz, 1)
                    pool.wait_ge(s_win, 32)
                    for tap in range(4):
                        make_tap(tap)
                    pool.wait_ge(s_gz, 2)
                    for t in range(NT):
                        for i in range(2):
                            nc.gpsimd.indirect_dma_start(back[i][:, t, :], None, eo_dram[:, :], bass.IndirectOffsetOnAxis(ap=rows_u[i][:, t:t + 1], axis=0),
                                                         bounds_check=ROWS - 1, oob_is_err=False).then_inc(s_gath, 16)
                    pool.wait_ge(s_fin, 4)
                    with pool.Fori(0, 4) as l:
                        for b in range(NB):
                            for u in range(UN):
                                k = u % 4
                                pool.wait_ge(s_sc, at(l, b, UN, u + 1))
                                if u % 16 < 4:
                                    pool.wait_ge(s_yr, at(l, b, 8, 4 * (u // 16) - 3 + k))
                                if u == 0:
                                    pool.wait_ge(s_bc[b % 2], loaded(l, b))
                                nc.gpsimd.tensor_tensor(hc[:, u % 16, :], hs[:, u % HR, :], bc[:, b % 2, 4 + k, :], ALU.mult).then_inc(s_hc, 1)
                                if b == 2 and u in (17, 20, 23, 26):
                                    if u == 17:
                                        pool.wait_ge(s_win, l * 32 + 64)
                                    make_tap((u - 17) // 3)

                @block.tensor
                def _(pe):
                    for s in (s_slot, s_du, s_yr):
                        pe.sem_inc(s, LEAD)
                    mm = nc.tensor.matmul

                    def in_proj(l, b, n, names):
                        for name in names:
                            sl = Slot(name, b, l)
                            sl.free(pe)
                            if name == "xi0":
                                if l is not None:
                                    pe.wait_ge(SCALAR, Slot("out", n % 4, l if n == 4 else l - 1).left_at())
                                pe.wait_ge(s_wc, 4 if l is None else l * 4 + 4 * (1 + n // 4))
                            c = P * int(name[-1])
                            if name[0] == "z":
                                mm(sl.bank[:, :], w_in[:, 256 + c:256 + c + P], XT[:, n % 4, :], start=True, stop=True).then_inc(s_slot, 1)
                                continue
                            for d in range(4):
                                last = mm(sl.bank[:, d:512], w_tap[:, 3 - d, c:c + P], XT[:, n % 4, 0:512 - d], start=(d == 0), stop=(d == 3))
                            last.then_inc(s_slot, 1)

                    def x_proj(l, b, n):
                        sl = Slot("xp", b, l)
                        sl.free(pe)
                        pe.wait_ge(s_xc, at(l, n, 2, 2))
                        pe.wait_ge(s_wpre, 48 if l is None else l * 48 + 48 * (1 + n // 4))
                        for h in range(2):
                            last = mm(sl.bank[0:40, :], w_xp[:, h, :], xc[:, n % 2, h, :], start=(h == 0), stop=(h == 1))
                        last.then_inc(s_slot, 1)

                    def dt_proj(l, b):
                        pe.wait_ge(SCALAR, Slot("xp", b, l).left_at())
                        for h in range(2):
                            sl = Slot(f"dt{h}", b, l)
                            sl.free(pe)
                            mm(sl.bank[:, :], w_dt[:, P * h:P * h + P], dbc[:, :], start=True, stop=True).then_inc(s_slot, 1)

                    def spread_du(l, b, g, n):
                        if g == 0:
                            pe.wait_ge(s_dun, at(l, n, 2, 2))
                        pe.wait_ge(s_bx, at(l, n, UN, 4 * g - 4))
                        mm(du_bank[g % 2][:, :], spread[:, g % 4, :], du[:, n % 2, g // 4, :], start=True, stop=True).then_inc(s_du, 1)

                    def sum_states(l, b, half, in_turn):
                        sl = Slot(f"y{half}", b, l)
                        sl.free(pe)
                        for k in range(KS):
                            pe.wait_ge(s_hc, at(l, b, UN, 16 * half + 13 + k))
                            for j in range(4):
                                last = mm(sl.bank[32 * j:32 * j + 32, :], fold[:, :], hc[:, 4 * j + k, :], start=(k == 0), stop=(k == KS - 1),
                                          tile_position=(0, 32 * j), skip_group_check=True)
                            last.then_inc(s_yr, 1)

                    def out_proj(l, b):
                        sl = Slot("out", b, l)
                        sl.free(pe)
                        pe.wait_ge(s_yv, at(l, b, 2, 2))
                        pe.wait_ge(s_wpost, l * 32 + 32)
                        for h in range(2):
                            last = mm(sl.bank[:, :], w_out[:, h, :], yv[:, h, :], start=(h == 0), stop=(h == 1))
                        last.then_inc(s_slot, 1)

                    in_proj(None, None, 0, ("xi0", "xi1", "z0", "z1"))
                    x_proj(None, None, 0)
                    dt_proj(None, None)
                    sl = Slot("out", None, None)
                    sl.free(pe)
                    mm(sl.bank[:, :], ident[:, :], XT[:, NB - 1, :], start=True, stop=True).then_inc(s_slot, 1)
                    pe.wait_ge(SCALAR, LEAD + pre_left[SCALAR] - 1)
                    pe.wait_ge(s_cst, 16 * len(consts))
                    spread_du(0, None, 0, 0)
                    spread_du(0, None, 1, 0)
                    with pe.Fori(0, 4) as l:
                        for b in range(NB):
                            if b:
                                sum_states(l, b - 1, 1, b)
                            in_proj(l, b, b + 1, ("xi0",))
                            spread_du(l, b, 2, b)
                            in_proj(l, b, b + 1, ("xi1",))
                            if b:
                                out_proj(l, b - 1)
                            in_proj(l, b, b + 1, ("z0",))
                            spread_du(l, b, 3, b)
                            in_proj(l, b, b + 1, ("z1",))
                            x_proj(l, b, b + 1)
                            spread_du(l, b, 4, b)
                            dt_proj(l, b)
                            sum_states(l, b, 0, b)
                            spread_du(l, b, 5, b)
                            spread_du(l, b, 6, b)
                            spread_du(l, b, 7, b)
                            spread_du(l, b, 0, b + 1)
                            spread_du(l, b, 1, b + 1)
                        sum_states(l, NB - 1, 1, NB)
                        out_proj(l, NB - 1)

                @block.scalar
                def _(act):
                    for s in (s_fA, s_dec, s_xc, s_ln, s_spx):
                        act.sem_inc(s, LEAD)
                    act.wait_ge(s_cst, 16 * len(consts))
                    act.preload_act_table_set("natural_log_exp_and_others")
                    flat = a_all[:, :, :].rearrange("p l u -> p (l u)")
                    nc.scalar.activation(flat, flat, ACT.Exp).then_inc(s_neg, 1)
                    act.wait_ge(s_neg, 1)
                    nc.scalar.activation(flat, flat, ACT.Copy, scale=-1.0).then_inc(s_neg, 1)
                    act.wait_ge(s_neg, 2)

                    def silus(l, b, n):
                        if l is not None:
                            act.wait_ge(s_yv, at(l, b, 2, 0))
                        act.wait_ge(s_wpre, 48 if l is None else l * 48 + 48 * (1 + n // 4))
                        for h in range(2):
                            sl = Slot(f"xi{h}", b, l)
                            act.wait_ge(s_slot, sl.written())
                            nc.scalar.activation(xc[:, n % 2, h, :], sl.bank[:, :], ACT.Silu, bias=pre_cols[:, h:h + 1]).then_inc(s_xc, 1)
                        act.wait_ge(s_xc, at(l, n, 2, 2))
                        act.sem_inc(SCALAR, 2)
                        if b:
                            copy_out(l, b - 1)
                        for h in range(2):
                            sl = Slot(f"z{h}", b, l)
                            act.wait_ge(s_slot, sl.written())
                            nc.scalar.activation(zs[:, n % 2, h, :], sl.bank[:, :], ACT.Silu).then_inc(SCALAR, 1)

                    def copy_dbc(l, b):
                        sl = Slot("xp", b, l)
                        if l is not None:
                            act.wait_ge(s_bst, stored(l, b))
                            act.wait_ge(s_hc, at(l, b, UN, 0))
                        act.wait_ge(s_slot, sl.written())
                        nc.scalar.activation(dbc[:, :], sl.bank[0:40, :], ACT.Copy).then_inc(SCALAR, 1)

                    def softplus(l, b, n):
                        act.wait_ge(s_dt, at(l, n, 2, 0))
                        for h in range(2):
                            sl = Slot(f"dt{h}", b, l)
                            act.wait_ge(s_slot, sl.written())
                            bias = pre_cols[:, 2 + h:3 + h]
                            nc.scalar.activation(spa[:, h, :], sl.bank[:, :], ACT.Abs, bias=bias).then_inc(s_spx, 1)
                            nc.scalar.activation(spr[:, h, :], sl.bank[:, :], ACT.Relu, bias=bias).then_inc(SCALAR, 1)
                        act.wait_ge(s_spx, at(l, n, 3, 2))
                        nc.scalar.activation(spa[:, :, :], spa[:, :, :], ACT.Exp, scale=-1.0).then_inc(s_spx, 1)
                        act.wait_ge(s_spx, at(l, n, 3, 3))
                        nc.scalar.activation(spa[:, :, :], spa[:, :, :], ACT.Ln, bias=1.0).then_inc(s_ln, 1)

                    def copy_out(l, b):
                        sl = Slot("out", b, l)
                        act.wait_ge(s_slot, sl.written())
                        nc.scalar.activation(XT[:, b, :], sl.bank[:, :], ACT.Copy).then_inc(SCALAR, 1)

                    silus(None, None, 0)
                    act.preload_act_table_set("natural_log_exp_and_others")
                    copy_dbc(None, None)
                    softplus(None, None, 0)
                    with act.Fori(0, 4) as l:
                        act.wait_ge(s_dec, at(l, 0, UN, 0))
                        act.wait_ge(s_cst, 16 * len(consts))
                        nc.scalar.activation(a_cur[:, :], a_all[:, bass.ds(l, 1), :].rearrange("p l u -> p (l u)"), ACT.Copy).then_inc(s_ac, 1)
                        act.wait_ge(s_ac, l + 1)
                        for b in range(NB):
                            for u in range(UN):
                                if u == 0:
                                    act.wait_ge(s_dtr[b % 2], loaded(l, b))
                                act.wait_ge(s_sc, at(l, b, UN, u - DR + 1))
                                nc.scalar.activation(dec[:, u % DR, :], dtr[:, b % 2, u // 4, :], ACT.Exp, scale=a_cur[:, u:u + 1]).then_inc(s_dec, 1)
                                if b == 0 and u == ACT_AT["out"]:
                                    copy_out(l - 1, NB - 1)
                                if u == ACT_AT["silus"]:
                                    silus(l, b, b + 1)
                                    act.preload_act_table_set("natural_log_exp_and_others")
                                if u == ACT_AT["dbc"]:
                                    copy_dbc(l, b)
                                if u == ACT_AT["softplus"]:
                                    softplus(l, b, b + 1)
                    copy_out(NB - 1, NB - 1)

                @block.vector
                def _(dve):
                    for s in (s_fV, s_bx, s_sc, s_dt, s_dun, s_yd, s_yv):
                        dve.sem_inc(s, LEAD)
                    TT = nc.vector.tensor_tensor

                    def make_dt(l, b, n, h):
                        if h == 0:
                            dve.wait_ge(s_ln, at(l, n, 1, 1))
                            dve.wait_ge(SCALAR, Slot("dt1", b, l).left_at())
                            if l is not None:
                                dve.wait_ge(s_dst, stored(l, n - 1))
                        TT(dt[:, h, :], spa[:, h, :], spr[:, h, :], ALU.add).then_inc(s_dt, 1)

                    def make_du(l, b, n, h):
                        dve.wait_ge(s_dt, at(l, n, 2, h + 1))
                        dve.wait_ge(s_xc, at(l, n, 2, 2))
                        TT(du[:, n % 2, h, :], dt[:, h, :], xc[:, n % 2, h, :], ALU.mult).then_inc(s_dun, 1)

                    def add_d(l, b, half):
                        sl = Slot(f"y{half}", b, l)
                        dve.wait_ge(s_yr, at(l, b, 8, 4 * half + 4))
                        dve.wait_ge(s_wpost, l * 32 + 32)
                        dve.wait_ge(s_yd, at(l, b, 2, half))
                        if half == 0:
                            dve.wait_ge(s_slot, (Slot("out", b - 1, l) if b else Slot("out", NB - 1, l - 1)).written())
                        nc.vector.scalar_tensor_tensor(yv[:, half, :], xc[:, b % 2, half, :], d_col[:, half:half + 1], sl.bank[:, :],
                                                       ALU.mult, ALU.add).then_inc(s_yd, 1)

                    def gate_y(l, b, half):
                        dve.wait_ge(s_yd, at(l, b, 2, half + 1))
                        dve.sem_inc(VECTOR, 1)
                        TT(yv[:, half, :], yv[:, half, :], zs[:, b % 2, half, :], ALU.mult).then_inc(s_yv, 1)

                    def input_of(l, b, u):
                        g, k = u // 4, u % 4
                        if k == 0:
                            dve.wait_ge(s_du, at(l, b, 8, g + 1))
                        if u == 0:
                            dve.wait_ge(s_bc[b % 2], loaded(l, b))
                        dve.wait_ge(s_sc, at(l, b, UN, u - XR + 1))
                        TT(dbx[:, u % XR, :], du_bank[g % 2][:, :], bc[:, b % 2, k, :], ALU.mult).then_inc(s_bx, 1)

                    for h in range(2):
                        make_dt(None, None, 0, h)
                    for h in range(2):
                        make_du(None, None, 0, h)
                    dve.sem_inc(VECTOR, 1)
                    dve.wait_ge(s_gath, 16 * 2 * NT)
                    for i in range(2):
                        weight = share[:, i, :].unsqueeze(2).broadcast_to([P, NT, D])
                        TT(back[i][:, :, :], back[i][:, :, :], weight, ALU.mult).then_inc(s_fin, 1)
                    for i in range(2):
                        dve.wait_ge(s_fin, 2 + i)
                        TT(GATE[:, :, :], GATE[:, :, :], back[i][:, :, :], ALU.add).then_inc(s_fin, 1)
                    with dve.Fori(0, 4) as l:
                        for b in range(NB):
                            input_of(l, b, 0)
                            for u in range(UN):
                                if u + 1 < UN:
                                    input_of(l, b, u + 1)
                                for h in range(2):
                                    if u == DVE_AT["dt"] + h:
                                        make_dt(l, b, b + 1, h)
                                    if u == DVE_AT["du"] + h:
                                        make_du(l, b, b + 1, h)
                                if u == DVE_AT["y0"]:
                                    add_d(l, b, 0)
                                if u == DVE_AT["y0"] + 2:
                                    gate_y(l, b, 0)
                                if b and u == DVE_AT["y1"]:
                                    add_d(l, b - 1, 1)
                                if b and u == DVE_AT["y1"] + 2:
                                    gate_y(l, b - 1, 1)
                                dve.wait_ge(s_dec, at(l, b, UN, u + 1))
                                dve.wait_ge(s_hc, at(l, b, UN, u - HR + 1))
                                dve.wait_ge(s_bx, at(l, b, UN, u + 1))
                                nc.vector.tensor_tensor_scan(hs[:, u % HR, :], dec[:, u % DR, :], dbx[:, u % XR, :], 0.0, ALU.mult, ALU.add).then_inc(s_sc, 1)
                        add_d(l, NB - 1, 1)
                        gate_y(l, NB - 1, 1)
        st6 = ExitStack()
        with st6:
            X = sb(st6, "X6", [P, NT, D])
            bank = [st6.enter_context(nc.psum_tensor(f"s6_bank{i}", [P, 4, D], fp32)) for i in range(4)]
            sem = lambda name: st6.enter_context(nc.semaphore(name))
            s_g6 = sem("gate_ready")
            s_t6, s_r6, s_o6 = map(sem, ("s_by_token", "x_steps", "x_transfers"))
            with nc.Block() as block:
                @block.tensor
                def _(pe):
                    for b in range(B):
                        for t in range(4):
                            last = nc.tensor.transpose(bank[b][:, t, :], XT[:, b, P * t:P * t + P], ident[:, :])
                        last.then_inc(s_t6, 1)

                @block.scalar
                def _(act):
                    nc.scalar.activation(GATE[:, :, :], GATE[:, :, :], ACT.Silu).then_inc(s_g6, 1)

                @block.vector
                def _(dve):
                    for b in range(B):
                        tl = slice(4 * b, 4 * b + 4)
                        dve.wait_ge(s_t6, b + 1)
                        dve.wait_ge(s_g6, 1)
                        nc.vector.tensor_tensor(GATE[:, tl, :], bank[b][:, :, :], GATE[:, tl, :], ALU.mult).then_inc(s_r6, 1)
                        dve.wait_ge(s_r6, 2 * b + 1)
                        dve.wait_ge(s_o6, 16)
                        nc.vector.tensor_tensor(X[:, tl, :], X[:, tl, :], GATE[:, tl, :], ALU.add).then_inc(s_r6, 1)

                @block.sync
                def _(sp):
                    sp.dma_start(X[:, :, :], x_dram).then_inc(s_o6, 16)
                    for b in range(B):
                        sp.wait_ge(s_r6, 2 * b + 2)
                        sp.wait_ge(s_o6, 16 + 16 * b)
                        sp.dma_start(out[b].rearrange("(k p) d -> p k d", p=P), X[:, 4 * b:4 * b + 4, :]).then_inc(s_o6, 16)
                    sp.wait_ge(s_o6, 16 + 16 * B)


def laid_out(i):
    import numpy as np

    f = lambda name: np.asarray(i[name])
    row = lambda name: np.ascontiguousarray(f(name).reshape(-1))
    t2 = lambda a: np.ascontiguousarray(np.swapaxes(a, -1, -2))
    L = 4
    wrap = lambda a, n=1: np.concatenate([a, a[:n]], 0)
    part = np.arange(128)
    spread = np.stack([(np.arange(128)[:, None] == 32 * j + part[None] % 32) for j in range(4)], 1).astype(np.float32)
    a = {
        "x": f("L0_attn_x"),
        "w_att": np.concatenate([f("L0_attn_Wq").T, f("L0_attn_Wk").T, f("L0_attn_Wv").T], 1),
        "w_mha": t2(f("L0_ffn_Wqkv")), "b_mha": row("L0_ffn_bqkv"), "w_mo": t2(f("L0_ffn_Wo")), "b_mo": row("L0_ffn_bo"),
        "w_gate0": t2(f("L0_ffn_Wg")), "g1": row("L0_ffn_g1"), "be1": row("L0_ffn_be1"), "g2": row("L0_ffn_g2"), "be2": row("L0_ffn_be2"),
        "cos_head_delta": row("L0_attn_cos_head_delta"), "cos_raw": row("L0_attn_cos_logit_scale_raw"), "delta_gain": row("L0_attn_delta_gain"),
        "bo": row("L0_attn_bo"), "subln": row("L0_attn_subln_weight"), "wo_att": t2(f("L0_attn_Wo")),
        "lq1": row("L0_attn_lambda_q1"), "lk1": row("L0_attn_lambda_k1"), "lq2": row("L0_attn_lambda_q2"), "lk2": row("L0_attn_lambda_k2"),
        "w1": f("L0_ffn_W1"), "w2": f("L0_ffn_W2"), "b2": f("L0_ffn_b2"),
        "b1": t2(f("L0_ffn_b1").reshape(8, 4, 128)),
        "ident": np.eye(128, dtype=np.float32),
        "w_in": wrap(t2(f("L1_attn_in_proj_w"))),
        "w_xp": wrap(t2(f("L1_attn_x_proj_w")).reshape(L, 2, 128, 40).transpose(0, 2, 1, 3)),
        "w_dt": wrap(t2(f("L1_attn_dt_proj_w"))),
        "conv_row": wrap(t2(f("L1_attn_conv_w"))),
        "pre_cols": wrap(np.concatenate([t2(f("L1_attn_conv_b").reshape(L, 2, 128)), t2(f("L1_attn_dt_proj_b").reshape(L, 2, 128))], 2)),
        "w_out": t2(f("L1_attn_out_proj_w")).reshape(L, 2, 128, 128).transpose(0, 2, 1, 3),
        "d_col": t2(f("L1_attn_D").reshape(L, 2, 128)),
        "a_log": f("L1_attn_A_log").reshape(L, 8, 32, 4, 4).transpose(4, 2, 0, 1, 3).reshape(128, L, 32),
        "spread": spread, "fold": np.tile(np.eye(32, dtype=np.float32), (4, 1)),
        "w_router": t2(f("L1_ffn_router_w")), "below": np.triu(np.ones((128, 128), np.float32), 1),
        "w_sg": f("L1_ffn_sg"), "w_su": f("L1_ffn_su"), "w_sd": f("L1_ffn_sd").reshape(8, 128, 128).transpose(1, 0, 2),
        "w_rg": f("L1_ffn_rg"), "w_ru": f("L1_ffn_ru"), "w_rd": f("L1_ffn_rd"),
    }
    return {k: np.ascontiguousarray(v) for k, v in a.items()}


def kernel(**inputs):
    import concourse.bacc as _bacc
    from concourse.bass_utils import run_bass_kernel_spmd as _run

    nc = _bacc.Bacc("TRN2", target_bir_lowering=False, num_devices=1)
    arrays, aps = {}, {}
    for name, a in laid_out(inputs).items():
        arrays[f"in_{name}"] = a
        aps[name] = nc.dram_tensor(f"in_{name}", list(a.shape), mybir.dt.from_np(a.dtype), kind="ExternalInput").ap()
    out = nc.dram_tensor("out_x", [B, N, D], fp32, kind="ExternalOutput").ap()
    build_stages(nc, aps, out)
    r = _run(nc, [arrays], core_ids=[0])
    return r.results[0]["out_x"]
```

```python
import concourse.bass as bass
from concourse import mybir
from contextlib import ExitStack

fp32 = mybir.dt.float32
bf16 = mybir.dt.bfloat16
u32 = mybir.dt.uint32
ALU = mybir.AluOpType
ACT = mybir.ActivationFunctionType
AX = mybir.AxisListType

P = 128
B, N, D = 4, 512, 128
T = B * N
NT = T // P
NH = 8
NE = 8
EPS = 1e-5


class Chain:

    def __init__(self, engine, semaphore, start=0):
        self.engine, self.semaphore, self.done = engine, semaphore, start

    def __call__(self, instruction, then=None):
        self.done += 1
        instruction.then_inc(self.semaphore, 1)
        self.engine.wait_ge(self.semaphore, self.done)
        if then is not None:
            self.engine.sem_inc(then, 1)


def first_max(nc, link, lg, cand, lmax, source, rank_desc, onehot):
    link(nc.vector.tensor_copy(lg[:, :, :], source))
    link(nc.vector.tensor_reduce(lmax[:, :], lg[:, :, :], AX.X, ALU.max))
    link(nc.vector.tensor_tensor(cand[:, :, :], lg[:, :, :], lmax[:, :].unsqueeze(2).broadcast_to([P, NT, NE]), ALU.is_ge))
    link(nc.vector.tensor_tensor(cand[:, :, :], cand[:, :, :], rank_desc[:, :, :], ALU.mult))
    link(nc.vector.tensor_reduce(lmax[:, :], cand[:, :, :], AX.X, ALU.max))
    link(nc.vector.tensor_tensor(onehot[:, :, :], cand[:, :, :], lmax[:, :].unsqueeze(2).broadcast_to([P, NT, NE]), ALU.is_equal))




def build_stages(nc, A, out):
    keep = ExitStack()
    with keep:
        def sb(stack, name, shape, dtype=fp32):
            return stack.enter_context(nc.sbuf_tensor(name, shape, dtype))

        XT = sb(keep, "XT", [P, B, 512])
        ident = sb(keep, "ident_sb", [P, P])
        rank_desc = sb(keep, "rank_desc", [P, NT, NE])
        GATE = sb(keep, "GATE", [P, NT, D])
        rows_u = [sb(keep, f"rows_u{i}", [P, NT], u32) for i in range(2)]
        share = sb(keep, "share", [P, 2, NT])
        eo_dram = nc.dram_tensor("expert_outs", [NE * (5 * T // (4 * NE)), D], fp32).ap()
        w_in = sb(keep, "w_in", [P, 512])
        conv_row = sb(keep, "conv_row", [P, 4, 256])
        w_tap = sb(keep, "w_tap", [P, 4, 256])
        s_win, s_wc = (keep.enter_context(nc.semaphore(name)) for name in ("in_weights", "tap_weights"))
        x_dram = nc.dram_tensor("x_kept", [P, NT, D], fp32).ap()
        keepx = ExitStack()
        X = sb(keepx, "X", [P, NT, D])
        XN = sb(keepx, "XN", [P, NT, D])
        keep0 = ExitStack()
        with keep0:
            Y1 = sb(keep0, "Y1", [P, NT, D])
            Y1T = sb(keep0, "Y1T", [P, T])
            ACC = sb(keep0, "ACC", [P, NT, D])
            v_tok = sb(keep0, "v_tok", [P, NT, D])
            mask0 = sb(keep0, "mask0", [P, NT, NE])
            ybig = sb(keep0, "ybig", [P, NT, NH * 34])
            delta_gain = sb(keep0, "delta_gain_sb", [P, NH])
            neg_lam = sb(keep0, "neg_lam", [P, 1])
            subln = sb(keep0, "subln_sb", [P, 16])
            bo_row = sb(keep0, "bo_row", [P, D])
            g2_row = sb(keep0, "g2_row", [P, D])
            be2_row = sb(keep0, "be2_row", [P, D])
            wo_att = sb(keep0, "wo_att_sb", [P, D])
            row_u = sb(keep0, "row_u", [P, NT], u32)
            BLOCKS = 4 * (-(-(NT + NE - 1) // 4))
            AHEAD = 2
            yx_dram = nc.dram_tensor("block_rows", [(BLOCKS + AHEAD) * P, D], fp32).ap()
            yo_dram = nc.dram_tensor("block_outs", [BLOCKS * P, D], fp32).ap()
            qk_dram = nc.dram_tensor("qk_parts", [2, 3, P, T], bf16).ap()
            st1 = ExitStack()
            with st1:
                PR = 3
                psum = [st1.enter_context(nc.psum_tensor(f"s1_bank{i}", [P, 512], fp32)) for i in range(8)]
                w_att = sb(st1, "w_att", [P, 3 * D])
                w_mha = sb(st1, "w_mha", [P, 3 * D])
                w_mo = sb(st1, "w_mo", [P, D])
                w_gate = sb(st1, "w_gate", [P, NE])
                b_mha = sb(st1, "b_mha", [P, 3 * D])
                b_mo = sb(st1, "b_mo", [P, D])
                g1_row = sb(st1, "g1_row", [P, D])
                be1_row = sb(st1, "be1_row", [P, D])
                chd = sb(st1, "chd", [P, NH])
                craw = sb(st1, "craw", [P, 1])
                lam_in = sb(st1, "lam_in", [P, 4, 8])
                stats = sb(st1, "stats", [P, NT, 6])
                mv = sb(st1, "mv", [P, NT, 2])
                rstd = sb(st1, "rstd", [P, NT])
                neghalf = sb(st1, "neghalf", [P, 4])
                qkv = sb(st1, "qkv", [P, NT, 3 * D])
                sq = sb(st1, "sq", [P, 4, 2 * D])
                ss = sb(st1, "ss", [P, NT, 32])
                cosb = sb(st1, "cosb", [P, 16])
                xnT = sb(st1, "xnT", [P, T])
                parts = {(w, i): sb(st1, f"part_{w}{i}", [P, T], bf16) for w in "qk" for i in range(3)}
                rest = {w: sb(st1, f"rest_{w}", [P, 512]) for w in "qk"}
                prod = sb(st1, "prod", [P, PR, 4, D])
                att = sb(st1, "att", [P, 4, 4, 4, 4])
                amax = sb(st1, "amax", [P, 64])
                mo = sb(st1, "mo", [P, NT, D])
                mh = sb(st1, "mh", [P, NT, 3 * D])
                smalls = sb(st1, "smalls", [P, 64])
                lg, lgt = ss[:, :, 0:NE], ss[:, :, NE:2 * NE]
                lmax = amax[:, 0:NT]

                used1 = []

                def sem(name):
                    used1.append(nc.alloc_semaphore(name=name))
                    return used1[-1]

                s_x = [sem(f"x_loaded{b}") for b in range(B)]
                s_w = sem("weights_loaded")
                s_stat, s_rstd, s_xn, s_xnt_ps, s_xnt = map(sem, ("stats_ready", "rstd_ready", "xn_ready", "xnT_in_psum", "xnT_ready"))
                s_proj, s_qkv, s_mh = map(sem, ("proj_in_psum", "qkv_ready", "mha_in_ready"))
                s_sq, s_ss, s_rn, s_nrm, s_qkn = map(sem, ("squares_ready", "sumsq_ready", "sumsq_bounded", "norms_ready", "qk_normed"))
                s_qkt, s_hi, s_r1, s_mid, s_lo, s_qkst = map(sem, ("qkT_in_psum", "hi_ready", "rest_ready", "mid_ready", "lo_ready", "parts_stored"))
                s_cos, s_act, s_nh = map(sem, ("cos_steps", "act_steps", "neghalf_ready"))
                s_pr, s_sc, s_ex, s_at, s_pv, s_o = map(sem, ("qk_products", "scores_ready", "exps_ready", "att_ready", "pv_products", "mha_out"))
                s_ot_ps, s_ot, s_wo, s_y0, s_ys, s_yr, s_y1 = map(sem, ("oT_in_psum", "oT_ready", "wo_in_psum", "y_summed", "y_stats", "y_rstd", "y_normed"))
                s_yt_ps, s_yt, s_lgp, s_dch, s_pch, s_ach = map(sem, ("yT_in_psum", "yT_ready", "logits_in_psum", "vector_steps", "pool_steps", "scalar_steps"))
                s_pw = sem("weighted_on_vector")

                with nc.Block() as block:
                    loads = [(ident[:, :], A["ident"]), (w_att[:, :], A["w_att"]), (w_mha[:, :], A["w_mha"]), (w_mo[:, :], A["w_mo"]),
                             (w_gate[:, :], A["w_gate0"]), (b_mha[:, :], A["b_mha"].partition_broadcast(P)),
                             (b_mo[:, :], A["b_mo"].partition_broadcast(P)), (g1_row[:, :], A["g1"].partition_broadcast(P)),
                             (be1_row[:, :], A["be1"].partition_broadcast(P)), (chd[:, :], A["cos_head_delta"].partition_broadcast(P)),
                             (craw[:, :], A["cos_raw"].partition_broadcast(P)), (delta_gain[:, :], A["delta_gain"].partition_broadcast(P)),
                             (bo_row[:, :], A["bo"].partition_broadcast(P)), (subln[:, :], A["subln"].partition_broadcast(P)),
                             (g2_row[:, :], A["g2"].partition_broadcast(P)), (be2_row[:, :], A["be2"].partition_broadcast(P)),
                             (wo_att[:, :], A["wo_att"])]
                    loads += [(lam_in[:, i, :], A[n].partition_broadcast(P)) for i, n in enumerate(("lq1", "lk1", "lq2", "lk2"))]
                    ALL_W = 16 * len(loads)

                    on_pool = [u for u in range(16) if u % 3 != 2]

                    def weigh_values(engine, u, done):
                        nb, b1 = u // 4, u % 4
                        mt = mh[:, :, :].rearrange("p (b n) c -> p n b c", n=4)
                        for b2 in range(4):
                            last = engine.tensor_tensor(prod[:, u % PR, b2, :].rearrange("p (h d) -> p h d", d=32),
                                                        mt[:, nb, b2, 2 * D:3 * D].rearrange("p (h d) -> p h d", d=32),
                                                        att[:, nb, b1, b2, :].unsqueeze(2).broadcast_to([P, 4, 32]), ALU.mult)
                        last.then_inc(done, 1)

                    @block.sync
                    def _(sp):
                        for b in range(B):
                            sp.dma_start(X[:, 4 * b:4 * b + 4, :], A["x"][b].rearrange("(k p) d -> p k d", p=P)).then_inc(s_x[b], 16)
                        for dst, src in loads:
                            sp.dma_start(dst, src).then_inc(s_w, 16)
                        for b in range(B):
                            sp.wait_ge(s_mid, 2 * b + 2)
                            sp.wait_ge(s_lo, 2 * b + 2)
                            for n, w in enumerate("qk"):
                                for i in range(3):
                                    sp.dma_start(qk_dram[n, i, :, 512 * b:512 * b + 512], parts[w, i][:, 512 * b:512 * b + 512]).then_inc(s_qkst, 16)
                        sp.wait_ge(s_qkst, 16 * 6 * B)

                    @block.vector
                    def _(dve):
                        link = Chain(dve, s_dch)
                        nc.vector.memset(neghalf[:, :], -0.5).then_inc(s_nh, 1)
                        for b in range(B):
                            dve.wait_ge(s_x[b], 16)
                            for t in range(4 * b, 4 * b + 4):
                                last = nc.vector.bn_stats(stats[:, t, :], X[:, t, :])
                            link(last)
                            for t in range(4 * b, 4 * b + 4):
                                last = nc.vector.bn_aggr(mv[:, t, :], stats[:, t, :])
                            last.then_inc(s_stat, 1)
                        for b in range(B):
                            dve.wait_ge(s_rstd, b + 1)
                            for t in range(4 * b, 4 * b + 4):
                                last = nc.vector.tensor_scalar(XN[:, t, :], X[:, t, :], mv[:, t, 0:1], rstd[:, t:t + 1], ALU.subtract, ALU.mult)
                            last.then_inc(s_xn, 1)
                        dve.wait_ge(s_w, ALL_W)
                        link(nc.vector.tensor_reduce(smalls[:, 0:1], chd[:, :], AX.X, ALU.add))
                        link(nc.vector.tensor_scalar(smalls[:, 1:2], smalls[:, 0:1], 1.0 / NH, None, ALU.mult))
                        nc.vector.tensor_scalar(smalls[:, 8:16], chd[:, :], smalls[:, 1:2], None, ALU.subtract).then_inc(s_cos, 1)
                        link(nc.vector.tensor_tensor(smalls[:, 16:24], lam_in[:, 0, :], lam_in[:, 1, :], ALU.mult))
                        link(nc.vector.tensor_tensor(smalls[:, 24:32], lam_in[:, 2, :], lam_in[:, 3, :], ALU.mult))
                        nc.vector.tensor_reduce(smalls[:, 2:4], smalls[:, 16:32].rearrange("p (a b) -> p a b", b=8), AX.X, ALU.add).then_inc(s_cos, 1)
                        dve.wait_ge(s_act, 3)
                        link(nc.vector.tensor_scalar(smalls[:, 6:7], smalls[:, 4:5], 1.0, None, ALU.add))
                        link(nc.vector.reciprocal(smalls[:, 7:8], smalls[:, 6:7]))
                        link(nc.vector.tensor_scalar(smalls[:, 40:48], smalls[:, 32:40], 0.5, 1.0, ALU.mult, ALU.add))
                        link(nc.vector.tensor_scalar(smalls[:, 48:56], smalls[:, 40:48], smalls[:, 7:8], 15.0, ALU.mult, ALU.mult))
                        cv = cosb[:, :].rearrange("p (h s) -> p h s", s=2)
                        link(nc.vector.tensor_scalar(cv[:, :, 0], smalls[:, 48:56], 1.0, None, ALU.mult))
                        link(nc.vector.tensor_scalar(cv[:, :, 1], smalls[:, 48:56], -1.0, None, ALU.mult))
                        link(nc.vector.tensor_tensor(smalls[:, 56:57], smalls[:, 59:60], smalls[:, 58:59], ALU.subtract))
                        link(nc.vector.tensor_scalar(neg_lam[:, :], smalls[:, 56:57], 0.5, None, ALU.subtract))
                        def score(u):
                            dve.wait_ge(s_pr, u + 1)
                            nc.vector.tensor_reduce(att[:, u // 4, u % 4, :, :].rearrange("p k h -> p (k h)"),
                                                    prod[:, u % PR, :, :].rearrange("p k (h d) -> p (k h) d", d=32), AX.X, ALU.add).then_inc(s_sc, 1)

                        def norm_and_split(b):
                            dve.wait_ge(s_sq, b + 1)
                            ssb = ss[:, 4 * b:4 * b + 4, :]
                            nc.vector.tensor_reduce(ssb.rearrange("p t g -> p (t g)"), sq[:, :, :].rearrange("p t (g d) -> p (t g) d", d=8),
                                                    AX.X, ALU.add).then_inc(s_ss, 1)
                            score(4 * b)
                            dve.wait_ge(s_nrm, b + 1)
                            link(nc.vector.reciprocal(ssb.rearrange("p t g -> p (t g)"), ssb.rearrange("p t g -> p (t g)")))
                            link(nc.vector.tensor_tensor(ssb[:, :, 0:16], ssb[:, :, 0:16], cosb[:, :].unsqueeze(1).broadcast_to([P, 4, 16]), ALU.mult))
                            qk = qkv[:, 4 * b:4 * b + 4, 0:2 * D].rearrange("p t (g d) -> p t g d", d=8)
                            nc.vector.tensor_tensor(qk, qk, ssb.unsqueeze(3).broadcast_to([P, 4, 32, 8]), ALU.mult).then_inc(s_qkn, 1)
                            score(4 * b + 1)
                            for n, w in enumerate("qk"):
                                c = slice(512 * b, 512 * b + 512)
                                dve.wait_ge(s_hi, 2 * b + n + 1)
                                if b:
                                    dve.wait_ge(s_lo, 2 * b + n - 1)
                                    dve.wait_ge(s_mid, 2 * b + n - 1)
                                nc.vector.tensor_tensor(rest[w][:, :], psum[4 + n][:, :], parts[w, 0][:, c], ALU.subtract).then_inc(s_r1, 1)
                            for n, w in enumerate("qk"):
                                score(4 * b + 2 + n)
                                dve.wait_ge(s_mid, 2 * b + n + 1)
                                nc.vector.tensor_tensor(parts[w, 2][:, c], rest[w][:, :], parts[w, 1][:, c], ALU.subtract).then_inc(s_lo, 1)
                        for b in range(B):
                            for t in range(4 * b, 4 * b + 4):
                                dve.wait_ge(s_proj, t + 1)
                                nc.vector.tensor_tensor(mh[:, t, :], psum[2 * (t % 2) + 1][:, 0:3 * D], b_mha[:, :], ALU.add).then_inc(s_mh, 1)
                        for b in range(B):
                            norm_and_split(b)
                        a_kh = att[:, :, :, :, :].rearrange("p n q k h -> p (n q) k h")
                        a_hk = att[:, :, :, :, :].rearrange("p n q k h -> p (n q) h k")
                        am = amax[:, :].rearrange("p (a h) -> p a h", h=4)
                        dve.wait_ge(s_sc, 16)
                        link(nc.vector.tensor_reduce(am, a_hk, AX.X, ALU.max))
                        nc.vector.tensor_tensor(a_kh, a_kh, am.unsqueeze(2).broadcast_to([P, 16, 4, 4]), ALU.subtract).then_inc(s_sc, 1)
                        dve.wait_ge(s_ex, 1)
                        link(nc.vector.tensor_reduce(am, a_hk, AX.X, ALU.add))
                        link(nc.vector.reciprocal(amax[:, :], amax[:, :]))
                        nc.vector.tensor_tensor(a_kh, a_kh, am.unsqueeze(2).broadcast_to([P, 16, 4, 4]), ALU.mult).then_inc(s_at, 1)
                        for u in range(16):
                            nb, b1 = u // 4, u % 4
                            if u in on_pool:
                                dve.wait_ge(s_pv, on_pool.index(u) + 1)
                            else:
                                if u >= PR:
                                    dve.wait_ge(s_o, u - PR + 1)
                                weigh_values(nc.vector, u, s_pw)
                                dve.wait_ge(s_pw, u - sum(1 for x in on_pool if x < u) + 1)
                            nc.vector.tensor_reduce(mo[:, 4 * b1 + nb, :], prod[:, u % PR, :, :].rearrange("p k d -> p d k"), AX.X, ALU.add).then_inc(s_o, 1)
                        for b in range(B):
                            dve.wait_ge(s_wo, b + 1)
                            tl = slice(4 * b, 4 * b + 4)
                            link(nc.vector.tensor_tensor(Y1[:, tl, :], psum[6 + b % 2][:, :].rearrange("p (t d) -> p t d", d=D), XN[:, tl, :], ALU.add))
                            nc.vector.tensor_tensor(Y1[:, tl, :], Y1[:, tl, :], b_mo[:, :].unsqueeze(1).broadcast_to([P, 4, D]), ALU.add).then_inc(s_y0, 1)
                            dve.wait_ge(s_y0, b + 1)
                            for t in range(4 * b, 4 * b + 4):
                                last = nc.vector.bn_stats(stats[:, t, :], Y1[:, t, :])
                            link(last)
                            for t in range(4 * b, 4 * b + 4):
                                last = nc.vector.bn_aggr(mv[:, t, :], stats[:, t, :])
                            last.then_inc(s_ys, 1)
                        for b in range(B):
                            tl = slice(4 * b, 4 * b + 4)
                            dve.wait_ge(s_yr, b + 1)
                            for t in range(4 * b, 4 * b + 4):
                                last = nc.vector.tensor_scalar(Y1[:, t, :], Y1[:, t, :], mv[:, t, 0:1], rstd[:, t:t + 1], ALU.subtract, ALU.mult)
                            link(last)
                            link(nc.vector.tensor_tensor(Y1[:, tl, :], Y1[:, tl, :], g1_row[:, :].unsqueeze(1).broadcast_to([P, 4, D]), ALU.mult))
                            nc.vector.tensor_tensor(Y1[:, tl, :], Y1[:, tl, :], be1_row[:, :].unsqueeze(1).broadcast_to([P, 4, D]), ALU.add).then_inc(s_y1, 1)
                        dve.wait_ge(s_lgp, 1)
                        first_max(nc, link, lg, lgt, lmax, psum[0][:, 0:NT * NE].rearrange("p (t e) -> p t e", e=NE), rank_desc, mask0)

                    @block.gpsimd
                    def _(pool):
                        link = Chain(pool, s_pch)
                        pool.wait_ge(s_nh, 1)
                        for e in range(NE):
                            link(nc.gpsimd.memset(rank_desc[:, :, e:e + 1], float(NE - e)))
                        for b in range(B):
                            pool.wait_ge(s_stat, b + 1)
                            link(nc.gpsimd.tensor_scalar(rstd[:, 4 * b:4 * b + 4], mv[:, 4 * b:4 * b + 4, 1], EPS, None, ALU.add))
                            nc.gpsimd.tensor_tensor(rstd[:, 4 * b:4 * b + 4], rstd[:, 4 * b:4 * b + 4], neghalf[:, 0:4], ALU.pow).then_inc(s_rstd, 1)
                        mt = mh[:, :, :].rearrange("p (b n) c -> p n b c", n=4)

                        def product(u):
                            nb, b1 = u // 4, u % 4
                            if u >= PR:
                                pool.wait_ge(s_sc, u - PR + 1)
                            nc.gpsimd.tensor_tensor(prod[:, u % PR, :, :], mt[:, nb, b1, 0:D].unsqueeze(1).broadcast_to([P, 4, D]),
                                                    mt[:, nb, :, D:2 * D], ALU.mult).then_inc(s_pr, 1)

                        for b in range(B):
                            tl = slice(4 * b, 4 * b + 4)
                            pool.wait_ge(s_qkv, 4 * b + 4)
                            if b:
                                pool.wait_ge(s_ss, b)
                            nc.gpsimd.tensor_tensor(sq[:, :, :], qkv[:, tl, 0:2 * D], qkv[:, tl, 0:2 * D], ALU.mult).then_inc(s_sq, 1)
                            if b == 0:
                                pool.wait_ge(s_mh, NT)
                            product(4 * b)
                            pool.wait_ge(s_ss, b + 1)
                            ssb = ss[:, tl, :].rearrange("p t g -> p (t g)")
                            nc.gpsimd.tensor_scalar(ssb, ssb, 1e-12, None, ALU.max).then_inc(s_rn, 1)
                            for u in range(1, 4):
                                product(4 * b + u)
                        pool.wait_ge(s_at, 1)
                        for u in range(16):
                            if u in on_pool:
                                if u >= PR:
                                    pool.wait_ge(s_o, u - PR + 1)
                                weigh_values(nc.gpsimd, u, s_pv)
                        for b in range(B):
                            pool.wait_ge(s_ys, b + 1)
                            link(nc.gpsimd.tensor_scalar(rstd[:, 4 * b:4 * b + 4], mv[:, 4 * b:4 * b + 4, 1], EPS, None, ALU.add))
                            nc.gpsimd.tensor_tensor(rstd[:, 4 * b:4 * b + 4], rstd[:, 4 * b:4 * b + 4], neghalf[:, 0:4], ALU.pow).then_inc(s_yr, 1)

                    @block.scalar
                    def _(act):
                        act.preload_act_table_set("exp_and_others")

                        def parts_of(b):
                            act.wait_ge(s_rn, b + 1)
                            ssb = ss[:, 4 * b:4 * b + 4, :].rearrange("p t g -> p (t g)")
                            nc.scalar.activation(ssb, ssb, ACT.Sqrt).then_inc(s_nrm, 1)
                            c = slice(512 * b, 512 * b + 512)
                            for n, w in enumerate("qk"):
                                act.wait_ge(s_qkt, 2 * b + n + 1)
                                nc.scalar.activation(parts[w, 0][:, c], psum[4 + n][:, :], ACT.Copy).then_inc(s_hi, 1)
                            for n, w in enumerate("qk"):
                                act.wait_ge(s_r1, 2 * b + n + 1)
                                nc.scalar.activation(parts[w, 1][:, c], rest[w][:, :], ACT.Copy).then_inc(s_mid, 1)

                        for b in range(B):
                            act.wait_ge(s_xnt_ps, b + 1)
                            nc.scalar.activation(xnT[:, 512 * b:512 * b + 512], psum[6 + b % 2][:, :], ACT.Copy).then_inc(s_xnt, 1)
                            if b == 0:
                                act.wait_ge(s_w, ALL_W)
                                nc.scalar.activation(smalls[:, 4:5], craw[:, :], ACT.Exp, scale=-1.0).then_inc(s_act, 1)
                                act.wait_ge(s_cos, 2)
                                nc.scalar.activation(smalls[:, 32:40], smalls[:, 8:16], ACT.Tanh).then_inc(s_act, 1)
                                nc.scalar.activation(smalls[:, 58:60], smalls[:, 2:4], ACT.Exp).then_inc(s_act, 1)
                            for t in range(4 * b, 4 * b + 4):
                                act.wait_ge(s_proj, t + 1)
                                nc.scalar.activation(qkv[:, t, :], psum[2 * (t % 2)][:, 0:3 * D], ACT.Copy).then_inc(s_qkv, 1)
                        for b in range(B):
                            parts_of(b)
                        nc.scalar.activation(v_tok[:, :, :], qkv[:, :, 2 * D:3 * D], ACT.Copy).then_inc(s_ach, 1)
                        act.wait_ge(s_sc, 17)
                        af = att[:, :, :, :, :].rearrange("p n q k h -> p (n q k h)")
                        nc.scalar.activation(af, af, ACT.Exp, scale=32.0 ** -0.5).then_inc(s_ex, 1)
                        for b in range(B):
                            act.wait_ge(s_ot_ps, b + 1)
                            nc.scalar.activation(xnT[:, 512 * b:512 * b + 512], psum[b % 2][:, :], ACT.Copy).then_inc(s_ot, 1)
                        for b in range(B):
                            act.wait_ge(s_yt_ps, b + 1)
                            nc.scalar.activation(Y1T[:, 512 * b:512 * b + 512], psum[2 + b % 2][:, :], ACT.Copy).then_inc(s_yt, 1)

                    @block.tensor
                    def _(pe):
                        pe.wait_ge(s_w, ALL_W)

                        def qk_transposes(b):
                            pe.wait_ge(s_qkn, b + 1)
                            for n in range(2):
                                if b:
                                    pe.wait_ge(s_r1, 2 * b + n - 1)
                                for t in range(4):
                                    last = nc.tensor.transpose(psum[4 + n][:, P * t:P * t + P], qkv[:, 4 * b + t, n * D:n * D + D], ident[:, :])
                                last.then_inc(s_qkt, 1)

                        for b in range(B):
                            pe.wait_ge(s_xn, b + 1)
                            if b >= 2:
                                pe.wait_ge(s_xnt, b - 1)
                            for t in range(4):
                                last = nc.tensor.transpose(psum[6 + b % 2][:, P * t:P * t + P], XN[:, 4 * b + t, :], ident[:, :])
                            last.then_inc(s_xnt_ps, 1)
                            pe.wait_ge(s_xnt, b + 1)
                            for t in range(4 * b, 4 * b + 4):
                                if t >= 2:
                                    pe.wait_ge(s_qkv, t - 1)
                                    pe.wait_ge(s_mh, t - 1)
                                nc.tensor.matmul(psum[2 * (t % 2)][:, 0:3 * D], xnT[:, P * t:P * t + P], w_att[:, :], start=True, stop=True)
                                nc.tensor.matmul(psum[2 * (t % 2) + 1][:, 0:3 * D], xnT[:, P * t:P * t + P], w_mha[:, :], start=True, stop=True).then_inc(s_proj, 1)
                        for b in range(B):
                            qk_transposes(b)
                        for b in range(B):
                            pe.wait_ge(s_o, 12 + b + 1)
                            pe.wait_ge(s_qkv, NT)
                            pe.wait_ge(s_mh, NT)
                            if b >= 2:
                                pe.wait_ge(s_ot, b - 1)
                            for t in range(4):
                                last = nc.tensor.transpose(psum[b % 2][:, P * t:P * t + P], mo[:, 4 * b + t, :], ident[:, :])
                            last.then_inc(s_ot_ps, 1)
                        for b in range(B):
                            pe.wait_ge(s_ot, b + 1)
                            if b >= 2:
                                pe.wait_ge(s_y0, b - 1)
                            for t in range(4):
                                last = nc.tensor.matmul(psum[6 + b % 2][:, P * t:P * t + P], xnT[:, 512 * b + P * t:512 * b + P * t + P], w_mo[:, :], start=True, stop=True)
                            last.then_inc(s_wo, 1)
                        for b in range(B):
                            pe.wait_ge(s_y1, b + 1)
                            if b >= 2:
                                pe.wait_ge(s_yt, b - 1)
                            for t in range(4):
                                last = nc.tensor.transpose(psum[2 + b % 2][:, P * t:P * t + P], Y1[:, 4 * b + t, :], ident[:, :])
                            last.then_inc(s_yt_ps, 1)
                        pe.wait_ge(s_yt, B)
                        pe.wait_ge(s_ot, B)
                        for t in range(NT):
                            last = nc.tensor.matmul(psum[0][:, NE * t:NE * t + NE], Y1T[:, P * t:P * t + P], w_gate[:, :], start=True, stop=True)
                        last.then_inc(s_lgp, 1)
                nc.all_engine_barrier()
                nc.clear_and_free_semaphores(used1)
                nc.all_engine_barrier()
            st2 = ExitStack()
            with st2:
                RING = 4
                bank_d = [st2.enter_context(nc.psum_tensor(f"bank_d{i}", [P, 512], fp32)) for i in range(2)]
                bank_l = [st2.enter_context(nc.psum_tensor(f"bank_l{i}", [P, 2, 512], fp32)) for i in range(2)]
                bank_pv = st2.enter_context(nc.psum_tensor("bank_pv", [P, 512], fp32))
                bank_e = st2.enter_context(nc.psum_tensor("bank_e", [P, 4, D], fp32))
                kst = [sb(st2, f"k_stack{i}", [112, T], bf16) for i in range(2)]
                qst = [sb(st2, f"q_stack{i}", [112, T], bf16) for i in range(2)]
                weights = [sb(st2, f"expert_weights{i}", [P, 1028]) for i in range(2)]
                w1 = [w[:, 0:512] for w in weights]
                b1 = [w[:, 512:516] for w in weights]
                w2 = [w[:, 516:1028].rearrange("p (f d) -> p f d", f=4) for w in weights]
                xb = [sb(st2, f"block_in{i}", [P, D]) for i in range(2)]
                xbT = sb(st2, "block_inT", [P, P])
                eo = [sb(st2, f"block_out{i}", [P, D]) for i in range(2)]
                at_w = [sb(st2, f"weight_rows{i}", [P, 1], u32) for i in range(2)]
                zeros = sb(st2, "zeros2", [P, (BLOCKS + AHEAD) // 2, D])
                below = sb(st2, "below2", [P, P])
                ones = sb(st2, "ones2", [P, P])
                starts = sb(st2, "tile_starts_sb", [P, NT])
                blocks = sb(st2, "blocks_sb", [P, BLOCKS + AHEAD])
                lane = sb(st2, "lane_sb", [P, 1])
                cum = [sb(st2, f"cum2_{i}", [P, NT + 1, NE]) for i in range(2)]
                over = sb(st2, "over", [P, NE, NT])
                past = sb(st2, "past", [P, BLOCKS + AHEAD, NE])
                tiles = sb(st2, "tiles", [P, 3, NE])
                place0 = sb(st2, "place0", [P, NT, NE])
                row_f = sb(st2, "row_f", [P, NT])
                w_row = sb(st2, "w_row", [P, BLOCKS + AHEAD])
                vh = [sb(st2, f"v_head{i}", [P, NT, 32]) for i in range(2)]
                dgh = sb(st2, "dgh", [P, 2])
                gt = sb(st2, "gt", [P, RING, 512])
                tt = sb(st2, "tt", [P, RING, 2, 512])
                ex = sb(st2, "ex", [P, 2, 4, 2, 512])
                hid = sb(st2, "hid", [P, 4, P])
                pvs = sb(st2, "pvs", [P, 512])

                sem = lambda name: st2.enter_context(nc.semaphore(name))
                s_ld = [sem(f"head_loaded{i}") for i in range(2)]
                s_zv, s_zz = sem("v_heads_cleared"), sem("zeros_ready2")
                s_z, s_vh, s_dg = sem("stacks_cleared"), sem("v_head_ready"), sem("gain_of_head")
                s_D, s_L, s_G, s_T, s_E = map(sem, ("diff_in_psum", "logits_in_psum2", "gate_ready", "sums_ready", "exp_ready"))
                s_pvd, s_pvs, s_pvt, s_yb = map(sem, ("pv_done", "pv_copied", "pv_turned", "pv_kept"))
                s_cst, s_ones, s_cum, s_rk, s_rows, s_zf, s_scat, s_dch = map(sem, ("consts2", "ones_ready2", "counts_ready", "ranks2", "rows_known2", "rows_cleared2", "scattered2", "vector_steps2"))
                s_xt, s_xk, s_h, s_relu, s_dn, s_ek, s_cur, s_asked = map(sem, ("block_turned", "block_inT_kept", "hidden_in_psum", "hidden_ready", "block_done", "block_out_kept", "weight_rows_ready", "weights_asked"))
                s_xl = [sem(f"block_loaded{i}") for i in range(2)]
                s_wl = [sem(f"weights_gathered{i}") for i in range(2)]
                s_es = [sem(f"block_stored{i}") for i in range(2)]
                LEAD, STEPS, UNITS, LOADS, PER = 4, 32, 8, 12, BLOCKS // 4
                step = lambda q, n: LEAD + STEPS * q + n
                unit = lambda q, n: LEAD + UNITS * q + n
                blk = lambda q, n: LEAD + PER * q + n
                loaded = lambda q, k: q * (8 * PER) + 16 * (k // 2 + 1)

                with nc.Block() as block:
                    def load_head(sp, h, i):
                        for s in range(2):
                            rows = bass.ds(h * 16 + 8 * s, 8)
                            for n, (stack, order) in enumerate(((qst[i], (0, 1, 2, 0, 1, 0)), (kst[i], (0, 0, 0, 1, 1, 2)))):
                                if n == 0:
                                    groups = [(0, 0, 3), (3, 0, 2), (5, 0, 1)]
                                    for at, part, k in groups:
                                        sp.dma_start(stack[64 * s + 8 * at:64 * s + 8 * (at + k), :], qk_dram[0, part:part + k, rows, :]).then_inc(s_ld[i], 16)
                                else:
                                    groups = [(0, 0, 3), (3, 1, 2), (5, 2, 1)]
                                    for at, part, k in groups:
                                        sp.dma_start(stack[64 * s + 8 * at:64 * s + 8 * (at + k), :],
                                                     qk_dram[1, part:part + 1, rows, :].broadcast_to([k, 8, T])).then_inc(s_ld[i], 16)

                    @block.sync
                    def _(sp):
                        for dst, src in ((starts[:, :], A["tile_starts"].partition_broadcast(P)), (blocks[:, :], A["blocks"].partition_broadcast(P)),
                                         (lane[:, :], A["lane"]), (below[:, :], A["below"])):
                            sp.dma_start(dst, src).then_inc(s_cst, 16)
                        sp.wait_ge(s_z, 4)
                        for i in range(2):
                            load_head(sp, i, i)
                        sp.wait_ge(s_zz, 1)
                        half = P * (BLOCKS + AHEAD) // 2
                        for i in range(2):
                            sp.dma_start(yx_dram[half * i:half * i + half, :].rearrange("(p k) d -> p k d", p=P), zeros[:, :, :]).then_inc(s_zf, 16)

                        def load_block(j, i):
                            sp.dma_start(xb[i][:, :], yx_dram[bass.ds(j * P, P), :]).then_inc(s_xl[i], 16)

                        sp.wait_ge(s_scat, 16 * NT)
                        for i in range(AHEAD):
                            load_block(i, i)

                        def turn(q, more):
                            for k in range(PER):
                                if k == 2 and more:
                                    sp.wait_ge(s_L, step(q, 16))
                                    sp.wait_ge(s_z, 4)
                                    load_head(sp, q * 2 + 2, 0)
                                sp.wait_ge(s_ek, blk(q, k + 1))
                                sp.wait_ge(s_z, 4)
                                sp.dma_start(yo_dram[bass.ds((q * PER + k) * P, P), :], eo[k % 2][:, :]).then_inc(s_es[k % 2], 16)
                                load_block(q * PER + (k + AHEAD), k % 2)
                            if more:
                                sp.wait_ge(s_L, step(q, 32))
                                sp.wait_ge(s_z, 4)
                                load_head(sp, q * 2 + 3, 1)

                        with sp.Fori(0, 3) as q:
                            turn(q, True)
                        turn(3, False)
                        for i in range(2):
                            sp.wait_ge(s_es[i], 16 + loaded(3, PER - 2))
                            sp.wait_ge(s_xl[i], loaded(3, PER))

                    @block.gpsimd
                    def _(pool):
                        for t in (kst[0], qst[0]):
                            nc.gpsimd.memset(t[:, :], 0.0).then_inc(s_z, 1)
                        for i in range(2):
                            nc.gpsimd.memset(vh[i][:, :, :], 0.0).then_inc(s_zv, 1)
                        nc.gpsimd.memset(ones[:, :], 1.0).then_inc(s_ones, 1)
                        pool.wait_ge(s_zv, 2)
                        for i in range(2):
                            nc.gpsimd.memset(vh[i][:, :, 16:17], 1.0).then_inc(s_zv, 1)
                        pool.sem_inc(s_cur, LEAD)

                        def copy_v(h, i):
                            nc.gpsimd.tensor_copy(dgh[:, i:i + 1], delta_gain[:, bass.ds(h, 1)]).then_inc(s_dg, 1)
                            nc.gpsimd.tensor_copy(vh[i][:, :, 0:16], v_tok[:, :, bass.ds(h * 16, 16)]).then_inc(s_vh, 1)

                        def gather_weights(q, j, i, n):
                            nc.gpsimd.tensor_copy(at_w[i][:, :], w_row[:, bass.ds(j, 1)]).then_inc(s_cur, 1)
                            pool.wait_ge(s_cur, blk(q, n + 1))
                            pool.sem_inc(s_asked, 1)
                            nc.gpsimd.indirect_dma_start(weights[i][:, :], None, A["w_expert"], bass.IndirectOffsetOnAxis(ap=at_w[i][:, 0:1], axis=0),
                                                         bounds_check=NE * P - 1, oob_is_err=False).then_inc(s_wl[i], 16)

                        for i in range(2):
                            copy_v(i, i)
                        nc.gpsimd.memset(zeros[:, :, :], 0.0).then_inc(s_zz, 1)
                        pool.wait_ge(s_rows, 1)
                        pool.wait_ge(s_zf, 32)
                        for t in range(NT):
                            nc.gpsimd.indirect_dma_start(yx_dram[:, :], bass.IndirectOffsetOnAxis(ap=row_u[:, t:t + 1], axis=0), Y1[:, t, :], None,
                                                         bounds_check=(BLOCKS + AHEAD) * P - 1, oob_is_err=False).then_inc(s_scat, 16)
                        for i in range(AHEAD):
                            gather_weights(0, i, i, i)

                        def turn(q, more):
                            for k in range(PER):
                                if k == 2 and more:
                                    pool.wait_ge(s_pvd, unit(q, 4))
                                    copy_v(q * 2 + 2, 0)
                                pool.wait_ge(s_dn, blk(q, k + 1))
                                gather_weights(q, q * PER + (k + AHEAD), k % 2, k + AHEAD)
                            if more:
                                pool.wait_ge(s_pvd, unit(q, 8))
                                copy_v(q * 2 + 3, 1)

                        with pool.Fori(0, 3) as q:
                            turn(q, True)
                        turn(3, False)
                        for i in range(2):
                            pool.wait_ge(s_wl[i], loaded(3, PER))

                    @block.tensor
                    def _(pe):
                        for s in (s_D, s_L, s_pvd, s_pvt, s_xt, s_h, s_dn):
                            pe.sem_inc(s, LEAD)
                        pe.wait_ge(s_zv, 4)
                        pe.wait_ge(s_ones, 1)
                        pe.wait_ge(s_cst, 16 * 4)
                        pe.wait_ge(s_cum, 1)
                        rank_bank = bank_e[:, :, :].rearrange("p t d -> p (t d)")
                        nc.tensor.matmul(rank_bank[:, 0:P], below[:, :], mask0[:, :, :].rearrange("p t e -> p (t e)"), start=True, stop=False)
                        nc.tensor.matmul(rank_bank[:, 0:P], ones[:, :], cum[0][:, 0:NT, :].rearrange("p t e -> p (t e)"), start=False, stop=True)
                        nc.tensor.matmul(rank_bank[:, P:P + NE], ones[:, :], cum[0][:, NT, :], start=True, stop=True).then_inc(s_rk, 1)

                        def operands(q, st):
                            u, mb = st // 4, st % 4
                            i, b = u // 4, u % 4
                            if st % 16 == 0:
                                pe.wait_ge(s_ld[i], q * (16 * LOADS) + 16 * LOADS)
                            k = slice(512 * b + P * mb, 512 * b + P * mb + P)
                            return kst[i], qst[i], k, slice(512 * b, 512 * b + 512)

                        def difference(q, st):
                            ks, qs, k, n = operands(q, st)
                            pe.wait_ge(s_G, step(q, st - 1))
                            nc.tensor.matmul(bank_d[st % 2][:, :], ks[:, k], qs[:, n], start=True, stop=True).then_inc(s_D, 1)

                        def scores(q, st):
                            ks, qs, k, n = operands(q, st)
                            pe.wait_ge(s_T, step(q, st - 1))
                            nc.tensor.matmul(bank_l[st % 2][:, 0, :], ks[0:48, k], qs[0:48, n], start=True, stop=True)
                            nc.tensor.matmul(bank_l[st % 2][:, 1, :], ks[64:112, k], qs[64:112, n], start=True, stop=True).then_inc(s_L, 1)

                        def turn_block(q, k):
                            pe.wait_ge(s_xl[k % 2], loaded(q, k))
                            pe.wait_ge(s_ek, blk(q, k))
                            pe.wait_ge(s_rows, 1)
                            nc.tensor.transpose(bank_e[:, 0, :], xb[k % 2][:, :], ident[:, :]).then_inc(s_xt, 1)

                        def hidden(q, k):
                            pe.wait_ge(s_xk, blk(q, k + 1))
                            pe.wait_ge(s_wl[k % 2], loaded(q, k))
                            for f in range(4):
                                last = nc.tensor.matmul(bank_e[:, f, :], w1[k % 2][:, P * f:P * f + P], xbT[:, :], start=True, stop=True)
                            last.then_inc(s_h, 1)

                        def block_out(q, k):
                            pe.wait_ge(s_relu, blk(q, k + 1))
                            for f in range(4):
                                last = nc.tensor.matmul(bank_e[:, 0, :], hid[:, f, :], w2[k % 2][:, f, :], start=(f == 0), stop=(f == 3))
                            last.then_inc(s_dn, 1)

                        def weigh(q, u, pair):
                            i, b = u // 4, u % 4
                            if pair == 0:
                                pe.wait_ge(s_yb, unit(q, u))
                                pe.wait_ge(s_vh, q * 2 + (i + 1))
                            pe.wait_ge(s_E, step(q, 4 * u + 2 * pair + 2))
                            for m in range(2):
                                for s in range(2):
                                    j = 2 * s + m
                                    mb = 2 * pair + m
                                    last = nc.tensor.matmul(bank_pv[32 * j:32 * j + 32, :], vh[i][:, 4 * b + mb, :], ex[:, u % 2, mb, s, :],
                                                            start=(pair == 0), stop=(pair == 1), tile_position=(0, 32 * j), skip_group_check=True)
                            if pair == 1:
                                last.then_inc(s_pvd, 1)

                        def turn(q, u):
                            pe.wait_ge(s_pvs, unit(q, u + 1))
                            for t in range(4):
                                last = nc.tensor.transpose(bank_pv[:, P * t:P * t + P], pvs[:, P * t:P * t + P], ident[:, :])
                            last.then_inc(s_pvt, 1)

                        with pe.Fori(0, 4) as q:
                            difference(q, 0)
                            difference(q, 1)
                            scores(q, 0)
                            for st in range(STEPS):
                                u, mb = st // 4, st % 4
                                if st < STEPS - 2:
                                    difference(q, st + 2)
                                if st < STEPS - 1:
                                    scores(q, st + 1)
                                k = u - 2
                                if mb == 0 and u >= 2:
                                    turn(q, u - 2)
                                if mb == 0 and k >= 0:
                                    turn_block(q, k)
                                if mb == 1 and k >= 0:
                                    hidden(q, k)
                                if mb == 1 and u:
                                    weigh(q, u - 1, 0)
                                if mb == 2 and k >= 0:
                                    block_out(q, k)
                                if mb == 2 and u:
                                    weigh(q, u - 1, 1)
                            turn(q, UNITS - 2)
                            weigh(q, UNITS - 1, 0)
                            weigh(q, UNITS - 1, 1)
                            turn(q, UNITS - 1)

                    @block.scalar
                    def _(act):
                        act.preload_act_table_set("exp_and_others")
                        for s in (s_G, s_E, s_pvs, s_xk, s_ek):
                            act.sem_inc(s, LEAD)
                        for s in s_es:
                            act.sem_inc(s, 16)
                        with act.Fori(0, 4) as q:
                            def gate(st):
                                if st % 16 == 0:
                                    act.wait_ge(s_dg, q * 2 + (st // 16 + 1))
                                act.wait_ge(s_D, step(q, st + 1))
                                act.wait_ge(s_T, step(q, st - RING + 1))
                                nc.scalar.activation(gt[:, st % RING, :], bank_d[st % 2][:, :], ACT.Tanh, scale=dgh[:, st // 16:st // 16 + 1]).then_inc(s_G, 1)

                            def exps(st):
                                act.wait_ge(s_T, step(q, st + 1))
                                if st % 4 == 0:
                                    act.wait_ge(s_pvd, unit(q, st // 4 - 1))
                                nc.scalar.activation(ex[:, (st // 4) % 2, st % 4, :, :], tt[:, st % RING, :, :], ACT.Exp).then_inc(s_E, 1)

                            def keep(u):
                                act.wait_ge(s_pvd, unit(q, u + 1))
                                act.wait_ge(s_pvt, unit(q, u))
                                nc.scalar.activation(pvs[:, :], bank_pv[:, :], ACT.Copy).then_inc(s_pvs, 1)

                            def keep_in(k):
                                act.wait_ge(s_xt, blk(q, k + 1))
                                nc.scalar.activation(xbT[:, :], bank_e[:, 0, :], ACT.Copy).then_inc(s_xk, 1)

                            def keep_out(k):
                                act.wait_ge(s_dn, blk(q, k + 1))
                                act.wait_ge(s_es[k % 2], loaded(q, k))
                                nc.scalar.activation(eo[k % 2][:, :], bank_e[:, 0, :], ACT.Copy).then_inc(s_ek, 1)

                            gate(0)
                            gate(1)
                            for st in range(1, STEPS):
                                if st + 1 < STEPS:
                                    gate(st + 1)
                                exps(st - 1)
                                if st % 4 == 3 and st > 4:
                                    keep(st // 4 - 1)
                                k = st // 4 - 2
                                if st % 4 == 0 and k >= 0:
                                    keep_in(k)
                                if st % 4 == 3 and k >= 0:
                                    keep_out(k)
                            exps(STEPS - 1)
                            keep(UNITS - 1)

                    @block.vector
                    def _(dve):
                        for s in (s_T, s_yb, s_relu):
                            dve.sem_inc(s, LEAD)
                        for t in (kst[1], qst[1]):
                            nc.vector.memset(t[:, :], 0.0).then_inc(s_z, 1)
                        link = Chain(dve, s_dch)
                        TT = nc.vector.tensor_tensor
                        for c in range(2):
                            link(nc.vector.memset(cum[c][:, :, :], 0.0))
                        link(nc.vector.tensor_copy(cum[0][:, 1:NT + 1, :], mask0[:, :, :]))
                        for n, far in enumerate((1, 2, 4, 8)):
                            a, z = cum[n % 2], cum[(n + 1) % 2]
                            link(nc.vector.tensor_copy(z[:, 0:far, :], a[:, 0:far, :]))
                            link(TT(z[:, far:NT + 1, :], a[:, far:NT + 1, :], a[:, 0:NT + 1 - far, :], ALU.add), s_cum if n == 3 else None)
                        dve.wait_ge(s_rk, 1)
                        dve.wait_ge(s_cst, 16 * 4)
                        dve.wait_ge(s_ones, 1)
                        rank_bank = bank_e[:, :, :].rearrange("p t d -> p (t d)")
                        link(TT(over[:, :, :], rank_bank[:, P:P + NE].unsqueeze(2).broadcast_to([P, NE, NT]), starts[:, :].unsqueeze(1).broadcast_to([P, NE, NT]), ALU.is_gt))
                        link(nc.vector.tensor_reduce(tiles[:, 0, :], over[:, :, :], AX.X, ALU.add))
                        link(nc.vector.tensor_tensor_scan(tiles[:, 1, :], ones[:, 0:NE], tiles[:, 0, :], 0.0, ALU.mult, ALU.add))
                        link(TT(tiles[:, 2, :], tiles[:, 1, :], tiles[:, 0, :], ALU.subtract))
                        link(nc.vector.tensor_scalar(tiles[:, 2, :], tiles[:, 2, :], float(P), None, ALU.mult))
                        link(TT(place0[:, :, :], rank_bank[:, 0:P].rearrange("p (t e) -> p t e", e=NE), tiles[:, 2, :].unsqueeze(1).broadcast_to([P, NT, NE]), ALU.add))
                        link(TT(place0[:, :, :], place0[:, :, :], mask0[:, :, :], ALU.mult))
                        link(nc.vector.tensor_reduce(row_f[:, :], place0[:, :, :], AX.X, ALU.add))
                        link(nc.vector.tensor_copy(row_u[:, :], row_f[:, :]))
                        link(TT(past[:, :, :], blocks[:, :].unsqueeze(2).broadcast_to([P, BLOCKS + AHEAD, NE]), tiles[:, 1, :].unsqueeze(1).broadcast_to([P, BLOCKS + AHEAD, NE]), ALU.is_ge))
                        link(nc.vector.tensor_reduce(w_row[:, :], past[:, :, :], AX.X, ALU.add))
                        link(nc.vector.tensor_scalar(w_row[:, :], w_row[:, :], float(NE - 1), float(P), ALU.min, ALU.mult))
                        link(nc.vector.tensor_scalar(w_row[:, :], w_row[:, :], lane[:, 0:1], None, ALU.add), s_rows)
                        with dve.Fori(0, 4) as q:
                            def settle(u):
                                b = u % 4
                                h = q * 2 + u // 4
                                dve.wait_ge(s_pvt, unit(q, u + 1))
                                nc.vector.tensor_reduce(ybig[:, 4 * b:4 * b + 4, bass.ds(h * 34, 34)].rearrange("p t (s c) -> p t s c", s=2),
                                                        bank_pv[:, :].rearrange("p (t s m c) -> p t s c m", t=4, s=2, m=2)[:, :, :, 0:17, :],
                                                        AX.X, ALU.add).then_inc(s_yb, 1)

                            for st in range(STEPS):
                                u, mb = st // 4, st % 4
                                i = u // 4
                                dve.wait_ge(s_L, step(q, st + 1))
                                dve.wait_ge(s_G, step(q, st + 1))
                                dve.wait_ge(s_E, step(q, st - RING + 1))
                                nc.vector.tensor_tensor(tt[:, st % RING, 0, :], bank_l[st % 2][:, 0, :], gt[:, st % RING, :], ALU.add)
                                nc.vector.scalar_tensor_tensor(tt[:, st % RING, 1, :], bank_l[st % 2][:, 1, :], -1.0, gt[:, st % RING, :],
                                                               ALU.mult, ALU.subtract).then_inc(s_T, 1)
                                k = u - 2
                                if mb == 1 and k >= 0:
                                    dve.wait_ge(s_h, blk(q, k + 1))
                                    dve.wait_ge(s_wl[k % 2], loaded(q, k))
                                    for f in range(4):
                                        last = nc.vector.tensor_scalar(hid[:, f, :], bank_e[:, f, :], b1[k % 2][:, f:f + 1], 0.0, ALU.add, ALU.max)
                                    last.then_inc(s_relu, 1)
                                if mb == 0 and u >= 2:
                                    settle(u - 2)
                            settle(UNITS - 2)
                            settle(UNITS - 1)
            st3 = ExitStack()
            with st3:
                bank = [st3.enter_context(nc.psum_tensor(f"s3_bank{i}", [P, 4, D], fp32)) for i in range(8)]
                b2blk = sb(st3, "b2blk", [P, NT, D])
                rs = sb(st3, "rs", [P, NT * NH * 2])
                yv = sb(st3, "yv", [P, NT, D])
                y2 = sb(st3, "y2", [P, NT, D])
                ms = sb(st3, "ms", [P, NT * NH])
                yT = sb(st3, "yT", [P, T])
                maskT = sb(st3, "maskT", [P, P])
                z = sb(st3, "z", [P, NT, D])
                gg = sb(st3, "gg", [P, NT, D])
                stats = sb(st3, "stats3", [P, NT, 6])
                mv = sb(st3, "mv3", [P, NT, 2])
                mw = sb(st3, "mw3", [P, NT, 2])
                rstd = sb(st3, "rstd3", [P, NT])
                rstw = sb(st3, "rstw3", [P, NT])
                neghalf = sb(st3, "neghalf3", [P, P])
                sem = lambda name: st3.enter_context(nc.semaphore(name))
                s_acc = sem("rows_back3")
                s_b2, s_dch, s_pch, s_z0 = map(sem, ("b2_loaded", "vector_steps3", "pool_steps3", "b2_cleared"))
                s_ms, s_rms, s_yv, s_yt_ps, s_yt, s_so = map(sem, ("meansq3", "rms3", "y_ready3", "yT_in_psum3", "yT_ready3", "attention_out"))
                s_mt_ps, s_mt, s_b2o, s_zst, s_zr, s_zz, s_gg = map(sem, ("maskT_in_psum", "maskT_ready", "b2_in_psum", "z_stats", "z_rstd", "z_ready", "gate_done"))
                s_xst, s_xr, s_xn, s_xt_ps, s_xt = map(sem, ("x_stats", "x_rstd", "xn_ready3", "xT_in_psum", "xT_ready"))

                with nc.Block() as block:
                    @block.sync
                    def _(sp):
                        sp.wait_ge(s_z0, 1)
                        for t in range(NT):
                            sp.dma_start(b2blk[NE * t:NE * t + NE, t, :], A["b2"]).then_inc(s_b2, 16)

                    @block.gpsimd
                    def _(pool):
                        link = Chain(pool, s_pch)
                        nc.gpsimd.memset(b2blk[:, :, :], 0.0).then_inc(s_z0, 1)
                        link(nc.gpsimd.memset(neghalf[:, :], -0.5))
                        for t in range(NT):
                            nc.gpsimd.indirect_dma_start(ACC[:, t, :], None, yo_dram[:, :], bass.IndirectOffsetOnAxis(ap=row_u[:, t:t + 1], axis=0),
                                                         bounds_check=BLOCKS * P - 1, oob_is_err=False).then_inc(s_acc, 16)
                        pool.wait_ge(s_zst, 1)
                        link(nc.gpsimd.tensor_scalar(rstd[:, :], mv[:, :, 1], EPS, None, ALU.add))
                        nc.gpsimd.tensor_tensor(rstd[:, :], rstd[:, :], neghalf[:, 0:NT], ALU.pow).then_inc(s_zr, 1)
                        pool.wait_ge(s_xst, 1)
                        link(nc.gpsimd.tensor_scalar(rstw[:, :], mw[:, :, 1], EPS, None, ALU.add))
                        nc.gpsimd.tensor_tensor(rstw[:, :], rstw[:, :], neghalf[:, 0:NT], ALU.pow).then_inc(s_xr, 1)

                    @block.scalar
                    def _(act):
                        act.preload_act_table(ACT.Sqrt)
                        act.wait_ge(s_mt_ps, 1)
                        nc.scalar.activation(maskT[:, :], bank[0][:, 0, :], ACT.Copy).then_inc(s_mt, 1)
                        act.wait_ge(s_ms, 1)
                        nc.scalar.activation(ms[:, :], ms[:, :], ACT.Sqrt).then_inc(s_rms, 1)
                        act.preload_act_table(ACT.Silu)
                        for b in range(B):
                            act.wait_ge(s_yt_ps, b + 1)
                            nc.scalar.activation(yT[:, 512 * b:512 * b + 512], bank[b % 2][:, :, :].rearrange("p t d -> p (t d)"), ACT.Copy).then_inc(s_yt, 1)
                        act.wait_ge(s_zz, 1)
                        nc.scalar.activation(gg[:, :, :], z[:, :, :], ACT.Silu).then_inc(s_gg, 1)
                        for b in range(B):
                            act.wait_ge(s_xt_ps, b + 1)
                            nc.scalar.activation(XT[:, b, :], bank[4 + b][:, :, :].rearrange("p t d -> p (t d)"), ACT.Copy).then_inc(s_xt, 1)

                    @block.tensor
                    def _(pe):
                        nc.tensor.transpose(bank[0][:, 0, :], mask0[:, :, :].rearrange("p t e -> p (t e)"), ident[:, :]).then_inc(s_mt_ps, 1)
                        pe.wait_ge(s_mt, 1)
                        pe.wait_ge(s_b2, 16 * NT)
                        for t in range(NT):
                            last = nc.tensor.matmul(bank[4 + t // 4][:, t % 4, :], maskT[:, :], b2blk[:, t, :], start=True, stop=True)
                        last.then_inc(s_b2o, 1)
                        pe.wait_ge(s_yv, 1)
                        for b in range(B):
                            if b >= 2:
                                pe.wait_ge(s_yt, b - 1)
                            for t in range(4):
                                last = nc.tensor.transpose(bank[b % 2][:, t, :], yv[:, 4 * b + t, :], ident[:, :])
                            last.then_inc(s_yt_ps, 1)
                        pe.wait_ge(s_yt, B)
                        for b in range(B):
                            for t in range(4):
                                last = nc.tensor.matmul(bank[b][:, t, :], yT[:, P * (4 * b + t):P * (4 * b + t) + P], wo_att[:, :], start=True, stop=True)
                        last.then_inc(s_so, 1)
                        pe.wait_ge(s_xn, 1)
                        for b in range(B):
                            for t in range(4):
                                last = nc.tensor.transpose(bank[4 + b][:, t, :], XN[:, 4 * b + t, :], ident[:, :])
                            last.then_inc(s_xt_ps, 1)

                    @block.vector
                    def _(dve):
                        link = Chain(dve, s_dch)
                        yb = ybig[:, :, :].rearrange("p t (h s c) -> p (t h s) c", s=2, c=17)
                        link(nc.vector.reciprocal(rs[:, :].unsqueeze(2), yb[:, :, 16:17]))
                        rv = rs[:, :].rearrange("p (a s) -> p a s", s=2)
                        link(nc.vector.tensor_scalar(rv[:, :, 1], rv[:, :, 1], neg_lam[:, :], None, ALU.mult))
                        link(nc.vector.tensor_scalar(subln[:, :], subln[:, :], 0.5, None, ALU.mult))
                        link(nc.vector.tensor_tensor(yb[:, :, 0:16], yb[:, :, 0:16], rs[:, :].unsqueeze(2).broadcast_to([P, NT * NH * 2, 16]), ALU.mult))
                        y4 = ybig[:, :, :].rearrange("p t (h s c) -> p (t h) s c", s=2, c=17)
                        yf = yv[:, :, :].rearrange("p t (h d) -> p (t h) d", d=16)
                        y2f = y2[:, :, :].rearrange("p t (h d) -> p (t h) d", d=16)
                        link(nc.vector.tensor_tensor(yf, y4[:, :, 0, 0:16], y4[:, :, 1, 0:16], ALU.add))
                        link(nc.vector.tensor_tensor(y2[:, :, :], yv[:, :, :], yv[:, :, :], ALU.mult))
                        link(nc.vector.tensor_reduce(ms[:, :], y2f, AX.X, ALU.add))
                        nc.vector.tensor_scalar(ms[:, :], ms[:, :], 1.0 / 16, 1e-5, ALU.mult, ALU.add).then_inc(s_ms, 1)
                        dve.wait_ge(s_rms, 1)
                        link(nc.vector.reciprocal(ms[:, :], ms[:, :]))
                        link(nc.vector.tensor_tensor(yf, yf, ms[:, :].unsqueeze(2).broadcast_to([P, NT * NH, 16]), ALU.mult))
                        nc.vector.tensor_tensor(yf, yf, subln[:, :].unsqueeze(1).broadcast_to([P, NT * NH, 16]), ALU.mult).then_inc(s_yv, 1)
                        dve.wait_ge(s_b2o, 1)
                        dve.wait_ge(s_acc, 16 * NT)
                        link(nc.vector.tensor_tensor(z[:, :, :], ACC[:, :, :], Y1[:, :, :], ALU.add))
                        for b in range(B):
                            last = nc.vector.tensor_tensor(z[:, 4 * b:4 * b + 4, :], z[:, 4 * b:4 * b + 4, :], bank[4 + b][:, :, :], ALU.add)
                        link(last)
                        for t in range(NT):
                            last = nc.vector.bn_stats(stats[:, t, :], z[:, t, :])
                        link(last)
                        for t in range(NT):
                            last = nc.vector.bn_aggr(mv[:, t, :], stats[:, t, :])
                        last.then_inc(s_zst, 1)
                        dve.wait_ge(s_zr, 1)
                        for t in range(NT):
                            last = nc.vector.tensor_scalar(z[:, t, :], z[:, t, :], mv[:, t, 0:1], rstd[:, t:t + 1], ALU.subtract, ALU.mult)
                        link(last)
                        link(nc.vector.tensor_tensor(z[:, :, :], z[:, :, :], g2_row[:, :].unsqueeze(1).broadcast_to([P, NT, D]), ALU.mult))
                        nc.vector.tensor_tensor(z[:, :, :], z[:, :, :], be2_row[:, :].unsqueeze(1).broadcast_to([P, NT, D]), ALU.add).then_inc(s_zz, 1)
                        dve.wait_ge(s_so, 1)
                        for b in range(B):
                            last = nc.vector.tensor_tensor(y2[:, 4 * b:4 * b + 4, :], bank[b][:, :, :], bo_row[:, :].unsqueeze(1).broadcast_to([P, 4, D]), ALU.add)
                        link(last)
                        dve.wait_ge(s_gg, 1)
                        link(nc.vector.tensor_tensor(y2[:, :, :], y2[:, :, :], gg[:, :, :], ALU.mult))
                        link(nc.vector.tensor_tensor(X[:, :, :], X[:, :, :], y2[:, :, :], ALU.add))
                        for t in range(NT):
                            last = nc.vector.bn_stats(stats[:, t, :], X[:, t, :])
                        link(last)
                        for t in range(NT):
                            last = nc.vector.bn_aggr(mw[:, t, :], stats[:, t, :])
                        last.then_inc(s_xst, 1)
                        dve.wait_ge(s_xr, 1)
                        for t in range(NT):
                            last = nc.vector.tensor_scalar(XN[:, t, :], X[:, t, :], mw[:, t, 0:1], rstw[:, t:t + 1], ALU.subtract, ALU.mult)
                        last.then_inc(s_xn, 1)
        st4 = ExitStack()
        with st4:
            CAP = int(1.25 * T / NE)
            ROWS = NE * CAP
            FAR = 1.0e6
            g_bank = [st4.enter_context(nc.psum_tensor(f"g_bank{i}", [P, 512], fp32)) for i in range(2)]
            u_bank = [st4.enter_context(nc.psum_tensor(f"u_bank{i}", [P, 512], fp32)) for i in range(2)]
            o_bank = st4.enter_context(nc.psum_tensor("o_bank4", [P, 4, D], fp32))
            e_bank = st4.enter_context(nc.psum_tensor("e_bank4", [P, 4, D], fp32))
            x_bank = st4.enter_context(nc.psum_tensor("x_bank4", [P, 512], fp32))
            r_bank = st4.enter_context(nc.psum_tensor("r_bank4", [P, 512], fp32))
            xg_dram = nc.dram_tensor("expert_rows", [ROWS, D], fp32).ap()
            w_r = sb(st4, "w_r", [P, NE])
            w_sg = sb(st4, "w_sg", [P, 1024])
            w_su = sb(st4, "w_su", [P, 1024])
            w_sd = sb(st4, "w_sd", [P, 8, D])
            w_rg = [sb(st4, f"w_rg{i}", [P, 512]) for i in range(2)]
            w_ru = [sb(st4, f"w_ru{i}", [P, 512]) for i in range(2)]
            w_rd = [sb(st4, f"w_rd{i}", [P, 4, D]) for i in range(2)]
            below = sb(st4, "below_sb", [P, P])
            ones = sb(st4, "ones4", [P, P])
            zeros = sb(st4, "zeros4", [P, 20, D])
            neghalf = sb(st4, "neghalf4", [P, NT])
            base_row = sb(st4, "base_row", [P, NT, NE])
            sq = sb(st4, "sq4", [P, NT, D])
            pr = sb(st4, "pr", [P, NT, NE])
            p2 = sb(st4, "p2", [P, NT, NE])
            cand = sb(st4, "cand4", [P, NT, NE])
            oh = [sb(st4, f"oh{i}", [P, NT, NE]) for i in range(2)]
            sel = sb(st4, "sel", [P, NT, NE])
            cum = [sb(st4, f"cum{i}", [P, NT + 1, NE]) for i in range(2)]
            kept = sb(st4, "kept", [P, NT, NE])
            row = sb(st4, "row4", [P, NT, NE])
            cols = sb(st4, "cols4", [P, 12, NT])
            hid = sb(st4, "hid4", [P, 2, 8, 512])
            sil = sb(st4, "sil4", [P, 2, 512])
            xg = [sb(st4, f"xg{i}", [P, 3, D]) for i in range(2)]
            xgT = sb(st4, "xgT", [P, 2, CAP])
            eo = sb(st4, "eo", [P, 2, 3, D])

            sem = lambda name: st4.enter_context(nc.semaphore(name))
            s_wr = sem("router_loaded")
            s_w4, s_w8 = sem("shared_loaded"), [sem(f"expert_loaded{i}") for i in range(2)]
            s_xg = [sem(f"rows_loaded{i}") for i in range(2)]
            s_lg4, s_sq4, s_ms4, s_rn4, s_x4, s_e4, s_sel, s_rk, s_rows = map(sem, ("logits4", "squares4", "meansq4", "rnorm4", "logits_shifted", "exps4", "selected", "ranks", "rows_known"))
            s_dch, s_pch, s_clr, s_zf, s_scat = map(sem, ("vector_steps4", "pool_steps4", "cleared4", "rows_cleared_x_stored", "scattered"))
            s_gu, s_si, s_hd, s_od, s_oc = map(sem, ("gate_up_in_psum", "silu_done", "hidden_done", "shared_out_in_psum", "shared_out_kept"))
            s_tp, s_tc, s_gu8, s_si8, s_hd8, s_ed, s_ec = map(sem, ("rowsT_in_psum", "rowsT_kept", "gate_up_in_psum8", "silu_done8", "hidden_done8", "expert_out_in_psum", "expert_out_kept"))
            s_es = [sem(f"expert_out_stored{i}") for i in range(2)]
            LEAD = 4
            at = lambda i, per, k: i * per + (LEAD + k)

            with nc.Block() as block:
                @block.sync
                def _(sp):
                    for dst, src in ((w_r[:, :], A["w_router"]), (below[:, :], A["below"])):
                        sp.dma_start(dst, src).then_inc(s_wr, 16)
                    for dst, src in ((w_sg[:, :], A["w_sg"]), (w_su[:, :], A["w_su"]), (w_sd[:, :, :], A["w_sd"])):
                        sp.dma_start(dst, src).then_inc(s_w4, 16)
                    sp.dma_start(w_in[:, :], A["w_in"][0:1].rearrange("o p e -> p (o e)")).then_inc(s_win, 16)
                    sp.dma_start(conv_row[:, :, :], A["conv_row"][0:1].broadcast_to([P, 4, 256])).then_inc(s_win, 16)
                    sp.dma_start(x_dram, X[:, :, :]).then_inc(s_zf, 16)
                    sp.wait_ge(s_clr, 1)
                    sp.dma_start(xg_dram.rearrange("(p k) d -> p k d", p=P), zeros[:, :, :]).then_inc(s_zf, 16)

                    def load_weights(e, i):
                        one = lambda x: x[bass.ds(e, 1)]
                        sp.dma_start(w_rg[i][:, :], one(A["w_rg"]).rearrange("o p f -> p (o f)")).then_inc(s_w8[i], 16)
                        sp.dma_start(w_ru[i][:, :], one(A["w_ru"]).rearrange("o p f -> p (o f)")).then_inc(s_w8[i], 16)
                        sp.dma_start(w_rd[i][:, :, :], one(A["w_rd"]).rearrange("o (k p) d -> p (o k) d", p=P)).then_inc(s_w8[i], 16)

                    def load_rows(e, i):
                        for k in range(3):
                            n = min(P, CAP - P * k)
                            sp.dma_start(xg[i][0:n, k, :], xg_dram[bass.ds(e * CAP + P * k, n), :]).then_inc(s_xg[i], 16)

                    for i in range(2):
                        load_weights(i, i)
                    sp.wait_ge(s_scat, 16 * 2 * NT)
                    for i in range(2):
                        load_rows(i, i)
                    def turn(q, more):
                        for i in range(2):
                            if more:
                                sp.wait_ge(s_tc, at(q, 2, i + 1))
                                sp.wait_ge(s_clr, 1)
                                load_rows(q * 2 + (2 + i), i)
                            sp.wait_ge(s_ec, at(q, 2, i + 1))
                            sp.wait_ge(s_clr, 1)
                            for k in range(3):
                                n = min(P, CAP - P * k)
                                sp.dma_start(eo_dram[bass.ds((q * 2 + i) * CAP + P * k, n), :], eo[0:n, i, k, :]).then_inc(s_es[i], 16)
                            if more:
                                load_weights(q * 2 + (2 + i), i)

                    with sp.Fori(0, 3) as q:
                        turn(q, True)
                    turn(3, False)
                    for i in range(2):
                        sp.wait_ge(s_es[i], 16 + 4 * 48)

                @block.gpsimd
                def _(pool):
                    link = Chain(pool, s_pch)
                    link(nc.gpsimd.memset(neghalf[:, :], -0.5))
                    nc.gpsimd.memset(zeros[:, :, :], 0.0).then_inc(s_clr, 1)
                    for e in range(NE):
                        nc.gpsimd.memset(base_row[:, :, e:e + 1], float(CAP * e)).then_inc(s_clr, 1)
                    nc.gpsimd.memset(ones[:, :], 1.0).then_inc(s_clr, 1)
                    pool.wait_ge(s_ms4, 1)
                    link(nc.gpsimd.tensor_scalar(cols[:, 0, :], cols[:, 0, :], 1.0 / D, 1.1920929e-07, ALU.mult, ALU.add))
                    nc.gpsimd.tensor_tensor(cols[:, 0, :], cols[:, 0, :], neghalf[:, :], ALU.pow).then_inc(s_rn4, 1)
                    pool.wait_ge(s_win, 32)
                    for tap in range(4):
                        nc.gpsimd.tensor_tensor(w_tap[:, tap, :], w_in[:, 0:256], conv_row[:, tap, :], ALU.mult).then_inc(s_wc, 1)
                    pool.wait_ge(s_rows, 1)
                    pool.wait_ge(s_zf, 32)
                    for t in range(NT):
                        for i in range(2):
                            nc.gpsimd.indirect_dma_start(xg_dram[:, :], bass.IndirectOffsetOnAxis(ap=rows_u[i][:, t:t + 1], axis=0), XN[:, t, :], None,
                                                         bounds_check=ROWS - 1, oob_is_err=False).then_inc(s_scat, 16)

                @block.tensor
                def _(pe):
                    for s in (s_gu, s_od, s_tp, s_gu8, s_ed):
                        pe.sem_inc(s, LEAD)
                    mm = nc.tensor.matmul
                    pe.wait_ge(s_wr, 16 * 2)
                    for t in range(NT):
                        last = mm(r_bank[:, NE * t:NE * t + NE], XT[:, t // 4, P * (t % 4):P * (t % 4) + P], w_r[:, :], start=True, stop=True)
                    last.then_inc(s_lg4, 1)

                    pe.wait_ge(s_w4, 16 * 3)

                    def shared(c):
                        for f in range(8):
                            pe.wait_ge(s_hd, at(c, 8, f - 1))
                            mm(g_bank[f % 2][:, :], w_sg[:, P * f:P * f + P], XT[:, bass.ds(c, 1), :], start=True, stop=True)
                            mm(u_bank[f % 2][:, :], w_su[:, P * f:P * f + P], XT[:, bass.ds(c, 1), :], start=True, stop=True).then_inc(s_gu, 1)

                    def shared_down(c):
                        pe.wait_ge(s_hd, at(c, 8, 8))
                        pe.wait_ge(s_oc, at(c, 1, 0))
                        for t in range(4):
                            for f in range(8):
                                last = mm(o_bank[:, t, :], hid[:, 0, f, P * t:P * t + P], w_sd[:, f, :], start=(f == 0), stop=(f == 7))
                        last.then_inc(s_od, 1)

                    pe.wait_ge(s_clr, 10)
                    pe.wait_ge(s_sel, 1)
                    mm(x_bank[:, 0:P], below[:, :], sel[:, :, :].rearrange("p t e -> p (t e)"), start=True, stop=False)
                    mm(x_bank[:, 0:P], ones[:, :], cum[0][:, 0:NT, :].rearrange("p t e -> p (t e)"), start=False, stop=True).then_inc(s_rk, 1)
                    with pe.Fori(0, 4) as c:
                        shared(c)
                        shared_down(c)
                    pe.wait_ge(s_rows, 1)

                    def turn_rows(q, i):
                        pe.wait_ge(s_xg[i], q * 48 + 48)
                        pe.wait_ge(s_tc, at(q, 2, i))
                        for k in range(3):
                            r = min(P, CAP - P * k)
                            last = nc.tensor.transpose(x_bank[:, P * k:P * k + r], xg[i][0:r, k, :], ident[0:r, 0:r])
                        last.then_inc(s_tp, 1)

                    def experts(q, more):
                        for i in range(2):
                            n = lambda per, k: at(q, 2 * per, i * per + k)
                            pe.wait_ge(s_tc, n(1, 1))
                            pe.wait_ge(s_w8[i], q * 48 + 48)
                            for f in range(4):
                                pe.wait_ge(s_hd8, n(4, f - 1))
                                mm(g_bank[f % 2][:, 0:CAP], w_rg[i][:, P * f:P * f + P], xgT[:, i, :], start=True, stop=True)
                                mm(u_bank[f % 2][:, 0:CAP], w_ru[i][:, P * f:P * f + P], xgT[:, i, :], start=True, stop=True).then_inc(s_gu8, 1)
                            if i == 0:
                                turn_rows(q, 1)
                            elif more:
                                turn_rows(q + 1, 0)
                            pe.wait_ge(s_hd8, n(4, 4))
                            pe.wait_ge(s_ec, n(1, 0))
                            for k in range(3):
                                r = min(P, CAP - P * k)
                                for f in range(4):
                                    last = mm(e_bank[0:r, k, :], hid[:, i, f, P * k:P * k + r], w_rd[i][:, f, :], start=(f == 0), stop=(f == 3))
                            last.then_inc(s_ed, 1)

                    turn_rows(0, 0)
                    with pe.Fori(0, 3) as q:
                        experts(q, True)
                    experts(3, False)

                @block.scalar
                def _(act):
                    for s in (s_si, s_oc, s_tc, s_si8, s_ec):
                        act.sem_inc(s, LEAD)
                    for s in s_es:
                        act.sem_inc(s, 16)
                    act.wait_ge(s_x4, 1)
                    nc.scalar.activation(pr[:, :, :], pr[:, :, :], ACT.Exp).then_inc(s_e4, 1)
                    act.preload_act_table(ACT.Silu)
                    with act.Fori(0, 4) as c:
                        for f in range(8):
                            act.wait_ge(s_gu, at(c, 8, f + 1))
                            act.wait_ge(s_hd, at(c, 8, f - 1))
                            nc.scalar.activation(sil[:, f % 2, :], g_bank[f % 2][:, :], ACT.Silu).then_inc(s_si, 1)
                        act.wait_ge(s_od, at(c, 1, 1))
                        nc.scalar.activation(GATE[:, bass.ds(c * 4, 4), :], o_bank[:, :, :], ACT.Copy).then_inc(s_oc, 1)
                    def keep_rows(q, i):
                        act.wait_ge(s_tp, at(q, 2, i + 1))
                        act.wait_ge(s_ed, at(q, 2, i - 1))
                        nc.scalar.activation(xgT[:, i, :], x_bank[:, 0:CAP], ACT.Copy).then_inc(s_tc, 1)

                    def experts(q, more):
                        for i in range(2):
                            n = lambda per, k: at(q, 2 * per, i * per + k)
                            for f in range(4):
                                act.wait_ge(s_gu8, n(4, f + 1))
                                act.wait_ge(s_hd8, n(4, f - 1))
                                nc.scalar.activation(sil[:, f % 2, 0:CAP], g_bank[f % 2][:, 0:CAP], ACT.Silu).then_inc(s_si8, 1)
                            if i == 0:
                                keep_rows(q, 1)
                            elif more:
                                keep_rows(q + 1, 0)
                            act.wait_ge(s_ed, n(1, 1))
                            act.wait_ge(s_es[i], q * 48 + 16)
                            nc.scalar.activation(eo[:, i, 0:2, :], e_bank[:, 0:2, :], ACT.Copy)
                            nc.scalar.activation(eo[0:CAP - 2 * P, i, 2, :], e_bank[0:CAP - 2 * P, 2, :], ACT.Copy).then_inc(s_ec, 1)

                    keep_rows(0, 0)
                    with act.Fori(0, 3) as q:
                        experts(q, True)
                    experts(3, False)

                @block.vector
                def _(dve):
                    link = Chain(dve, s_dch)
                    for s in (s_hd, s_hd8):
                        dve.sem_inc(s, LEAD)
                    TT = nc.vector.tensor_tensor
                    wide = lambda col: col.unsqueeze(2).broadcast_to([P, NT, NE])
                    TT(sq[:, :, :], XN[:, :, :], XN[:, :, :], ALU.mult).then_inc(s_sq4, 1)
                    dve.wait_ge(s_sq4, 1)
                    nc.vector.tensor_reduce(cols[:, 0, :], sq[:, :, :], AX.X, ALU.add).then_inc(s_ms4, 1)
                    dve.wait_ge(s_rn4, 1)
                    dve.wait_ge(s_lg4, 1)
                    link(TT(pr[:, :, :], r_bank[:, 0:NT * NE].rearrange("p (t e) -> p t e", e=NE), wide(cols[:, 0, :]), ALU.mult))
                    link(nc.vector.tensor_reduce(cols[:, 1, :], pr[:, :, :], AX.X, ALU.max))
                    TT(pr[:, :, :], pr[:, :, :], wide(cols[:, 1, :]), ALU.subtract).then_inc(s_x4, 1)
                    dve.wait_ge(s_e4, 1)
                    link(nc.vector.tensor_reduce(cols[:, 2, :], pr[:, :, :], AX.X, ALU.add))
                    link(nc.vector.reciprocal(cols[:, 2, :], cols[:, 2, :]))
                    link(TT(pr[:, :, :], pr[:, :, :], wide(cols[:, 2, :]), ALU.mult))
                    for i, src in enumerate((pr, p2)):
                        link(nc.vector.tensor_reduce(cols[:, 3 + i, :], src[:, :, :], AX.X, ALU.max))
                        link(TT(cand[:, :, :], src[:, :, :], wide(cols[:, 3 + i, :]), ALU.is_ge))
                        link(TT(cand[:, :, :], cand[:, :, :], rank_desc[:, :, :], ALU.mult))
                        link(nc.vector.tensor_reduce(cols[:, 5, :], cand[:, :, :], AX.X, ALU.max))
                        link(TT(oh[i][:, :, :], cand[:, :, :], wide(cols[:, 5, :]), ALU.is_equal))
                        if i == 0:
                            link(nc.vector.scalar_tensor_tensor(p2[:, :, :], oh[0][:, :, :], -2.0, pr[:, :, :], ALU.mult, ALU.add))
                    link(TT(cols[:, 6, :], cols[:, 3, :], cols[:, 4, :], ALU.add))
                    link(nc.vector.reciprocal(cols[:, 6, :], cols[:, 6, :]))
                    link(TT(cols[:, 3:5, :], cols[:, 3:5, :], cols[:, 6, :].unsqueeze(1).broadcast_to([P, 2, NT]), ALU.mult))
                    link(TT(sel[:, :, :], oh[0][:, :, :], oh[1][:, :, :], ALU.add))
                    for c in range(2):
                        link(nc.vector.memset(cum[c][:, :, :], 0.0))
                    link(nc.vector.tensor_copy(cum[0][:, 1:NT + 1, :], sel[:, :, :]))
                    for n, step4 in enumerate((1, 2, 4, 8)):
                        a, z = cum[n % 2], cum[(n + 1) % 2]
                        link(nc.vector.tensor_copy(z[:, 0:step4, :], a[:, 0:step4, :]))
                        link(TT(z[:, step4:NT + 1, :], a[:, step4:NT + 1, :], a[:, 0:NT + 1 - step4, :], ALU.add), s_sel if n == 3 else None)

                    dve.wait_ge(s_rk, 1)
                    dve.wait_ge(s_clr, 10)
                    rk = x_bank[:, 0:P].rearrange("p (t e) -> p t e", e=NE)
                    link(nc.vector.tensor_scalar(kept[:, :, :], rk, float(CAP), None, ALU.is_lt))
                    link(TT(row[:, :, :], rk, base_row[:, :, :], ALU.add))
                    link(nc.vector.tensor_scalar(cand[:, :, :], kept[:, :, :], -FAR, FAR, ALU.mult, ALU.add))
                    link(TT(row[:, :, :], row[:, :, :], cand[:, :, :], ALU.add))
                    for i in range(2):
                        link(TT(cand[:, :, :], oh[i][:, :, :], row[:, :, :], ALU.mult))
                        link(nc.vector.tensor_reduce(cols[:, 7, :], cand[:, :, :], AX.X, ALU.add))
                        link(nc.vector.tensor_copy(rows_u[i][:, :], cols[:, 7, :]))
                        link(TT(cand[:, :, :], oh[i][:, :, :], kept[:, :, :], ALU.mult))
                        link(nc.vector.tensor_reduce(cols[:, 8 + i, :], cand[:, :, :], AX.X, ALU.add))
                    link(TT(share[:, :, :], cols[:, 3:5, :], cols[:, 8:10, :], ALU.mult), s_rows)

                    def shared(c):
                        for f in range(8):
                            dve.wait_ge(s_si, at(c, 8, f + 1))
                            if f == 0:
                                dve.wait_ge(s_od, at(c, 1, 0))
                            TT(hid[:, 0, f, :], sil[:, f % 2, :], u_bank[f % 2][:, :], ALU.mult).then_inc(s_hd, 1)

                    with dve.Fori(0, 4) as c:
                        shared(c)
                    with dve.Fori(0, 4) as q:
                        for i in range(2):
                            n = lambda per, k: at(q, 2 * per, i * per + k)
                            for f in range(4):
                                dve.wait_ge(s_si8, n(4, f + 1))
                                if f == 0:
                                    dve.wait_ge(s_ed, n(1, -1))
                                TT(hid[:, i, f, 0:CAP], sil[:, f % 2, 0:CAP], u_bank[f % 2][:, 0:CAP], ALU.mult).then_inc(s_hd8, 1)
        keepx.close()
        st5 = ExitStack()
        with st5:
            NB, GR, KS, UN = B, 8, 4, 32
            DR, XR, HR = 8, 4, 4
            slot_bank = [st5.enter_context(nc.psum_tensor(f"slot_bank{i}", [P, 512], fp32)) for i in range(4)]
            du_bank = [st5.enter_context(nc.psum_tensor(f"du_bank{i}", [P, 512], fp32)) for i in range(2)]
            dt_dram = nc.dram_tensor("dt_turn", [2, 256, 512], fp32).ap()
            bc_dram = nc.dram_tensor("bc_turn", [2, 32, 512], fp32).ap()
            w_xp = sb(st5, "w_xp", [P, 2, 40])
            w_dt = sb(st5, "w_dt", [40, 256])
            pre_cols = sb(st5, "pre_cols", [P, 4])
            w_out = sb(st5, "w_out", [P, 2, D])
            d_col = sb(st5, "d_col", [P, 2])
            a_all = sb(st5, "a_all", [P, 4, UN])
            a_cur = sb(st5, "a_cur", [P, UN])
            spread = sb(st5, "spread_sb", [P, 4, P])
            fold = sb(st5, "fold_sb", [P, 32])
            bc = sb(st5, "bc", [P, 2, 8, 512])
            dtr = sb(st5, "dtr", [P, 2, GR, 512])
            xc = sb(st5, "xc", [P, 2, 2, 512])
            zs = sb(st5, "zs", [P, 2, 2, 512])
            du = sb(st5, "du", [P, 2, 2, 512])
            dt = sb(st5, "dt", [P, 2, 512])
            spa = sb(st5, "spa", [P, 2, 512])
            spr = sb(st5, "spr", [P, 2, 512])
            dbc = sb(st5, "dbc", [40, 512])
            dec = sb(st5, "decay", [P, DR, 512])
            dbx = sb(st5, "dbx", [P, XR, 512])
            hs = sb(st5, "hs", [P, HR, 512])
            hc = sb(st5, "hc", [P, 16, 512])
            back = [hc[:, 4 * i:4 * i + 4, :].rearrange("p a (b d) -> p (a b) d", d=D) for i in range(2)]
            yv = sb(st5, "yv5", [P, 2, 512])

            sem = lambda name: st5.enter_context(nc.semaphore(name))
            s_cst, s_wpre, s_wpost, s_zero, s_neg = map(sem, ("consts5", "pre_weights", "post_weights", "w_dt_cleared", "a_steps"))
            s_slot, s_fA, s_fV = map(sem, ("slot_written", "slot_left_by_scalar", "slot_left_by_vector"))
            s_du, s_dec, s_bx, s_sc, s_hc, s_yr = map(sem, ("du_spread", "decay_ready", "dbx_ready", "scan_done", "hc_ready", "round_summed"))
            s_gz, s_fin = map(sem, ("rows_cleared5", "mixture_steps"))
            s_gath = [sem(f"rows_back{b}") for b in range(B)]
            s_xc, s_ln, s_dt, s_dun, s_yd, s_yv, s_ac = map(sem, ("xc_ready", "softplus_log", "dt_ready", "du_ready", "y_with_d", "yv_ready", "a_of_layer"))
            s_dtr = [sem(f"dt_spread{i}") for i in range(2)]
            s_bc = [sem(f"bc_spread{i}") for i in range(2)]
            s_dst, s_bst = sem("dt_stored"), sem("bc_stored")
            s_spx = sem("softplus_exp")

            ACT_AT = {'out': 10, 'silus': 13, 'dbc': 15, 'softplus': 18}
            DVE_AT = {'y1': 3, 'dt': 18, 'du': 20, 'y0': 28}
            LEAD = 64
            SCALAR, VECTOR = s_fA, s_fV
            PRE = [(name, SCALAR) for name in ("xi0", "xi1", "z0", "z1", "xp", "dt0", "dt1", "out")]
            TURN = ('y1', 'xi0', 'du2', 'xi1', 'out', 'z0', 'z1', 'du3', 'xp', 'du4', 'dt', 'y0', 'du5', 'du6', 'du7', 'du8', 'du9')
            order = []
            for b in range(NB):
                for name in TURN:
                    if name in ("y1", "out"):
                        if b:
                            order.append((name, b - 1, VECTOR if name == "y1" else SCALAR))
                    elif name == "y0":
                        order.append((name, b, VECTOR))
                    elif name == "dt":
                        order += [("dt0", b, SCALAR), ("dt1", b, SCALAR)]
                    elif name[:2] != "du":
                        order.append((name, b, SCALAR))
            order += [("y1", NB - 1, VECTOR), ("out", NB - 1, SCALAR)]
            place = {(name, b): n for n, (name, b, _) in enumerate(order)}
            left = lambda n, who: sum(1 for x in order[:n] if x[2] is who)
            per = {who: left(len(order), who) for who in (SCALAR, VECTOR)}
            assert len(order) % 4 == 0
            assert place["out", NB - 1] % 4 == (len(PRE) - 1) % 4
            pre_left = {SCALAR: len(PRE), VECTOR: 1}
            written_before = lambda n: sum(1 for x in order[:n] if x[0][0] != "y")

            class Slot:

                def __init__(self, name, b, l):
                    self.l = l
                    if l is None:
                        self.n = [x[0] for x in PRE].index(name)
                        self.who = PRE[self.n][1]
                    else:
                        self.n = place[name, b]
                        self.who = order[self.n][2]
                    self.bank = slot_bank[self.n % 4]

                def written(self):
                    if self.l is None:
                        return LEAD + self.n + 1
                    return self.l * written_before(len(order)) + (LEAD + len(PRE) + written_before(self.n + 1))

                def free(self, pe):
                    if self.l is None:
                        if self.n >= 4:
                            who = PRE[self.n - 4][1]
                            pe.wait_ge(who, LEAD + sum(1 for x in PRE[:self.n - 3] if x[1] is who))
                        return
                    m = self.n - 4
                    who = order[m][2]
                    count = left(m + 1, who) if m >= 0 else left(len(order) + m + 1, who) - per[who]
                    pe.wait_ge(who, self.l * per[who] + (LEAD + pre_left[who] + count))

                def left_at(self):
                    if self.l is None:
                        return LEAD + sum(1 for x in PRE[:self.n + 1] if x[1] is self.who)
                    return self.l * per[self.who] + (LEAD + pre_left[self.who] + left(self.n + 1, self.who))

            at = lambda l, b, per_turn, k: (0 if l is None else l) * (4 * per_turn) + (LEAD + per_turn * b + k)

            with nc.Block() as block:
                loaded = lambda l, n: l * 128 + 64 * (1 + n // 2)
                stored = lambda l, n: l * 64 + 16 * (n + 1)
                consts = [(spread[:, :, :], A["spread"]), (fold[:, :], A["fold"]), (a_all[:, :, :], A["a_log"])]

                @block.sync
                def _(sp):
                    def load_in(l):
                        one = lambda x: x[bass.ds(l, 1)]
                        sp.dma_start(w_in[:, :], one(A["w_in"]).rearrange("o p e -> p (o e)")).then_inc(s_win, 16)
                        sp.dma_start(conv_row[:, :, :], one(A["conv_row"]).broadcast_to([P, 4, 256])).then_inc(s_win, 16)

                    def load_pre(l):
                        one = lambda x: x[bass.ds(l, 1)]
                        sp.dma_start(w_xp[:, :, :], one(A["w_xp"]).rearrange("o p k e -> p (o k) e")).then_inc(s_wpre, 16)
                        sp.dma_start(w_dt[0:8, :], one(A["w_dt"]).rearrange("o p e -> p (o e)")).then_inc(s_wpre, 16)
                        sp.dma_start(pre_cols[:, :], one(A["pre_cols"]).rearrange("o p e -> p (o e)")).then_inc(s_wpre, 16)

                    def load_post(l):
                        one = lambda x: x[bass.ds(l, 1)]
                        sp.dma_start(w_out[:, :, :], one(A["w_out"]).rearrange("o p k e -> p (o k) e")).then_inc(s_wpost, 16)
                        sp.dma_start(d_col[:, :], one(A["d_col"]).rearrange("o p e -> p (o e)")).then_inc(s_wpost, 16)

                    def spread_dt(l, b, n):
                        sp.wait_ge(s_dt, at(l, n, 2, 2))
                        sp.dma_start(dt_dram[n % 2].rearrange("(h p) t -> p h t", p=P), dt[:, :, :]).then_inc(s_dst, 16)
                        sp.wait_ge(s_dst, stored(l, n))
                        for s in range(4):
                            sp.dma_start(dtr[32 * s:32 * s + 32, n % 2, :, :], dt_dram[n % 2].rearrange("(g c) t -> c g t", c=32)).then_inc(s_dtr[n % 2], 16)

                    def spread_bc(l, b, n):
                        sp.wait_ge(SCALAR, Slot("xp", b, l).left_at())
                        sp.dma_start(bc_dram[n % 2], dbc[8:40, :]).then_inc(s_bst, 16)
                        sp.wait_ge(s_bst, stored(0 if l is None else l, n))
                        for s in range(4):
                            sp.dma_start(bc[32 * s:32 * s + 32, n % 2, :, :],
                                         bc_dram[n % 2].rearrange("(i s) t -> s i t", s=4)[s:s + 1].broadcast_to([32, 8, 512])).then_inc(s_bc[n % 2], 16)

                    sp.wait_ge(s_zero, 1)
                    load_pre(0)
                    for dst, src in consts:
                        sp.dma_start(dst, src).then_inc(s_cst, 16)
                    spread_bc(None, None, 0)
                    spread_dt(0, None, 0)
                    with sp.Fori(0, 4) as l:
                        for b in range(NB):
                            if b == 0:
                                sp.wait_ge(s_slot, Slot("out", NB - 1, l - 1).written())
                                sp.wait_ge(s_zero, 1)
                                load_post(l)
                            if b == 2:
                                sp.wait_ge(s_slot, Slot("z1", b, l).written())
                                sp.wait_ge(s_zero, 1)
                                load_in(l + 1)
                            if b == 3:
                                load_pre(l + 1)
                            spread_bc(l, b, b + 1)
                            spread_dt(l, b, b + 1)

                @block.gpsimd
                def _(pool):
                    nc.gpsimd.memset(back[1][:, :, :], 0.0).then_inc(s_gz, 1)
                    nc.gpsimd.memset(w_dt[:, :], 0.0).then_inc(s_zero, 1)
                    pool.sem_inc(s_hc, LEAD)

                    def make_tap(tap):
                        nc.gpsimd.tensor_tensor(w_tap[:, tap, :], w_in[:, 0:256], conv_row[:, tap, :], ALU.mult).then_inc(s_wc, 1)

                    pool.wait_ge(s_gz, 2)
                    for t in range(NT):
                        for i in range(2):
                            nc.gpsimd.indirect_dma_start(back[i][:, t, :], None, eo_dram[:, :], bass.IndirectOffsetOnAxis(ap=rows_u[i][:, t:t + 1], axis=0),
                                                         bounds_check=ROWS - 1, oob_is_err=False).then_inc(s_gath[t // 4], 16)
                    pool.wait_ge(s_fin, 2 * B)
                    with pool.Fori(0, 4) as l:
                        for b in range(NB):
                            for u in range(UN):
                                k = u % 4
                                pool.wait_ge(s_sc, at(l, b, UN, u + 1))
                                if u % 16 < 4:
                                    pool.wait_ge(s_yr, at(l, b, 8, 4 * (u // 16) - 3 + k))
                                if u == 0:
                                    pool.wait_ge(s_bc[b % 2], loaded(l, b))
                                nc.gpsimd.tensor_tensor(hc[:, u % 16, :], hs[:, u % HR, :], bc[:, b % 2, 4 + k, :], ALU.mult).then_inc(s_hc, 1)
                                if b == 2 and u in (17, 20, 23, 26):
                                    if u == 17:
                                        pool.wait_ge(s_win, l * 32 + 64)
                                    make_tap((u - 17) // 3)

                @block.tensor
                def _(pe):
                    for s in (s_slot, s_du, s_yr):
                        pe.sem_inc(s, LEAD)
                    mm = nc.tensor.matmul

                    def in_proj(l, b, n, names):
                        for name in names:
                            sl = Slot(name, b, l)
                            sl.free(pe)
                            if name == "xi0":
                                if l is not None:
                                    pe.wait_ge(SCALAR, Slot("out", n % 4, l if n == 4 else l - 1).left_at())
                                pe.wait_ge(s_wc, 4 if l is None else l * 4 + 4 * (1 + n // 4))
                            c = P * int(name[-1])
                            if name[0] == "z":
                                mm(sl.bank[:, :], w_in[:, 256 + c:256 + c + P], XT[:, n % 4, :], start=True, stop=True).then_inc(s_slot, 1)
                                continue
                            for d in range(4):
                                last = mm(sl.bank[:, d:512], w_tap[:, 3 - d, c:c + P], XT[:, n % 4, 0:512 - d], start=(d == 0), stop=(d == 3))
                            last.then_inc(s_slot, 1)

                    def x_proj(l, b, n):
                        sl = Slot("xp", b, l)
                        sl.free(pe)
                        pe.wait_ge(s_xc, at(l, n, 2, 2))
                        pe.wait_ge(s_wpre, 48 if l is None else l * 48 + 48 * (1 + n // 4))
                        for h in range(2):
                            last = mm(sl.bank[0:40, :], w_xp[:, h, :], xc[:, n % 2, h, :], start=(h == 0), stop=(h == 1))
                        last.then_inc(s_slot, 1)

                    def dt_proj(l, b):
                        pe.wait_ge(SCALAR, Slot("xp", b, l).left_at())
                        for h in range(2):
                            sl = Slot(f"dt{h}", b, l)
                            sl.free(pe)
                            mm(sl.bank[:, :], w_dt[:, P * h:P * h + P], dbc[:, :], start=True, stop=True).then_inc(s_slot, 1)

                    def spread_du(l, b, g, n):
                        if g == 0:
                            pe.wait_ge(s_dun, at(l, n, 2, 2))
                        pe.wait_ge(s_bx, at(l, n, UN, 4 * g - 4))
                        mm(du_bank[g % 2][:, :], spread[:, g % 4, :], du[:, n % 2, g // 4, :], start=True, stop=True).then_inc(s_du, 1)

                    def sum_states(l, b, half, in_turn):
                        sl = Slot(f"y{half}", b, l)
                        sl.free(pe)
                        for k in range(KS):
                            pe.wait_ge(s_hc, at(l, b, UN, 16 * half + 13 + k))
                            for j in range(4):
                                last = mm(sl.bank[32 * j:32 * j + 32, :], fold[:, :], hc[:, 4 * j + k, :], start=(k == 0), stop=(k == KS - 1),
                                          tile_position=(0, 32 * j), skip_group_check=True)
                            last.then_inc(s_yr, 1)

                    def out_proj(l, b):
                        sl = Slot("out", b, l)
                        sl.free(pe)
                        pe.wait_ge(s_yv, at(l, b, 2, 2))
                        pe.wait_ge(s_wpost, l * 32 + 32)
                        for h in range(2):
                            last = mm(sl.bank[:, :], w_out[:, h, :], yv[:, h, :], start=(h == 0), stop=(h == 1))
                        last.then_inc(s_slot, 1)

                    in_proj(None, None, 0, ("xi0", "xi1", "z0", "z1"))
                    x_proj(None, None, 0)
                    dt_proj(None, None)
                    sl = Slot("out", None, None)
                    sl.free(pe)
                    mm(sl.bank[:, :], ident[:, :], XT[:, NB - 1, :], start=True, stop=True).then_inc(s_slot, 1)
                    pe.wait_ge(SCALAR, LEAD + pre_left[SCALAR] - 1)
                    pe.wait_ge(s_cst, 16 * len(consts))
                    spread_du(0, None, 0, 0)
                    spread_du(0, None, 1, 0)
                    with pe.Fori(0, 4) as l:
                        for b in range(NB):
                            for name in TURN:
                                if name == "y1" and b:
                                    sum_states(l, b - 1, 1, b)
                                if name == "y0":
                                    sum_states(l, b, 0, b)
                                if name == "out" and b:
                                    out_proj(l, b - 1)
                                if name in ("xi0", "xi1", "z0", "z1"):
                                    in_proj(l, b, b + 1, (name,))
                                if name == "xp":
                                    x_proj(l, b, b + 1)
                                if name == "dt":
                                    dt_proj(l, b)
                                if name[:2] == "du":
                                    g = int(name[2])
                                    spread_du(l, b, g % GR, b + g // GR)
                        sum_states(l, NB - 1, 1, NB)
                        out_proj(l, NB - 1)

                @block.scalar
                def _(act):
                    for s in (s_fA, s_dec, s_xc, s_ln, s_spx):
                        act.sem_inc(s, LEAD)
                    act.wait_ge(s_cst, 16 * len(consts))
                    act.preload_act_table_set("natural_log_exp_and_others")
                    flat = a_all[:, :, :].rearrange("p l u -> p (l u)")
                    nc.scalar.activation(flat, flat, ACT.Exp).then_inc(s_neg, 1)
                    act.wait_ge(s_neg, 1)
                    nc.scalar.activation(flat, flat, ACT.Copy, scale=-1.0).then_inc(s_neg, 1)
                    act.wait_ge(s_neg, 2)

                    def silus(l, b, n):
                        if l is not None:
                            act.wait_ge(s_yv, at(l, b, 2, 0))
                        act.wait_ge(s_wpre, 48 if l is None else l * 48 + 48 * (1 + n // 4))
                        for h in range(2):
                            sl = Slot(f"xi{h}", b, l)
                            act.wait_ge(s_slot, sl.written())
                            nc.scalar.activation(xc[:, n % 2, h, :], sl.bank[:, :], ACT.Silu, bias=pre_cols[:, h:h + 1]).then_inc(s_xc, 1)
                        act.wait_ge(s_xc, at(l, n, 2, 2))
                        act.sem_inc(SCALAR, 2)
                        if b:
                            copy_out(l, b - 1)
                        for h in range(2):
                            sl = Slot(f"z{h}", b, l)
                            act.wait_ge(s_slot, sl.written())
                            nc.scalar.activation(zs[:, n % 2, h, :], sl.bank[:, :], ACT.Silu).then_inc(SCALAR, 1)

                    def copy_dbc(l, b):
                        sl = Slot("xp", b, l)
                        if l is not None:
                            act.wait_ge(s_bst, stored(l, b))
                            act.wait_ge(s_hc, at(l, b, UN, 0))
                        act.wait_ge(s_slot, sl.written())
                        nc.scalar.activation(dbc[:, :], sl.bank[0:40, :], ACT.Copy).then_inc(SCALAR, 1)

                    def softplus(l, b, n):
                        act.wait_ge(s_dt, at(l, n, 2, 0))
                        for h in range(2):
                            sl = Slot(f"dt{h}", b, l)
                            act.wait_ge(s_slot, sl.written())
                            bias = pre_cols[:, 2 + h:3 + h]
                            nc.scalar.activation(spa[:, h, :], sl.bank[:, :], ACT.Abs, bias=bias).then_inc(s_spx, 1)
                            nc.scalar.activation(spr[:, h, :], sl.bank[:, :], ACT.Relu, bias=bias).then_inc(SCALAR, 1)
                        act.wait_ge(s_spx, at(l, n, 3, 2))
                        nc.scalar.activation(spa[:, :, :], spa[:, :, :], ACT.Exp, scale=-1.0).then_inc(s_spx, 1)
                        act.wait_ge(s_spx, at(l, n, 3, 3))
                        nc.scalar.activation(spa[:, :, :], spa[:, :, :], ACT.Ln, bias=1.0).then_inc(s_ln, 1)

                    def copy_out(l, b):
                        sl = Slot("out", b, l)
                        act.wait_ge(s_slot, sl.written())
                        nc.scalar.activation(XT[:, b, :], sl.bank[:, :], ACT.Copy).then_inc(SCALAR, 1)

                    silus(None, None, 0)
                    act.preload_act_table_set("natural_log_exp_and_others")
                    copy_dbc(None, None)
                    softplus(None, None, 0)
                    with act.Fori(0, 4) as l:
                        act.wait_ge(s_dec, at(l, 0, UN, 0))
                        act.wait_ge(s_cst, 16 * len(consts))
                        nc.scalar.activation(a_cur[:, :], a_all[:, bass.ds(l, 1), :].rearrange("p l u -> p (l u)"), ACT.Copy).then_inc(s_ac, 1)
                        act.wait_ge(s_ac, l + 1)
                        for b in range(NB):
                            for u in range(UN):
                                if u == 0:
                                    act.wait_ge(s_dtr[b % 2], loaded(l, b))
                                act.wait_ge(s_sc, at(l, b, UN, u - DR + 1))
                                nc.scalar.activation(dec[:, u % DR, :], dtr[:, b % 2, u // 4, :], ACT.Exp, scale=a_cur[:, u:u + 1]).then_inc(s_dec, 1)
                                if b == 0 and u == ACT_AT["out"]:
                                    copy_out(l - 1, NB - 1)
                                if u == ACT_AT["silus"]:
                                    silus(l, b, b + 1)
                                    act.preload_act_table_set("natural_log_exp_and_others")
                                if u == ACT_AT["dbc"]:
                                    copy_dbc(l, b)
                                if u == ACT_AT["softplus"]:
                                    softplus(l, b, b + 1)
                    copy_out(NB - 1, NB - 1)

                @block.vector
                def _(dve):
                    nc.vector.memset(back[0][:, :, :], 0.0).then_inc(s_gz, 1)
                    for s in (s_fV, s_bx, s_sc, s_dt, s_dun, s_yd, s_yv):
                        dve.sem_inc(s, LEAD)
                    TT = nc.vector.tensor_tensor

                    def make_dt(l, b, n, h):
                        if h == 0:
                            dve.wait_ge(s_ln, at(l, n, 1, 1))
                            dve.wait_ge(SCALAR, Slot("dt1", b, l).left_at())
                            if l is not None:
                                dve.wait_ge(s_dst, stored(l, n - 1))
                        TT(dt[:, h, :], spa[:, h, :], spr[:, h, :], ALU.add).then_inc(s_dt, 1)

                    def make_du(l, b, n, h):
                        dve.wait_ge(s_dt, at(l, n, 2, h + 1))
                        dve.wait_ge(s_xc, at(l, n, 2, 2))
                        TT(du[:, n % 2, h, :], dt[:, h, :], xc[:, n % 2, h, :], ALU.mult).then_inc(s_dun, 1)

                    def add_d(l, b, half):
                        sl = Slot(f"y{half}", b, l)
                        dve.wait_ge(s_yr, at(l, b, 8, 4 * half + 4))
                        dve.wait_ge(s_wpost, l * 32 + 32)
                        dve.wait_ge(s_yd, at(l, b, 2, half))
                        if half == 0:
                            dve.wait_ge(s_slot, (Slot("out", b - 1, l) if b else Slot("out", NB - 1, l - 1)).written())
                        nc.vector.scalar_tensor_tensor(yv[:, half, :], xc[:, b % 2, half, :], d_col[:, half:half + 1], sl.bank[:, :],
                                                       ALU.mult, ALU.add).then_inc(s_yd, 1)

                    def gate_y(l, b, half):
                        dve.wait_ge(s_yd, at(l, b, 2, half + 1))
                        dve.sem_inc(VECTOR, 1)
                        TT(yv[:, half, :], yv[:, half, :], zs[:, b % 2, half, :], ALU.mult).then_inc(s_yv, 1)

                    def input_of(l, b, u):
                        g, k = u // 4, u % 4
                        if k == 0:
                            dve.wait_ge(s_du, at(l, b, 8, g + 1))
                        if u == 0:
                            dve.wait_ge(s_bc[b % 2], loaded(l, b))
                        dve.wait_ge(s_sc, at(l, b, UN, u - XR + 1))
                        TT(dbx[:, u % XR, :], du_bank[g % 2][:, :], bc[:, b % 2, k, :], ALU.mult).then_inc(s_bx, 1)

                    def mix(b):
                        dve.wait_ge(s_gz, 2)
                        dve.wait_ge(s_gath[b], 16 * 2 * 4)
                        for i in range(2):
                            for t in range(4 * b, 4 * b + 4):
                                last = nc.vector.scalar_tensor_tensor(GATE[:, t, :], back[i][:, t, :], share[:, i, t:t + 1], GATE[:, t, :], ALU.mult, ALU.add)
                            last.then_inc(s_fin, 1)
                            dve.wait_ge(s_fin, 2 * b + i + 1)

                    mix(0)
                    for h in range(2):
                        make_dt(None, None, 0, h)
                    for h in range(2):
                        make_du(None, None, 0, h)
                    mix(1)
                    mix(2)
                    mix(3)
                    dve.sem_inc(VECTOR, 1)
                    with dve.Fori(0, 4) as l:
                        for b in range(NB):
                            input_of(l, b, 0)
                            for u in range(UN):
                                if u + 1 < UN:
                                    input_of(l, b, u + 1)
                                for h in range(2):
                                    if u == DVE_AT["dt"] + h:
                                        make_dt(l, b, b + 1, h)
                                    if u == DVE_AT["du"] + h:
                                        make_du(l, b, b + 1, h)
                                if u == DVE_AT["y0"]:
                                    add_d(l, b, 0)
                                if u == DVE_AT["y0"] + 2:
                                    gate_y(l, b, 0)
                                if b and u == DVE_AT["y1"]:
                                    add_d(l, b - 1, 1)
                                if b and u == DVE_AT["y1"] + 2:
                                    gate_y(l, b - 1, 1)
                                dve.wait_ge(s_dec, at(l, b, UN, u + 1))
                                dve.wait_ge(s_hc, at(l, b, UN, u - HR + 1))
                                dve.wait_ge(s_bx, at(l, b, UN, u + 1))
                                nc.vector.tensor_tensor_scan(hs[:, u % HR, :], dec[:, u % DR, :], dbx[:, u % XR, :], 0.0, ALU.mult, ALU.add).then_inc(s_sc, 1)
                        add_d(l, NB - 1, 1)
                        gate_y(l, NB - 1, 1)
        st6 = ExitStack()
        with st6:
            X = sb(st6, "X6", [P, NT, D])
            bank = [st6.enter_context(nc.psum_tensor(f"s6_bank{i}", [P, 4, D], fp32)) for i in range(4)]
            sem = lambda name: st6.enter_context(nc.semaphore(name))
            s_g6 = sem("gate_ready")
            s_t6, s_r6, s_o6 = map(sem, ("s_by_token", "x_steps", "x_transfers"))
            with nc.Block() as block:
                @block.tensor
                def _(pe):
                    for b in range(B):
                        for t in range(4):
                            last = nc.tensor.transpose(bank[b][:, t, :], XT[:, b, P * t:P * t + P], ident[:, :])
                        last.then_inc(s_t6, 1)

                @block.scalar
                def _(act):
                    nc.scalar.activation(GATE[:, :, :], GATE[:, :, :], ACT.Silu).then_inc(s_g6, 1)

                @block.vector
                def _(dve):
                    for b in range(B):
                        tl = slice(4 * b, 4 * b + 4)
                        dve.wait_ge(s_t6, b + 1)
                        dve.wait_ge(s_g6, 1)
                        nc.vector.tensor_tensor(GATE[:, tl, :], bank[b][:, :, :], GATE[:, tl, :], ALU.mult).then_inc(s_r6, 1)
                        dve.wait_ge(s_r6, 2 * b + 1)
                        dve.wait_ge(s_o6, 16)
                        nc.vector.tensor_tensor(X[:, tl, :], X[:, tl, :], GATE[:, tl, :], ALU.add).then_inc(s_r6, 1)

                @block.sync
                def _(sp):
                    sp.dma_start(X[:, :, :], x_dram).then_inc(s_o6, 16)
                    for b in range(B):
                        sp.wait_ge(s_r6, 2 * b + 2)
                        sp.wait_ge(s_o6, 16 + 16 * b)
                        sp.dma_start(out[b].rearrange("(k p) d -> p k d", p=P), X[:, 4 * b:4 * b + 4, :]).then_inc(s_o6, 16)
                    sp.wait_ge(s_o6, 16 + 16 * B)


def laid_out(i):
    import numpy as np

    f = lambda name: np.asarray(i[name])
    row = lambda name: np.ascontiguousarray(f(name).reshape(-1))
    t2 = lambda a: np.ascontiguousarray(np.swapaxes(a, -1, -2))
    L = 4
    wrap = lambda a, n=1: np.concatenate([a, a[:n]], 0)
    part = np.arange(128)
    spread = np.stack([(np.arange(128)[:, None] == 32 * j + part[None] % 32) for j in range(4)], 1).astype(np.float32)
    a = {
        "x": f("L0_attn_x"),
        "w_att": np.concatenate([f("L0_attn_Wq").T, f("L0_attn_Wk").T, f("L0_attn_Wv").T], 1),
        "w_mha": t2(f("L0_ffn_Wqkv")), "b_mha": row("L0_ffn_bqkv"), "w_mo": t2(f("L0_ffn_Wo")), "b_mo": row("L0_ffn_bo"),
        "w_gate0": t2(f("L0_ffn_Wg")), "g1": row("L0_ffn_g1"), "be1": row("L0_ffn_be1"), "g2": row("L0_ffn_g2"), "be2": row("L0_ffn_be2"),
        "cos_head_delta": row("L0_attn_cos_head_delta"), "cos_raw": row("L0_attn_cos_logit_scale_raw"), "delta_gain": row("L0_attn_delta_gain"),
        "bo": row("L0_attn_bo"), "subln": row("L0_attn_subln_weight"), "wo_att": t2(f("L0_attn_Wo")),
        "lq1": row("L0_attn_lambda_q1"), "lk1": row("L0_attn_lambda_k1"), "lq2": row("L0_attn_lambda_q2"), "lk2": row("L0_attn_lambda_k2"),
        "w_expert": np.concatenate([f("L0_ffn_W1"), t2(f("L0_ffn_b1").reshape(8, 4, 128)),
                                    f("L0_ffn_W2").reshape(8, 4, 128, 128).transpose(0, 2, 1, 3).reshape(8, 128, 512)], 2).reshape(8 * 128, 1028),
        "b2": f("L0_ffn_b2"), "tile_starts": 128 * np.arange(16, dtype=np.float32), "blocks": np.arange(26, dtype=np.float32),
        "lane": np.arange(128, dtype=np.float32)[:, None], "below": np.triu(np.ones((128, 128), np.float32), 1),
        "ident": np.eye(128, dtype=np.float32),
        "w_in": wrap(t2(f("L1_attn_in_proj_w"))),
        "w_xp": wrap(t2(f("L1_attn_x_proj_w")).reshape(L, 2, 128, 40).transpose(0, 2, 1, 3)),
        "w_dt": wrap(t2(f("L1_attn_dt_proj_w"))),
        "conv_row": wrap(t2(f("L1_attn_conv_w"))),
        "pre_cols": wrap(np.concatenate([t2(f("L1_attn_conv_b").reshape(L, 2, 128)), t2(f("L1_attn_dt_proj_b").reshape(L, 2, 128))], 2)),
        "w_out": t2(f("L1_attn_out_proj_w")).reshape(L, 2, 128, 128).transpose(0, 2, 1, 3),
        "d_col": t2(f("L1_attn_D").reshape(L, 2, 128)),
        "a_log": f("L1_attn_A_log").reshape(L, 8, 32, 4, 4).transpose(4, 2, 0, 1, 3).reshape(128, L, 32),
        "spread": spread, "fold": np.tile(np.eye(32, dtype=np.float32), (4, 1)),
        "w_router": t2(f("L1_ffn_router_w")),
        "w_sg": f("L1_ffn_sg"), "w_su": f("L1_ffn_su"), "w_sd": f("L1_ffn_sd").reshape(8, 128, 128).transpose(1, 0, 2),
        "w_rg": f("L1_ffn_rg"), "w_ru": f("L1_ffn_ru"), "w_rd": f("L1_ffn_rd"),
    }
    return {k: np.ascontiguousarray(v) for k, v in a.items()}


def kernel(**inputs):
    import concourse.bacc as _bacc
    from concourse.bass_utils import run_bass_kernel_spmd as _run

    nc = _bacc.Bacc("TRN2", target_bir_lowering=False, num_devices=1)
    arrays, aps = {}, {}
    for name, a in laid_out(inputs).items():
        arrays[f"in_{name}"] = a
        aps[name] = nc.dram_tensor(f"in_{name}", list(a.shape), mybir.dt.from_np(a.dtype), kind="ExternalInput").ap()
    out = nc.dram_tensor("out_x", [B, N, D], fp32, kind="ExternalOutput").ap()
    build_stages(nc, aps, out)
    r = _run(nc, [arrays], core_ids=[0])
    return r.results[0]["out_x"]
```
